# Optimizing a Trainium2 kernel written in Bass

```python
import numpy as np
import jax
import jax.numpy as jnp

def _softmax(x, axis=-1):
    return jax.nn.softmax(x, axis=axis)

def _gelu(x):
    return jax.nn.gelu(x, approximate=True)

def _silu(x):
    return jax.nn.silu(x)

def _sigmoid(x):
    return jax.nn.sigmoid(x)

def _layernorm(x, axis=-1, eps=1e-05):
    m = jnp.mean(x, axis=axis, keepdims=True)
    v = jnp.var(x, axis=axis, keepdims=True)
    return (x - m) / jnp.sqrt(v + eps)

def _scatter_add(tgt, idx, src, axis=0):
    return tgt.at[idx].add(src)

def _segment_sum(src, seg, n):
    return jax.ops.segment_sum(src, seg, n)
kernel_name = 'mk_adaln_ffn_d2_seqx_r4_e70700'

def setup_inputs(seed: int=0):
    np.random.seed(seed)
    _w = jnp.asarray

    def _rec_inputs():
        import jax
        import jax.numpy as jnp
        _rk = jax.random.key(seed)
        x = -0.0002928 + 1 * jax.random.normal(jax.random.fold_in(_rk, 1), (32, 64, 256), jnp.float32)
        _lenS = 64 - jax.random.randint(jax.random.fold_in(_rk, 7), (32,), 0, max(1, 64 // 4) + 1, jnp.int32)
        _lenS2 = 64 - jax.random.randint(jax.random.fold_in(_rk, 8), (32,), 0, max(1, 64 // 4) + 1, jnp.int32)
        cond_256 = -0.106481 + 1.03144 * jax.random.normal(jax.random.fold_in(_rk, 12), (32, 64), jnp.float32)
        _validS = jnp.arange(64)[None, :] < _lenS[:, None]
        _validS2 = jnp.arange(64)[None, :] < _lenS2[:, None]
        _causal = jnp.tril(jnp.ones((64, 64), dtype=bool))
        mask_SxS_bk1 = jnp.broadcast_to(_validS[0:1, :], (64, 64))
        return (x, cond_256, mask_SxS_bk1)
    x, cond_256, mask_SxS_bk1 = _rec_inputs()

    def _L0_cond_setup():
        import jax, jax.numpy as jnp
        import numpy as np
        EPS = 1e-06
        key = jax.random.key(seed)
        ks = jax.random.split(key, 8)
        B, S, E, C = (2, 512, 256, 64)
        x = jax.random.normal(ks[0], (B, S, E), dtype=jnp.float32)
        mask = jnp.triu(jnp.ones((S, S), dtype=bool), k=1)
        conditioning = jax.random.normal(ks[1], (B, C), dtype=jnp.float32)
        sc = 1.0 / np.sqrt(E)
        Wq = jax.random.normal(ks[2], (E, E), dtype=jnp.float32) * sc
        Wk = jax.random.normal(ks[3], (E, E), dtype=jnp.float32) * sc
        Wv = jax.random.normal(ks[4], (E, E), dtype=jnp.float32) * sc
        Wo = jax.random.normal(ks[5], (E, E), dtype=jnp.float32) * sc
        rms_scale = jnp.ones((E,), dtype=jnp.float32)
        Wc = jax.random.normal(ks[6], (2 * E, C), dtype=jnp.float32) * 0.02
        bc = jax.random.normal(ks[7], (2 * E,), dtype=jnp.float32) * 0.02
        return {'x': x, 'mask': mask, 'conditioning': conditioning, 'Wq': Wq, 'Wk': Wk, 'Wv': Wv, 'Wo': Wo, 'rms_scale': rms_scale, 'Wc': Wc, 'bc': bc}
    _L0_cond_all = _L0_cond_setup()
    _L0_cond_in = {k: v for k, v in _L0_cond_all.items() if k in ('Wq', 'Wk', 'Wv', 'Wo', 'rms_scale', 'Wc', 'bc')}
    del _L0_cond_all

    def _L0_ffn_setup():
        import jax, jax.numpy as jnp
        import numpy as np
        TOP_K = 2
        key = jax.random.key(seed)
        ks = jax.random.split(key, 6)
        B, T, H, E, F = (2, 512, 256, 8, 1024)
        s = 0.02
        return {'hidden_states': jax.random.normal(ks[0], (B, T, H), dtype=jnp.float32), 'router_w': jax.random.normal(ks[1], (E, H), dtype=jnp.float32) * s, 'w1': jax.random.normal(ks[2], (E, F, H), dtype=jnp.float32) * s, 'b1': jax.random.normal(ks[3], (E, F), dtype=jnp.float32) * s, 'w2': jax.random.normal(ks[4], (E, H, F), dtype=jnp.float32) * s, 'b2': jax.random.normal(ks[5], (E, H), dtype=jnp.float32) * s}
    _L0_ffn_all = _L0_ffn_setup()
    _L0_ffn_in = {k: v for k, v in _L0_ffn_all.items() if k in ('router_w', 'w1', 'b1', 'w2', 'b2')}
    del _L0_ffn_all

    def _L1_cond_setup():
        import jax, jax.numpy as jnp
        import numpy as np
        TOP_K = 2
        EPS = 1e-06
        B, S, H, G, E, M = (2, 512, 256, 64, 8, 512)
        key = jax.random.key(seed)
        ks = jax.random.split(key, 16)
        s_h = 1.0 / np.sqrt(H)
        s_g = 1.0 / np.sqrt(G)
        s_m = 1.0 / np.sqrt(M)
        return {'x': jax.random.normal(ks[0], (B, S, H), jnp.float32), 'genre_embed': jax.random.normal(ks[1], (B, 1, G), jnp.float32), 'rms_w': jnp.ones((H,), jnp.float32), 'wg_W': jax.random.normal(ks[2], (H, E), jnp.float32) * s_h, 'wg_b': jnp.zeros((E,), jnp.float32), 'gg_W': jax.random.normal(ks[3], (G, E), jnp.float32) * s_g, 'gg_b': jnp.zeros((E,), jnp.float32), 'W1': jax.random.normal(ks[4], (E, H, M), jnp.float32) * s_h, 'b1': jnp.zeros((E, M), jnp.float32), 'W2': jax.random.normal(ks[5], (E, M, M), jnp.float32) * s_m, 'b2': jnp.zeros((E, M), jnp.float32), 'W3': jax.random.normal(ks[6], (E, M, H), jnp.float32) * s_m, 'b3': jnp.zeros((E, H), jnp.float32)}
    _L1_cond_all = _L1_cond_setup()
    _L1_cond_in = {k: v for k, v in _L1_cond_all.items() if k in ('rms_w', 'wg_W', 'wg_b', 'gg_W', 'gg_b', 'W1', 'b1', 'W2', 'b2', 'W3', 'b3')}
    del _L1_cond_all

    def _L1_ffn_setup():
        import jax, jax.numpy as jnp
        import numpy as np
        EPS = 1e-05
        HEADS = 8
        DIM_KEY = 128
        K = 16
        NUM_KEYS = 64
        key = jax.random.key(seed)
        ks = jax.random.split(key, 5)
        B, T, D = (1, 256, 256)
        x = jax.random.normal(ks[0], (B, T, D), dtype=jnp.float32)
        norm_w = jnp.ones((D,), dtype=jnp.float32)
        wq = jax.random.normal(ks[1], (D, DIM_KEY * HEADS * 2), dtype=jnp.float32) * 0.02
        keys = jax.random.normal(ks[2], (HEADS, NUM_KEYS, 2, DIM_KEY), dtype=jnp.float32) * 0.02
        expert_down = jax.random.normal(ks[3], (NUM_KEYS * NUM_KEYS, D), dtype=jnp.float32) * 0.02
        expert_up = jax.random.normal(ks[4], (NUM_KEYS * NUM_KEYS, D), dtype=jnp.float32) * 0.02
        return {'x': x, 'norm_w': norm_w, 'wq': wq, 'keys': keys, 'expert_down': expert_down, 'expert_up': expert_up}
    _L1_ffn_all = _L1_ffn_setup()
    _L1_ffn_in = {k: v for k, v in _L1_ffn_all.items() if k in ('norm_w', 'wq', 'keys', 'expert_down', 'expert_up')}
    del _L1_ffn_all
    return {'x': x, 'cond_256': cond_256, 'mask_SxS_bk1': mask_SxS_bk1, 'L0_cond_Wq': _L0_cond_in['Wq'], 'L0_cond_Wk': _L0_cond_in['Wk'], 'L0_cond_Wv': _L0_cond_in['Wv'], 'L0_cond_Wo': _L0_cond_in['Wo'], 'L0_cond_rms_scale': _L0_cond_in['rms_scale'], 'L0_cond_Wc': _L0_cond_in['Wc'], 'L0_cond_bc': _L0_cond_in['bc'], 'L0_ffn_router_w': _L0_ffn_in['router_w'], 'L0_ffn_w1': _L0_ffn_in['w1'], 'L0_ffn_b1': _L0_ffn_in['b1'], 'L0_ffn_w2': _L0_ffn_in['w2'], 'L0_ffn_b2': _L0_ffn_in['b2'], 'L1_cond_rms_w': _L1_cond_in['rms_w'], 'L1_cond_wg_W': _L1_cond_in['wg_W'], 'L1_cond_wg_b': _L1_cond_in['wg_b'], 'L1_cond_gg_W': _L1_cond_in['gg_W'], 'L1_cond_gg_b': _L1_cond_in['gg_b'], 'L1_cond_W1': _L1_cond_in['W1'], 'L1_cond_b1': _L1_cond_in['b1'], 'L1_cond_W2': _L1_cond_in['W2'], 'L1_cond_b2': _L1_cond_in['b2'], 'L1_cond_W3': _L1_cond_in['W3'], 'L1_cond_b3': _L1_cond_in['b3'], 'L1_ffn_norm_w': _L1_ffn_in['norm_w'], 'L1_ffn_wq': _L1_ffn_in['wq'], 'L1_ffn_keys': _L1_ffn_in['keys'], 'L1_ffn_expert_down': _L1_ffn_in['expert_down'], 'L1_ffn_expert_up': _L1_ffn_in['expert_up']}

def reference(x, cond_256, mask_SxS_bk1, L0_cond_Wq, L0_cond_Wk, L0_cond_Wv, L0_cond_Wo, L0_cond_rms_scale, L0_cond_Wc, L0_cond_bc, L0_ffn_router_w, L0_ffn_w1, L0_ffn_b1, L0_ffn_w2, L0_ffn_b2, L1_cond_rms_w, L1_cond_wg_W, L1_cond_wg_b, L1_cond_gg_W, L1_cond_gg_b, L1_cond_W1, L1_cond_b1, L1_cond_W2, L1_cond_b2, L1_cond_W3, L1_cond_b3, L1_ffn_norm_w, L1_ffn_wq, L1_ffn_keys, L1_ffn_expert_down, L1_ffn_expert_up):
    import jax
    import jax.numpy as jnp

    def _L0_cond_ref(x, mask, conditioning, Wq, Wk, Wv, Wo, rms_scale, Wc, bc):
        import jax, jax.numpy as jnp
        import numpy as np
        EPS = 1e-06
        B, S, E = x.shape
        H = 16
        D = E // H
        scale = D ** (-0.5)

        def proj(W):
            return (x @ W.T).reshape(B, S, H, D).transpose(0, 2, 1, 3)
        q, k, v = (proj(Wq), proj(Wk), proj(Wv))
        scores = jnp.einsum('bhsd,bhtd->bhst', q, k) * scale
        scores = jnp.where(mask[None, None, :, :], -jnp.inf, scores)
        attn = jax.nn.softmax(scores, axis=-1)
        out = jnp.einsum('bhst,bhtd->bhsd', attn, v)
        out = out.transpose(0, 2, 1, 3).reshape(B, S, E)
        out = out @ Wo.T
        rms = jnp.sqrt(jnp.mean(out * out, axis=-1, keepdims=True) + EPS)
        xn = out / rms * rms_scale
        mod = jax.nn.silu(conditioning) @ Wc.T + bc
        shift, sc = jnp.split(mod, 2, axis=-1)
        xn = xn * (1.0 + sc[:, None, :]) + shift[:, None, :]
        return xn

    def _L0_ffn_ref(hidden_states, router_w, w1, b1, w2, b2):
        import jax, jax.numpy as jnp
        import numpy as np
        TOP_K = 2
        x = hidden_states
        router_logits = jnp.einsum('bth,eh->bte', x, router_w)
        topk_values, topk_indices = jax.lax.top_k(router_logits, TOP_K)
        topk_weights = jax.nn.softmax(topk_values.astype(jnp.float32), axis=-1).astype(x.dtype)
        h1 = jnp.einsum('bth,efh->btef', x, w1) + b1
        h1 = jax.nn.gelu(h1, approximate=False)
        expert_outputs = jnp.einsum('btef,ehf->bteh', h1, w2) + b2
        gather_idx = topk_indices[..., None]
        topk_expert_outputs = jnp.take_along_axis(expert_outputs, gather_idx, axis=2)
        mixed_output = jnp.sum(topk_expert_outputs * topk_weights[..., None], axis=2)
        return mixed_output

    def _L1_cond_ref(x, genre_embed, rms_w, wg_W, wg_b, gg_W, gg_b, W1, b1, W2, b2, W3, b3):
        import jax, jax.numpy as jnp
        import numpy as np
        TOP_K = 2
        EPS = 1e-06
        E = W1.shape[0]
        var = jnp.mean(x * x, axis=-1, keepdims=True)
        xn = rms_w * (x * jax.lax.rsqrt(var + EPS))
        gate = xn @ wg_W + wg_b + (genre_embed @ gg_W + gg_b)
        gate_w = jax.nn.softmax(gate, axis=-1)
        topk_w, topk_i = jax.lax.top_k(gate_w, TOP_K)
        cw = jnp.sum(jax.nn.one_hot(topk_i, E, dtype=x.dtype) * topk_w[..., None], axis=-2)
        h1 = jax.nn.relu(jnp.einsum('bsh,ehm->bsem', x, W1) + b1)
        h2 = jax.nn.relu(jnp.einsum('bsem,emn->bsen', h1, W2) + b2)
        out_e = jnp.einsum('bsen,enh->bseh', h2, W3) + b3
        return jnp.einsum('bseh,bse->bsh', out_e, cw)

    def _L1_ffn_ref(x, norm_w, wq, keys, expert_down, expert_up):
        import jax, jax.numpy as jnp
        import numpy as np
        EPS = 1e-05
        HEADS = 8
        DIM_KEY = 128
        K = 16
        NUM_KEYS = 64
        B, T, D = x.shape
        inv = jax.lax.rsqrt(jnp.mean(x * x, axis=-1, keepdims=True) + EPS)
        x_norm = x * inv * norm_w
        q = (x_norm @ wq).reshape(B, T, HEADS, 2, DIM_KEY)
        sim = jnp.einsum('bthpd,hkpd->pbthk', q, keys)
        s1, i1 = jax.lax.top_k(sim[0], K)
        s2, i2 = jax.lax.top_k(sim[1], K)
        all_idx = (i1[..., :, None] * NUM_KEYS + i2[..., None, :]).reshape(B, T, HEADS, K * K)
        all_scores = (s1[..., :, None] + s2[..., None, :]).reshape(B, T, HEADS, K * K)
        final_scores, pk = jax.lax.top_k(all_scores, K)
        final_idx = jnp.take_along_axis(all_idx, pk, axis=-1)
        wd = expert_down[final_idx]
        wu = expert_up[final_idx]
        hidden = jnp.einsum('btd,bthkd->bthk', x_norm, wd)
        hidden = jax.nn.gelu(hidden, approximate=False)
        hidden = hidden * jax.nn.relu(final_scores)
        out = jnp.einsum('bthk,bthkd->btd', hidden, wu)
        return out
    x = x + _L0_ffn_ref(_L0_cond_ref(x, mask_SxS_bk1, cond_256, L0_cond_Wq, L0_cond_Wk, L0_cond_Wv, L0_cond_Wo, L0_cond_rms_scale, L0_cond_Wc, L0_cond_bc), L0_ffn_router_w, L0_ffn_w1, L0_ffn_b1, L0_ffn_w2, L0_ffn_b2)
    x = x + _L1_ffn_ref(_L1_cond_ref(x, cond_256[:, None, :], L1_cond_rms_w, L1_cond_wg_W, L1_cond_wg_b, L1_cond_gg_W, L1_cond_gg_b, L1_cond_W1, L1_cond_b1, L1_cond_W2, L1_cond_b2, L1_cond_W3, L1_cond_b3), L1_ffn_norm_w, L1_ffn_wq, L1_ffn_keys, L1_ffn_expert_down, L1_ffn_expert_up)
    return x

_drawn_inputs = setup_inputs


def setup_inputs(seed=0):
    import zlib

    import numpy as np

    out = dict(_drawn_inputs(seed))
    spreads = {'L0_cond_rms_scale': (1.0, 0.2),
     'L1_cond_rms_w': (1.0, 0.6),
     'L1_cond_wg_b': (0.0, 0.8),
     'L1_cond_gg_b': (0.0, 0.8),
     'L1_cond_b1': (0.0, 0.8),
     'L1_cond_b2': (0.0, 0.8),
     'L1_cond_b3': (0.0, 0.8),
     'L1_ffn_norm_w': (1.0, 0.6)}
    factors = {'L0_cond_bc': 4.603,
     'L0_ffn_b1': 8.0,
     'L0_ffn_b2': 3.849,
     'L1_cond_wg_W': 4.747,
     'L1_cond_gg_W': 4.847,
     'L1_cond_W1': 4.529,
     'L1_cond_W2': 4.407,
     'L1_cond_W3': 4.403,
     'L1_ffn_wq': 4.462,
     'L1_ffn_keys': 4.418,
     'L1_ffn_expert_down': 4.509,
     'L1_ffn_expert_up': 4.355}
    for name, (base, spread) in spreads.items():
        noise = np.random.default_rng([zlib.crc32(name.encode()), seed]).standard_normal(out[name].shape)
        drawn = base * np.exp(spread * noise) if base else spread * noise
        out[name] = jnp.asarray(drawn.astype(out[name].dtype))
    for name, factor in factors.items():
        out[name] = (out[name] * factor).astype(out[name].dtype)
    return out
```

```python
from contextlib import ExitStack

import numpy as np

import concourse.bass as bass
from concourse import mybir

F32 = mybir.dt.float32
BF16 = mybir.dt.bfloat16
U32 = mybir.dt.uint32
I32 = mybir.dt.int32
U8 = mybir.dt.uint8
ALU = mybir.AluOpType
ACT = mybir.ActivationFunctionType
AX = mybir.AxisListType

P = 128
BATCH, SEQ, D = 32, 64, 256
TOK = BATCH * SEQ
NT = TOK // P
KD = D // P
HEADS, DH = 16, 16
COND = 64
NE, TOPK = 8, 2
F0 = 1024
M1 = 512
GT = TOPK * NT + NE - 1
PH, PK, PKEYS, PDK = 8, 16, 64, 128
PE_N = PKEYS * PKEYS
BIG = 1e30


class Lane:

    def __init__(self, eng, sem):
        self.eng, self.sem, self.count, self.passed = eng, sem, 0, {}

    def wait(self, *after):
        for sem, value in after:
            if self.passed.get(id(sem), 0) < value:
                self.passed[id(sem)] = value
                self.eng.wait_ge(sem, value)

    def do(self, emit, *after):
        self.wait(*after)
        self.count += 1
        emit(self.eng).then_inc(self.sem, 1)
        return self.sem, self.count

    def dma(self, slot, emit, *after):
        self.wait(*after)
        slot.count += 16
        emit(self.eng).then_inc(slot.sem, 16)
        return slot.sem, slot.count


class Slot:

    def __init__(self, sem):
        self.sem, self.count = sem, 0


def build(nc, io, out, upto=99, dbg=None):
    root = ExitStack()
    with root:
        scopes = [root]

        def sb(name, shape, dt=F32):
            return scopes[-1].enter_context(nc.sbuf_tensor(name, shape, dt))

        def slot(name):
            return Slot(root.enter_context(nc.semaphore(name)))

        pe, dve, act, pool, sp = (Lane(eng, root.enter_context(nc.semaphore("done_" + n))) for n, eng in (
            ("pe", nc.tensor), ("dve", nc.vector), ("act", nc.scalar), ("pool", nc.gpsimd), ("sp", nc.sync)))
        banks = root.enter_context(nc.psum_tensor("banks", [P, 8, 512], F32))

        ident = sb("ident", [P, P])
        lower = sb("lower", [P, P])
        ones = sb("ones", [P, P])
        x_sb = sb("x_sb", [P, NT, D])
        att = sb("att", [P, NT, D])
        REG = 4096
        NREG = NE
        iota16 = sb("iota16", [P, NE, 16])
        iota8 = sb("iota8", [P, NT, NE])
        iotag = sb("iotag", [P, GT, NE])
        b1c = sb("b1c", [P, NE, F0 // P])
        m1c = sb("m1c", [P, NE, M1 // P])
        m2c = sb("m2c", [P, NE, M1 // P])
        ybias = sb("ybias", [P, NE, D])
        cond1 = sb("cond1", [COND + 2, BATCH])
        gg1 = sb("gg1", [COND + 2, NE])
        rw = sb("rw", [P, KD, NE])
        wgw = sb("wgw", [P, KD, NE])
        rmsw = sb("rmsw", [P, KD])
        normw = sb("normw", [P, KD])
        gate = sb("gate", [P, NT, TOPK])
        slots = sb("slots", [P, TOPK, NT], U32)
        tile_e = sb("tile_e", [P, GT], I32)
        small = sb("small", [P, 64])

        rows_in = nc.dram_tensor("rows_in", [GT * P, D], F32, kind="Internal").ap()
        rows_out = nc.dram_tensor("rows_out", [GT * P, D], F32, kind="Internal").ap()

        ld = {n: slot("ld_" + n) for n in
              ("x", "bias", "small", "wqkvo", "mod", "w0", "w1", "xt0", "xt1", "zero", "scat",
               "store", "mask", "xg0", "xg1", "xg2", "ys0", "ys1", "mix0", "mix1", "mix2", "mix3")}

        c1 = pool.do(lambda e: e.memset(ident[:, :], 0.0))
        c1 = pool.do(lambda e: e.affine_select(out=ident[:, :], in_=ident[:, :], compare_op=ALU.not_equal,
                                               fill=1.0, base=0, pattern=[[-1, P]], channel_multiplier=1), c1)
        c2 = pool.do(lambda e: e.memset(ones[:, :], 1.0))
        c3 = pool.do(lambda e: e.affine_select(out=lower[:, :], in_=ones[:, :], compare_op=ALU.is_gt,
                                               fill=0.0, base=0, pattern=[[1, P]], channel_multiplier=-1), c2)
        c4 = pool.do(lambda e: e.iota(iota16[:, :, :], [[0, NE], [P, 16]], base=0, channel_multiplier=0,
                                      allow_small_or_imprecise_dtypes=True))
        c4 = pool.do(lambda e: e.iota(iota8[:, :, :], [[0, NT], [1, NE]], base=0, channel_multiplier=0,
                                      allow_small_or_imprecise_dtypes=True))
        c_all = pool.do(lambda e: e.iota(iotag[:, :, :], [[1, GT], [0, NE]], base=0, channel_multiplier=0,
                                         allow_small_or_imprecise_dtypes=True))

        hs_b = [sb(f"hs{n}", [P, 1024]) for n in range(2)]
        weights = sb("weights", [P, NREG * REG])

        NA = 4
        arena = [(NREG - NA) * REG]

        def carve(*shape):
            n = int(np.prod(shape))
            piece = weights[:, arena[0]:arena[0] + n]
            arena[0] += n
            if len(shape) == 1:
                return piece
            names = " ".join(f"d{j}" for j in range(len(shape)))
            return piece.rearrange(f"p ({names}) -> p {names}", **{f"d{j}": shape[j] for j in range(len(shape))})

        wq, wk, wv, wo = (carve(KD, D) for _ in range(4))
        xt = [carve(KD, 512) for _ in range(2)]
        qt = carve(KD, 512)
        kts = carve(KD, 512)
        kbd = [carve(KD, 8, SEQ) for _ in range(2)]
        scm = carve(HEADS, SEQ)
        prb = carve(HEADS, SEQ)
        pts = carve(8, P)
        vbd = [carve(8, 2 * DH) for _ in range(2)]
        ots = carve(KD, P)
        sqj = carve(D)
        hmask = sb("hmask", [P, 8, 1])
        mask4 = sb("mask4", [P, SEQ // 4], U32)
        mask8 = mask4[:, :].bitcast(U8)
        mneg = sb("mneg", [P, 1, SEQ])
        valid = sb("valid", [P, 4])
        mx = sb("mx", [P, HEADS])
        nmx = sb("nmx", [P, HEADS])
        rsum = sb("rsum", [P, HEADS])
        rinv = sb("rinv", [P, HEADS])
        ssq = sb("ssq", [P, NT])
        rms = sb("rms", [P, NT])

        sp.dma(ld["wqkvo"], lambda e: e.dma_start(wq[:, :, :], io["wqT"].rearrange("(c p) n -> p c n", p=P)))
        xt_ld = [sp.dma(ld[f"xt{n}"], lambda e, n=n: e.dma_start(
            xt[n][:, :, :], io["xT"][:, n * 512:(n + 1) * 512].rearrange("(c p) t -> p c t", p=P))) for n in range(2)]
        for t, n in ((wk, "wkT"), (wv, "wvT"), (wo, "woT")):
            w_ld = sp.dma(ld["wqkvo"], lambda e, t=t, n=n: e.dma_start(
                t[:, :, :], io[n].rearrange("(c p) n -> p c n", p=P)))
        sp.dma(ld["mask"], lambda e: e.dma_start(mask4[0:SEQ, :], io["mask"]))
        m_ld = sp.dma(ld["mask"], lambda e: e.dma_start(mask4[SEQ:P, :], io["mask"]))
        x_ld = sp.dma(ld["x"], lambda e: e.dma_start(x_sb[:, :, :], io["x"].rearrange("(n p) d -> p n d", p=P)))

        def small_load(dst, src):
            return sp.dma(ld["small"], lambda e: e.dma_start(dst, src))
        small_load(rw[:, :, :], io["routerT"].rearrange("(c p) n -> p c n", p=P))
        small_load(wgw[:, :, :], io["wg_W"].rearrange("(c p) n -> p c n", p=P))
        small_load(rmsw[:, :], io["rms_w"])
        small_load(normw[:, :], io["norm_w"])
        small_load(b1c[:, :, :], io["b1"])
        small_load(m1c[:, :, :], io["m1"])
        small_load(m2c[:, :, :], io["m2"])
        small_load(cond1[0:COND, :], io["condT"])
        small_load(gg1[0:COND, :], io["gg_W"])
        small_load(gg1[COND:COND + 1, :], io["gg_b"])
        small_load(gg1[COND + 1:COND + 2, :], io["wg_b"])
        small_load(ybias[:, :, :], io["b2"].rearrange("(a e) d -> a e d", a=1).to_broadcast([P, NE, D]))
        modw = carve(2 * D)[0:COND + 1, :]
        rsbc = carve(D)
        small_load(modw[0:COND, :], io["wcT"])
        small_load(modw[COND:COND + 1, :], io["bc"])
        s_ld = small_load(rsbc[:, :], io["rms_scale"].to_broadcast([P, D]))

        def region(r):
            return weights[:, r * REG:(r + 1) * REG]

        def load_l0(e_, *after):
            w = region(e_)
            sp.dma(ld["w0"], lambda e: e.dma_start(w[:, 0:2048].rearrange("p (c f) -> p c f", c=KD),
                                                   io["w1T"][e_].rearrange("(c p) f -> p c f", p=P)), *after)
            return sp.dma(ld["w0"], lambda e: e.dma_start(w[:, 2048:4096].rearrange("p (c f) -> p c f", c=F0 // P),
                                                          io["w2T"][e_].rearrange("(c p) f -> p c f", p=P)))

        for e_ in range(NREG - NA):
            load_l0(e_)
        zt = hs_b[1][:, 0:2 * D]
        z = pool.do(lambda e: e.memset(zt, 0.0))
        for j in range(0, GT - 1, 2):
            sp.dma(ld["zero"], lambda e: e.dma_start(rows_in[j * P:(j + 2) * P, :].rearrange("(a p) d -> p a d", p=P),
                                                     zt.rearrange("p (a d) -> p a d", a=2)), z)
        zero_ok = sp.dma(ld["zero"], lambda e: e.dma_start(rows_in[(GT - 1) * P:GT * P, :], zt[:, 0:D]))

        h1 = pool.do(lambda e: e.memset(hmask[:, :, :], 1.0))
        h1 = pool.do(lambda e: e.affine_select(out=hmask[:, :, 0], in_=hmask[:, :, 0], compare_op=ALU.is_ge, fill=0.0,
                                               base=0, pattern=[[-DH, 8]], channel_multiplier=1), h1)
        hm_ok = pool.do(lambda e: e.affine_select(out=hmask[:, :, 0], in_=hmask[:, :, 0], compare_op=ALU.is_ge, fill=0.0,
                                                  base=DH - 1, pattern=[[DH, 8]], channel_multiplier=-1), h1)
        v0 = [pool.do(lambda e, v=v: e.memset(v, 0.0)) for v in vbd][-1]
        mk = dve.do(lambda e: e.tensor_scalar(mneg[:, 0, :], mask8, -BIG, None, ALU.mult), m_ld)
        mk1 = dve.do(lambda e: e.tensor_scalar(scm[:, 0, :], mask8, -1.0, 1.0, ALU.mult, ALU.add))
        mk2 = dve.do(lambda e: e.tensor_reduce(valid[:, 0:1], scm[:, 0, :], AX.X, ALU.max), mk1)
        mk3 = dve.do(lambda e: e.reciprocal(valid[:, 1:2], valid[:, 0:1]), mk2)
        mk4 = dve.do(lambda e: e.tensor_tensor(valid[:, 2:3], valid[:, 0:1], valid[:, 1:2], ALU.mult), mk3)

        B_S, B_T, B_P, B_O, B_W = 0, 2, 4, 5, 6
        free = {n: [] for n in ("s", "t", "p4", "p7", "o", "w", "qt", "kts", "kbd0", "kbd1", "vbd0", "vbd1",
                                "scm", "prb", "pts", "ots", "xt0", "xt1", "rsum")}
        free["vbd0"] = free["vbd1"] = [v0]
        free["scm"] = [mk2]
        pb = [4, 7]
        nproj = 0

        def project(w, src, c, after):
            nonlocal nproj
            b = pb[nproj % 2]
            nproj += 1

            def emit(e):
                for k in range(KD):
                    m = e.matmul(banks[:, b, :], w[:, k, c * P:(c + 1) * P], src[:, k, :], start=(k == 0), stop=(k == KD - 1))
                return m
            return b, pe.do(emit, *after, *free[f"p{b}"])

        att_ok = []
        for g in range(4):
            xg = xt[g % 2]
            if g >= 2:
                xt_ld.append(sp.dma(ld[f"xt{g % 2}"], lambda e, g=g: e.dma_start(
                    xt[g % 2][:, :, :], io["xT"][:, g * 512:(g + 1) * 512].rearrange("(c p) t -> p c t", p=P)),
                    *free[f"xt{g % 2}"]))
            q_ok, k_ok = [], []
            for c in range(KD):
                b, t = project(wq, xg, c, [w_ld, xt_ld[g]])
                t = act.do(lambda e, b=b, c=c: e.copy(qt[:, c, :], banks[:, b, :]), t, *free["qt"])
                free[f"p{b}"] = [t]
                q_ok.append(t)
            for c in range(KD):
                b, t = project(wk, xg, c, [])
                t = act.do(lambda e, b=b, c=c: e.copy(kts[:, c, :], banks[:, b, :]), t, *free["kts"])
                free[f"p{b}"] = [t]
                k_ok.append(t)
            for i in range(4 * g, 4 * g + 4):
                tl = (i % 4) * P
                v_ok, kb_ok = [], []
                for bb in range(2):
                    t0 = tl + bb * SEQ
                    vb = pb[nproj % 2]
                    nproj += 1

                    def emit(e, t0=t0, vb=vb):
                        for par in range(2):
                            for k in range(KD):
                                m = e.matmul(banks[par * SEQ:(par + 1) * SEQ, vb, 0:P], xg[:, k, t0:t0 + SEQ],
                                             wv[:, k, par * P:(par + 1) * P], start=(k == 0), stop=(k == KD - 1))
                        return m
                    t = pe.do(emit, *free[f"p{vb}"])
                    free[f"xt{g % 2}"] = [t]
                    for par in range(2):
                        t2 = dve.do(lambda e, par=par, bb=bb, vb=vb: e.tensor_copy(
                            vbd[bb][par * SEQ:(par + 1) * SEQ, :, par * DH:(par + 1) * DH],
                            banks[par * SEQ:(par + 1) * SEQ, vb, 0:P].rearrange("p (h d) -> p h d", h=8)),
                            t, *free[f"vbd{bb}"])
                    free[f"p{vb}"] = [t2]
                    v_ok.append(t2)
                    t3 = dve.do(lambda e, bb=bb, t0=t0: e.tensor_tensor(
                        kbd[bb].rearrange("p c h t -> p c h t")[:, 0, :, :],
                        kts[:, 0:1, t0:t0 + SEQ].to_broadcast([P, 8, SEQ]),
                        hmask[:, :, :].to_broadcast([P, 8, SEQ]), ALU.mult),
                        k_ok[-1], hm_ok, *free[f"kbd{bb}"])
                    t3 = dve.do(lambda e, bb=bb, t0=t0: e.tensor_tensor(
                        kbd[bb][:, 1, :, :],
                        kts[:, 1:2, t0:t0 + SEQ].to_broadcast([P, 8, SEQ]),
                        hmask[:, :, :].to_broadcast([P, 8, SEQ]), ALU.mult))
                    kb_ok.append(t3)
                free["kts"] = [kb_ok[-1]]

                def emit(e, tl=tl):
                    for bb in range(2):
                        for c in range(KD):
                            m = e.matmul(banks[bb * SEQ:(bb + 1) * SEQ, B_S + c, :],
                                         qt[:, c, tl + bb * SEQ:tl + (bb + 1) * SEQ],
                                         kbd[bb][:, c, :, :].rearrange("p h t -> p (h t)"), start=True, stop=True)
                    return m
                s_ok = pe.do(emit, kb_ok[-1], q_ok[-1], *free["s"])
                free["kbd0"] = free["kbd1"] = free["qt"] = [s_ok]
                sc = banks[:, B_S:B_S + 2, :].rearrange("p a (h t) -> p (a h) t", h=8)
                t = dve.do(lambda e, sc=sc: e.tensor_tensor(scm, sc, mneg[:, :, :].to_broadcast([P, HEADS, SEQ]), ALU.add),
                           s_ok, mk, *free["scm"])
                free["s"] = [t]
                t = dve.do(lambda e: e.tensor_reduce(mx[:, :], scm, AX.X, ALU.max), t, *free["rsum"])
                t = dve.do(lambda e: e.tensor_scalar(nmx[:, :], mx[:, :], -(DH ** -0.5), None, ALU.mult), t)

                for h in range(HEADS):
                    t4 = act.do(lambda e, h=h: e.activation(prb[:, h, :], scm[:, h, :], ACT.Exp, bias=nmx[:, h:h + 1],
                                                            scale=DH ** -0.5, accum_out=rsum[:, h:h + 1]),
                                t, *free["prb"])
                free["scm"] = [t4]
                t = dve.do(lambda e: e.reciprocal(rinv[:, :], rsum[:, :]), t4)
                free["rsum"] = [t]
                t = dve.do(lambda e: e.tensor_scalar(rinv[:, :], rinv[:, :], valid[:, 2:3], None, ALU.mult), t, mk4)
                p_ok = dve.do(lambda e: e.tensor_tensor(
                    prb, prb, rinv[:, :].rearrange("p (h o) -> p h o", o=1).to_broadcast([P, HEADS, SEQ]), ALU.mult), t)

                def emit(e):
                    for hp in range(8):
                        m = e.transpose(banks[:, B_T + hp // 4, (hp % 4) * P:(hp % 4 + 1) * P],
                                        prb[:, 2 * hp:2 * hp + 2, :].rearrange("p h t -> p (h t)"), ident[:, :])
                    return m
                t = pe.do(emit, p_ok, c_all, *free["t"])
                free["prb"] = [t]
                t1 = act.do(lambda e: e.copy(pts[:, 0:4, :].rearrange("p h t -> p (h t)"), banks[:, B_T, :]), t, *free["pts"])
                t2 = act.do(lambda e: e.copy(pts[:, 4:8, :].rearrange("p h t -> p (h t)"), banks[:, B_T + 1, :]))
                free["t"] = [t2]

                def emit(e):
                    for bb in range(2):
                        for hp in range(8):
                            m = e.matmul(banks[32 * (hp % 4):32 * (hp % 4) + 32, B_O, (hp // 4) * P + bb * SEQ:(hp // 4) * P + (bb + 1) * SEQ],
                                         vbd[bb][:, hp, :], pts[:, hp, bb * SEQ:(bb + 1) * SEQ], start=True, stop=True,
                                         tile_position=(0, 32 * (hp % 4)))
                    return m
                t = pe.do(emit, t2, v_ok[-1], *free["o"])
                free["pts"] = free["vbd0"] = free["vbd1"] = [t]
                t = dve.do(lambda e: e.tensor_copy(ots.rearrange("p c t -> p (c t)"), banks[:, B_O, 0:2 * P]), t, *free["ots"])
                free["o"] = [t]

                def emit(e):
                    for c in range(KD):
                        m = e.matmul(banks[:, B_W, 0:D], ots[:, c, :], wo[:, c, :], start=(c == 0), stop=(c == KD - 1))
                    return m
                t = pe.do(emit, t, *free["w"])
                free["ots"] = [t]
                a_ok = dve.do(lambda e, i=i: e.tensor_copy(att[:, i, :], banks[:, B_W, 0:D]), t)
                free["w"] = [a_ok]
                t = act.do(lambda e, i=i: e.activation(sqj, att[:, i, :], ACT.Square, accum_out=ssq[:, i:i + 1]), a_ok)
                att_ok.append(t)

        def rsqrt_cols(dst, src, eps, after):
            t = dve.do(lambda e: e.tensor_scalar(dst, src, 1.0 / D, eps, ALU.mult, ALU.add), *after)
            t = act.do(lambda e: e.activation(dst, dst, ACT.Sqrt), t)
            return dve.do(lambda e: e.reciprocal(dst, dst), t)
        r_ok = rsqrt_cols(rms[:, :], ssq[:, :], 1e-6, att_ok)
        silu1 = sb("silu1", [COND + 1, BATCH])
        condx = sb("condx", [COND + 2, 2, P])
        t = dve.do(lambda e: e.memset(silu1[COND:COND + 1, :], 1.0))
        t1 = dve.do(lambda e: e.memset(cond1[COND:COND + 2, :], 1.0))
        si_ok = act.do(lambda e: e.activation(silu1[0:COND, :], cond1[0:COND, :], ACT.Silu), s_ld)

        gmod = sb("gmod", [P, 2, D])
        xnt = sb("xnt", [P, 2, KD, P])
        logit = sb("logit", [P, NT, NE])
        cfree = [[], []]
        mfree, gfree, tfree, xfree = [[], []], [[], []], [[], []], [[], []]
        xn_ok = []
        for i in range(NT):
            n = i % 2
            ce = act.do(lambda e, i=i, n=n: e.copy(
                condx[0:COND + 1, n, :].rearrange("p (b s) -> p b s", b=2),
                silu1[:, 2 * i:2 * i + 2].rearrange("p (b s) -> p b s", s=1).to_broadcast([COND + 1, 2, SEQ])),
                si_ok, t, *cfree[n])
            m_ok = pe.do(lambda e, n=n: e.matmul(banks[:, n, :], condx[0:COND + 1, n, :], modw[:, :], start=True, stop=True),
                         ce, s_ld, *mfree[n], *(free["s"] if i < 2 else []))
            cfree[n] = [m_ok]
            t1 = dve.do(lambda e, n=n: e.scalar_tensor_tensor(gmod[:, n, :], banks[:, n, D:2 * D], 1.0, rsbc[:, :], ALU.add, ALU.mult),
                        m_ok)
            t1 = dve.do(lambda e, n=n, i=i: e.scalar_tensor_tensor(att[:, i, :], att[:, i, :], rms[:, i:i + 1], gmod[:, n, :],
                                                                   ALU.mult, ALU.mult), t1, r_ok, att_ok[-1])
            t1 = dve.do(lambda e, n=n, i=i: e.tensor_tensor(att[:, i, :], att[:, i, :], banks[:, n, 0:D], ALU.add), t1)
            mfree[n] = [t1]
            xn_ok.append(t1)

            def emit(e, i=i, n=n):
                for c in range(KD):
                    m = e.transpose(banks[:, 2 + n, c * P:(c + 1) * P], att[:, i, c * P:(c + 1) * P], ident[:, :])
                return m
            t1 = pe.do(emit, t1, *tfree[n], *(free["t"] if i < 2 else []))
            t1 = act.do(lambda e, n=n: e.copy(xnt[:, n, :, :].rearrange("p c t -> p (c t)"), banks[:, 2 + n, 0:2 * P]), t1, *xfree[n])
            tfree[n] = [t1]

            def emit(e, i=i, n=n):
                for c in range(KD):
                    m = e.matmul(banks[:, 4, i * NE:(i + 1) * NE], xnt[:, n, c, :], rw[:, c, :], start=(c == 0), stop=(c == KD - 1))
                return m
            l_ok = pe.do(emit, t1, *(free["p4"] if i == 0 else []))
            xfree[n] = [l_ok]
        t = dve.do(lambda e: e.tensor_copy(logit[:, :, :].rearrange("p a b -> p (a b)"), banks[:, 4, 0:NT * NE]), l_ok)
        a_end = [att_ok[-1], xn_ok[-1], l_ok]
        for e_ in range(NREG - NA, NE):
            w0_ld = load_l0(e_, *a_end)

        if upto == 1:
            dbg.update(att=att, logit=logit)
            w1 = sp.dma(ld["store"], lambda e: e.dma_start(io["dbg0"].rearrange("(n p) d -> p n d", p=P), att[:, :, :]), t, xn_ok[-1])
            w1 = sp.dma(ld["store"], lambda e: e.dma_start(io["dbg1"].rearrange("(n p) d -> p n d", p=P), logit[:, :, :]), t)
            sp.wait(w1)
            return

        onehot = sb("onehot", [P, TOPK, NT, NE])
        both = sb("both", [P, NT, NE])
        before = sb("before", [P, NT, NE])
        top8 = sb("top8", [P, NT, 8])
        idx8 = sb("idx8", [P, NT, 8], U32)
        count = sb("count", [P, NE])
        ntile = sb("ntile", [P, NE])
        upto_e = sb("upto_e", [P, NE])
        base_e = sb("base_e", [P, NE])
        thr = sb("thr", [P, NE, 16])
        place = sb("place", [P, NT, NE])
        hit = sb("hit", [P, NT, NE])
        slot_f = sb("slot_f", [P, TOPK, NT])
        te = sb("te", [P, GT, NE])
        te_f = sb("te_f", [P, GT])
        zcol = sb("zcol", [P, NT])

        def route(score, region_of_first, *after):
            for i in range(NT):
                t = dve.do(lambda e: e.max(top8[:, i, :], score[:, i, :]), *after)
                t_i = dve.do(lambda e: e.max_index(idx8[:, i, :], top8[:, i, :], score[:, i, :]), t)
            for k in range(TOPK):
                t = dve.do(lambda e: e.tensor_tensor(onehot[:, k, :, :], iota8[:, :, :],
                                                     idx8[:, :, k:k + 1].to_broadcast([P, NT, NE]), ALU.is_equal), t_i, c_all)
            t = dve.do(lambda e: e.tensor_tensor(both[:, :, :], onehot[:, 0, :, :], onehot[:, 1, :, :], ALU.add), t)
            z = dve.do(lambda e: e.memset(before[:, 0, :], 0.0))
            for i in range(1, NT):
                t = z = dve.do(lambda e: e.tensor_tensor(before[:, i, :], before[:, i - 1, :], both[:, i - 1, :], ALU.add), t, z)
            t = dve.do(lambda e: e.tensor_tensor(hit[:, 0, :], before[:, NT - 1, :], both[:, NT - 1, :], ALU.add), t)
            p_ok = pe.do(lambda e: (e.matmul(banks[:, 4, 0:NT * NE], lower[:, :], both[:, :, :].rearrange("p a b -> p (a b)"), start=True, stop=False),
                                    e.matmul(banks[:, 4, 0:NT * NE], ones[:, :], before[:, :, :].rearrange("p a b -> p (a b)"), start=False, stop=True),
                                    )[-1], t, *after)
            n_ok = pe.do(lambda e: e.matmul(banks[:, 5, 0:NE], ones[:, :], hit[:, 0, :], start=True, stop=True))
            t = dve.do(lambda e: e.tensor_copy(place[:, :, :].rearrange("p a b -> p (a b)"), banks[:, 4, 0:NT * NE]), p_ok)
            t = dve.do(lambda e: e.tensor_copy(count[:, :], banks[:, 5, 0:NE]), n_ok)
            t = dve.do(lambda e: e.tensor_tensor(thr[:, :, :], count[:, :].rearrange("p (a o) -> p a o", o=1).to_broadcast([P, NE, 16]),
                                                 iota16[:, :, :], ALU.is_gt), t)
            t = dve.do(lambda e: e.tensor_reduce(ntile[:, :], thr[:, :, :], AX.X, ALU.add), t)
            t = dve.do(lambda e: e.tensor_copy(upto_e[:, 0:1], ntile[:, 0:1]), t)
            for k in range(1, NE):
                t = dve.do(lambda e: e.tensor_tensor(upto_e[:, k:k + 1], upto_e[:, k - 1:k], ntile[:, k:k + 1], ALU.add), t)
            t = dve.do(lambda e: e.tensor_tensor(base_e[:, :], upto_e[:, :], ntile[:, :], ALU.subtract), t)
            t1 = dve.do(lambda e: e.tensor_scalar(base_e[:, :], base_e[:, :], float(P), None, ALU.mult), t)
            t = dve.do(lambda e: e.tensor_tensor(te[:, :, :], iotag[:, :, :],
                                                 upto_e[:, :].rearrange("p (o a) -> p o a", o=1).to_broadcast([P, GT, NE]), ALU.is_ge), t)
            t = dve.do(lambda e: e.tensor_reduce(te_f[:, :], te[:, :, :], AX.X, ALU.add), t)
            te_ok = dve.do(lambda e: e.tensor_scalar(tile_e[:, :], te_f[:, :], float(NE - 1), None, ALU.min), t)
            t = dve.do(lambda e: e.tensor_tensor(place[:, :, :], place[:, :, :],
                                                 base_e[:, :].rearrange("p (o a) -> p o a", o=1).to_broadcast([P, NT, NE]), ALU.add), t1)
            for k in range(TOPK):
                t2 = dve.do(lambda e: e.tensor_tensor(hit[:, :, :], place[:, :, :], onehot[:, k, :, :], ALU.mult), t)
                t = dve.do(lambda e: e.tensor_reduce(slot_f[:, k, :], hit[:, :, :], AX.X, ALU.add), t2)
            slot_ok = dve.do(lambda e: e.tensor_copy(slots[:, :, :], slot_f[:, :, :]), t)
            return slot_ok, te_ok

        def scatter(src, *after):
            for i in range(NT):
                for k in range(TOPK):
                    t = pool.dma(ld["scat"], lambda e: e.indirect_dma_start(
                        rows_in[:, :], bass.IndirectOffsetOnAxis(ap=slots[:, k, i:i + 1], axis=0), src[:, i, :], None), *after)
            return t

        def gather_mix(use, *after):
            done = []
            for i in range(NT):
                for k in range(TOPK):
                    n = (i * TOPK + k) % 4
                    g = pool.dma(ld[f"mix{n}"], lambda e: e.indirect_dma_start(
                        mixb[:, n, :], None, rows_out[:, :], bass.IndirectOffsetOnAxis(ap=slots[:, k, i:i + 1], axis=0)),
                        *after, *mix_free[n])
                    if k == 0:
                        g0 = g
                n = i * TOPK % 4
                t = use(i, mixb[:, n, :], mixb[:, n + 1, :], g0, g)
                mix_free[n] = mix_free[n + 1] = [t]
                done.append(t)
            return done

        xg_b = [sb(f"xg{n}", [P, D]) for n in range(3)]
        ht_b = [sb(f"ht{n}", [P, 1024]) for n in range(2)]
        ys_b = [sb(f"ys{n}", [P, D]) for n in range(2)]
        xgt_b = [xnt[:, n, :, :] for n in range(2)]
        bcol = sb("bcol", [P, 2, 8])
        mixb = hs_b[0][:, :].rearrange("p (n d) -> p n d", n=4)
        mix_free = [[], [], [], []]
        B_X, B_H, B_T2, B_Y = 0, 1, 3, 5

        def expert_of(lane, j, te_ok):
            lane.wait(te_ok)
            return lane.eng.value_load(tile_e[0:1, j:j + 1], min_val=0, max_val=NE - 1)

        def expert_layer0(scat_ok, te_ok, w_ok, bank_free):
            xfree_, xtfree, hsfree, htfree, ysfree = [[], [], []], [[], []], [[], []], [[], []], [[], []]
            bfree = {b: list(bank_free) for b in range(8)}
            xt_ok, last_h, store = {}, {}, None
            bcfree = [[], []]

            def inputs(j):
                n = j % 3
                x_ok = sp.dma(ld[f"xg{n}"], lambda e: e.dma_start(xg_b[n][:, :], rows_in[j * P:(j + 1) * P, :]),
                              scat_ok, *xfree_[n])
                t = pe.do(lambda e: [e.transpose(banks[:, B_X, c * P:(c + 1) * P], xg_b[n][:, c * P:(c + 1) * P], ident[:, :])
                                     for c in range(KD)][-1], x_ok, *bfree[B_X])
                xfree_[n] = [t]
                t = dve.do(lambda e: e.tensor_copy(xgt_b[j % 2].rearrange("p c t -> p (c t)"), banks[:, B_X, 0:D]),
                           t, *xtfree[j % 2])
                bfree[B_X] = [t]
                xt_ok[j] = t

            def outputs(j, h_ok, rd):
                by = B_Y + j % 2
                w2 = 2048
                t = pe.do(lambda e: [e.matmul(banks[:, by, 0:D], ht_b[j % 2][:, c * P:(c + 1) * P],
                                              weights[:, bass.ds(rd * REG + w2 + c * D, D)],
                                              start=(c == 0), stop=(c == F0 // P - 1)) for c in range(F0 // P)][-1],
                          h_ok, *bfree[by])
                htfree[j % 2] = [t]
                rv = expert_of(dve, j, te_ok)
                t = dve.do(lambda e: e.tensor_tensor(ys_b[j % 2][:, :], banks[:, by, 0:D],
                                                     ybias_f[:, bass.ds(rv * D, D)], ALU.add), t, *ysfree[j % 2])
                bfree[by] = [t]
                t = sp.dma(ld[f"ys{j % 2}"], lambda e: e.dma_start(rows_out[j * P:(j + 1) * P, :], ys_b[j % 2][:, :]), t)
                ysfree[j % 2] = [t]
                return t

            inputs(0)
            pending, ends = None, []
            for j in range(GT):
                n = j % 2
                rd = expert_of(pe, j, te_ok)

                def emit(e):
                    for half in range(2):
                        for k in range(KD):
                            m = e.matmul(banks[:, B_H + half, :], xgt_b[n][:, k, :],
                                         weights[:, bass.ds(rd * REG + k * F0 + half * 512, 512)],
                                         start=(k == 0), stop=(k == KD - 1))
                    return m
                t = pe.do(emit, xt_ok[j], *w_ok, *bfree[B_H], *bfree[B_H + 1])
                xtfree[n] = [t]
                t1 = dve.do(lambda e: e.tensor_copy(hs_b[n][:, 0:512], banks[:, B_H, :]), t, *hsfree[n])
                t2 = act.do(lambda e: e.copy(hs_b[n][:, 512:1024], banks[:, B_H + 1, :]), t, *hsfree[n])
                bfree[B_H], bfree[B_H + 1] = [t1], [t2]
                if pending:
                    ends.append(outputs(*pending))
                if j + 1 < GT:
                    inputs(j + 1)
                t = pe.do(lambda e: [e.transpose(banks[:, B_T2 + c // 4, (c % 4) * P:(c % 4 + 1) * P],
                                                 hs_b[n][:, c * P:(c + 1) * P], ident[:, :]) for c in range(8)][-1],
                          t1, t2, *bfree[B_T2], *bfree[B_T2 + 1])
                hsfree[n] = [t]
                rv = expert_of(dve, j, te_ok)
                bc = dve.do(lambda e: e.tensor_copy(bcol[:, n, :], b1f[:, bass.ds(rv * 8, 8)]), *bcfree[n])
                for c in range(8):
                    h_ok = act.do(lambda e: e.activation(ht_b[n][:, c * P:(c + 1) * P],
                                                         banks[:, B_T2 + c // 4, (c % 4) * P:(c % 4 + 1) * P],
                                                         ACT.Gelu, bias=bcol[:, n, c:c + 1]), t, bc, *htfree[n])
                bcfree[n] = [h_ok]
                bfree[B_T2] = bfree[B_T2 + 1] = [h_ok]
                pending = (j, h_ok, rd)
            ends.append(outputs(*pending))
            return ends[-2:], [h_ok, bfree[B_Y + (GT - 1) % 2][0], bfree[B_Y + GT % 2][0]]

        ybias_f = ybias[:, :, :].rearrange("p e d -> p (e d)")
        b1f = b1c[:, :, :].rearrange("p e c -> p (e c)")

        slot_ok, te_ok = route(logit, None, t)
        g1 = dve.do(lambda e: e.tensor_tensor(slot_f[:, 0, :], top8[:, :, 1], top8[:, :, 0], ALU.subtract), slot_ok)
        g2 = act.do(lambda e: e.activation(slot_f[:, 1, :], slot_f[:, 0, :], ACT.Exp), g1)
        g3 = dve.do(lambda e: e.tensor_scalar(slot_f[:, 0, :], slot_f[:, 1, :], 1.0, None, ALU.add), g2)
        g4 = dve.do(lambda e: e.reciprocal(gate[:, :, 0], slot_f[:, 0, :]), g3)
        gate_ok = dve.do(lambda e: e.tensor_tensor(gate[:, :, 1], gate[:, :, 0], slot_f[:, 1, :], ALU.mult), g4)
        scat = scatter(att, slot_ok, zero_ok, xn_ok[-1])
        ends, drained = expert_layer0(scat, te_ok, [w0_ld], [t, slot_ok])

        def mix0(i, y0, y1, ok0, ok1):
            t = dve.do(lambda e: e.scalar_tensor_tensor(x_sb[:, i, :], y0, gate[:, i, 0:1], x_sb[:, i, :], ALU.mult, ALU.add),
                       ok0, gate_ok, x_ld)
            return dve.do(lambda e: e.scalar_tensor_tensor(x_sb[:, i, :], y1, gate[:, i, 1:2], x_sb[:, i, :], ALU.mult, ALU.add),
                          t, ok1)
        x1_ok = gather_mix(mix0, *ends, *drained)
        if upto == 2:
            w1 = sp.dma(ld["store"], lambda e: e.dma_start(io["dbg0"].rearrange("(n p) d -> p n d", p=P), x_sb[:, :, :]), x1_ok[-1])
            sp.wait(w1)
            return

        def load_l1(r, *after):
            w = region(r)
            sp.dma(ld["w1"], lambda e: e.dma_start(w[:, 0:1024].rearrange("p (c f) -> p c f", c=KD),
                                                   io["W1"][r].rearrange("(c p) f -> p c f", p=P)), *after)
            sp.dma(ld["w1"], lambda e: e.dma_start(w[:, 1024:3072].rearrange("p (c f) -> p c f", c=M1 // P),
                                                   io["W2"][r].rearrange("(c p) f -> p c f", p=P)))
            return sp.dma(ld["w1"], lambda e: e.dma_start(w[:, 3072:4096].rearrange("p (c f) -> p c f", c=M1 // P),
                                                          io["W3"][r].rearrange("(c p) f -> p c f", p=P)))
        for r_ in range(NE):
            w1_ld = load_l1(r_, *drained, *ends)
        yb_ld = sp.dma(ld["bias"], lambda e: e.dma_start(
            ybias[:, :, :], io["m3"].rearrange("(a e) d -> a e d", a=1).to_broadcast([P, NE, D])))

        wgr = sb("wgr", [P, KD, NE])
        score = sb("score", [P, NT, NE])
        smx = sb("smx", [P, NT])
        for c in range(KD):
            wg_ok = dve.do(lambda e: e.tensor_scalar(wgr[:, c, :], wgw[:, c, :], rmsw[:, c:c + 1], None, ALU.mult), s_ld)
        for i in range(NT):
            n = i % 2
            sq_ok = act.do(lambda e: e.activation(ys_b[n][:, :], x_sb[:, i, :], ACT.Square, accum_out=ssq[:, i:i + 1]), x1_ok[i], *ends)
            ce = act.do(lambda e: e.copy(
                condx[:, n, :].rearrange("p (b s) -> p b s", b=2),
                cond1[:, 2 * i:2 * i + 2].rearrange("p (b s) -> p b s", s=1).to_broadcast([COND + 2, 2, SEQ])),
                *cfree[n])
            cg_ok = pe.do(lambda e: e.matmul(banks[:, 5, i * NE:(i + 1) * NE], condx[:, n, :], gg1[:, :], start=True, stop=True),
                          ce, *drained)
            cfree[n] = [cg_ok]
            t1 = pe.do(lambda e: [e.transpose(banks[:, 2 + n, c * P:(c + 1) * P], x_sb[:, i, c * P:(c + 1) * P], ident[:, :])
                                  for c in range(KD)][-1], x1_ok[i], *tfree[n])
            t1 = act.do(lambda e: e.copy(xnt[:, n, :, :].rearrange("p c t -> p (c t)"), banks[:, 2 + n, 0:2 * P]), t1, *xfree[n])
            tfree[n] = [t1]
            l_ok = pe.do(lambda e: [e.matmul(banks[:, 4, i * NE:(i + 1) * NE], xnt[:, n, c, :], wgr[:, c, :],
                                             start=(c == 0), stop=(c == KD - 1)) for c in range(KD)][-1], t1, wg_ok)
            xfree[n] = [l_ok]
        r_ok = rsqrt_cols(rms[:, :], ssq[:, :], 1e-6, [sq_ok])
        rows8 = lambda a: a.rearrange("p (n o) -> p n o", o=1).to_broadcast([P, NT, NE])
        t = dve.do(lambda e: e.tensor_tensor(score[:, :, :], banks[:, 4, 0:NT * NE].rearrange("p (n k) -> p n k", k=NE),
                                             rows8(rms[:, :]), ALU.mult), r_ok, l_ok)
        t = dve.do(lambda e: e.tensor_tensor(score[:, :, :], score[:, :, :], banks[:, 5, 0:NT * NE].rearrange("p (n k) -> p n k", k=NE),
                                             ALU.add), t, cg_ok)
        t = dve.do(lambda e: e.tensor_reduce(smx[:, :], score[:, :, :], AX.X, ALU.max), t)
        t = dve.do(lambda e: e.tensor_tensor(score[:, :, :], score[:, :, :], rows8(smx[:, :]), ALU.subtract), t)
        t = act.do(lambda e: e.activation(score[:, :, :], score[:, :, :], ACT.Exp), t)
        t = dve.do(lambda e: e.tensor_reduce(smx[:, :], score[:, :, :], AX.X, ALU.add), t)
        t = dve.do(lambda e: e.reciprocal(smx[:, :], smx[:, :]), t)
        t = dve.do(lambda e: e.tensor_tensor(score[:, :, :], score[:, :, :], rows8(smx[:, :]), ALU.mult), t)
        slot_ok, te_ok = route(score, None, t)
        gate_ok = dve.do(lambda e: e.tensor_copy(gate[:, :, :], top8[:, :, 0:TOPK]), slot_ok)
        scat = scatter(x_sb, slot_ok, x1_ok[-1])

        m1f = m1c[:, :, :].rearrange("p e c -> p (e c)")
        m2f = m2c[:, :, :].rearrange("p e c -> p (e c)")

        def expert_layer1(scat_ok, te_ok, w_ok, bank_free):
            A_X, A_H1, A_H2, A_T1, A_T2, A_Y = 0, 1, 2, 3, 4, 5
            bfree = {b: list(bank_free) for b in range(8)}
            fr = {(n, k): [] for n in ("xg", "xgt", "h1", "h2", "t1", "t2", "bc", "ys") for k in range(3)}
            ok, rd, ends = {}, {}, []

            def inputs(j):
                n = j % 3
                x_ok = sp.dma(ld[f"xg{n}"], lambda e: e.dma_start(xg_b[n][:, :], rows_in[j * P:(j + 1) * P, :]),
                              scat_ok, *fr["xg", n])
                t = pe.do(lambda e: [e.transpose(banks[:, A_X, c * P:(c + 1) * P], xg_b[n][:, c * P:(c + 1) * P], ident[:, :])
                                     for c in range(KD)][-1], x_ok, *bfree[A_X])
                fr["xg", n] = [t]
                t = dve.do(lambda e: e.tensor_copy(xgt_b[j % 2].rearrange("p c t -> p (c t)"), banks[:, A_X, 0:D]),
                           t, *fr["xgt", j % 2])
                bfree[A_X] = [t]
                ok["x", j] = t

            def hidden(j, bank, src, chunks, offset):
                return pe.do(lambda e: [e.matmul(banks[:, bank, :], src(c), weights[:, bass.ds(rd[j] * REG + offset + c * M1, M1)],
                                                 start=(c == 0), stop=(c == chunks - 1)) for c in range(chunks)][-1],
                             ok["x" if offset == 0 else "t1", j], *w_ok, *bfree[bank])

            def turned(j, bank, src, after):
                return pe.do(lambda e: [e.transpose(banks[:, bank, c * P:(c + 1) * P], src[:, c * P:(c + 1) * P], ident[:, :])
                                        for c in range(M1 // P)][-1], after, *bfree[bank])

            inputs(0)
            for j in range(GT + 2):
                if j < GT:
                    n = j % 2
                    rd[j] = expert_of(pe, j, te_ok)
                    t = hidden(j, A_H1, lambda c: xgt_b[n][:, c, :], KD, 0)
                    fr["xgt", n] = [t]
                    h1 = dve.do(lambda e: e.tensor_copy(hs_b[n][:, 0:M1], banks[:, A_H1, :]), t, *fr["h1", n])
                    bfree[A_H1] = [h1]
                    rv = expert_of(dve, j, te_ok)
                    dve.do(lambda e: e.tensor_copy(bcol[:, n, 0:4], m1f[:, bass.ds(rv * 4, 4)]), *fr["bc", n])
                    bc = dve.do(lambda e: e.tensor_copy(bcol[:, n, 4:8], m2f[:, bass.ds(rv * 4, 4)]))
                    if j + 1 < GT:
                        inputs(j + 1)
                if 1 <= j <= GT:
                    q, m = j - 1, (j - 1) % 2
                    t = hidden(q, A_H2, lambda c: ht_b[m][:, c * P:(c + 1) * P], M1 // P, 1024)
                    fr["t1", m] = [t]
                    h2 = act.do(lambda e: e.copy(hs_b[m][:, M1:], banks[:, A_H2, :]), t, *fr["h2", m])
                    bfree[A_H2] = [h2]
                if j < GT:
                    t = turned(j, A_T1, hs_b[n][:, 0:M1], h1)
                    fr["h1", n] = [t]
                    for c in range(4):
                        t1 = act.do(lambda e: e.activation(ht_b[n][:, c * P:(c + 1) * P], banks[:, A_T1, c * P:(c + 1) * P],
                                                           ACT.Relu, bias=bcol[:, n, c:c + 1]), t, bc, *fr["t1", n])
                    bfree[A_T1], ok["t1", j] = [t1], t1
                if 2 <= j:
                    q2, m2 = j - 2, (j - 2) % 2
                    by = A_Y + q2 % 2
                    t = pe.do(lambda e: [e.matmul(banks[:, by, 0:D], ht_b[m2][:, M1 + c * P:M1 + (c + 1) * P],
                                                  weights[:, bass.ds(rd[q2] * REG + 3072 + c * D, D)],
                                                  start=(c == 0), stop=(c == M1 // P - 1)) for c in range(M1 // P)][-1],
                              ok["t2", q2], *bfree[by])
                    fr["t2", m2] = [t]
                    rv = expert_of(dve, q2, te_ok)
                    t = dve.do(lambda e: e.tensor_tensor(ys_b[m2][:, :], banks[:, by, 0:D],
                                                         ybias_f[:, bass.ds(rv * D, D)], ALU.add), t, yb_ld, *fr["ys", m2])
                    bfree[by] = [t]
                    t = sp.dma(ld[f"ys{m2}"], lambda e: e.dma_start(rows_out[q2 * P:(q2 + 1) * P, :], ys_b[m2][:, :]), t)
                    fr["ys", m2] = [t]
                    ends.append(t)
                if 1 <= j <= GT:
                    t = turned(q, A_T2, hs_b[m][:, M1:], h2)
                    fr["h2", m] = [t]
                    for c in range(4):
                        t2 = dve.do(lambda e: e.tensor_scalar(ht_b[m][:, M1 + c * P:M1 + (c + 1) * P], banks[:, A_T2, c * P:(c + 1) * P],
                                                              bcol[:, m, 4 + c:5 + c], 0.0, ALU.add, ALU.max), t, *fr["t2", m])
                    bfree[A_T2], ok["t2", q] = [t2], t2
                    fr["bc", m] = [ok["t1", q], t2]
            return ends[-2:], [t2, ok["t1", GT - 1], bfree[A_Y][0], bfree[A_Y + 1][0], fr["t2", 0][0], fr["t2", 1][0]]

        ends, drained = expert_layer1(scat, te_ok, [w1_ld], [t, slot_ok, gate_ok])
        mix_free = [[], [], [], []]

        def mix1(i, y0, y1, ok0, ok1):
            t = dve.do(lambda e: e.tensor_scalar(att[:, i, :], y0, gate[:, i, 0:1], None, ALU.mult), ok0)
            return dve.do(lambda e: e.scalar_tensor_tensor(att[:, i, :], y1, gate[:, i, 1:2], att[:, i, :], ALU.mult, ALU.add),
                          t, ok1)
        x2_ok = gather_mix(mix1, *ends, *drained)
        if upto == 3:
            w1 = sp.dma(ld["store"], lambda e: e.dma_start(io["dbg0"].rearrange("(n p) d -> p n d", p=P), att[:, :, :]), x2_ok[-1])
            sp.wait(w1)
            return

        NC, G2, SUB = PE_N // P, 2 * P, 16
        arena[0] = 0
        downT = carve(KD, PE_N)
        up_sb = carve(NC, D)
        wkey = carve(KD, 2 * PH * PKEYS)
        xnT = carve(KD, TOK)
        iotax = carve(P * SUB // 2).bitcast(BF16).rearrange("p (a t) -> p a t", t=SUB)
        hid = carve(NC, G2)
        hidf = hid.rearrange("p c t -> p (c t)")
        wqp = hidf[:, 0:4096].rearrange("p (g n) -> p g n", g=2 * PH)
        keyp = hidf[:, 4096:5120].rearrange("p (g n) -> p g n", g=2 * PH)
        attf = att[:, :, :].rearrange("p n d -> p (n d)")
        lo_b, hi_b, hw_b = [], [], []
        for n in range(2):
            o = n * 2048
            lo_b.append(attf[:, o:o + 1024].bitcast(BF16).rearrange("p (a t) -> p a t", t=SUB))
            hi_b.append(attf[:, o + 1024:o + 1280].bitcast(BF16).rearrange("p (a t) -> p a t", t=SUB))
            hw_b.append(attf[:, o + 1280:o + 2048].bitcast(BF16).rearrange("p (m a t) -> p m a t", m=3, t=SUB))
        sims, rest = ht_b[0][:, :], ht_b[1][:, :]
        scr = [hs_b[0][:, :], hs_b[1][:, :]]
        top = scr[0][:, 0:256]
        topi = scr[0][:, 256:512].bitcast(U32)
        w16 = scr[0][:, 512:640]
        j16 = scr[0][:, 640:768].bitcast(U32)
        packs = scr[1][:, 0:384]
        cand = ybias_f[:, 0:432].rearrange("p (h j) -> p h j", h=PH)
        cand2 = ybias_f[:, 432:864].rearrange("p (h j) -> p h j", h=PH)
        lk = ybias_f[:, 864:2048].bitcast(BF16)
        xntf = xnt[:, :, :, :].rearrange("p n c t -> p (n c t)").bitcast(BF16)
        ta, tm, td = (xntf[:, k * P:(k + 1) * P].rearrange("p (m h) -> p m h", h=PH) for k in range(3))
        di = scr[1][:, 384:512].bitcast(BF16).rearrange("p (s m h) -> p s m h", s=2, m=16)
        key_f = scr[1][:, 512:768]
        cmp_b = carve(16 * P // 2).bitcast(BF16).rearrange("p (m n) -> p m n", m=16)
        prod = lk[:, 0:2048].rearrange("p (m n) -> p m n", m=16)
        jh = lk[:, 2048:2176]
        bh = lk[:, 2176:2304]
        i1h = scr[1][:, 768:832].bitcast(BF16)
        i2h = scr[1][:, 832:896].bitcast(BF16)
        q_h = scr[1][:, 896:960].bitcast(BF16)
        turn = [xg_b[0][:, n * P:(n + 1) * P].bitcast(BF16).rearrange("p (a n) -> p a n", a=2) for n in range(2)]
        wpart = [xg_b[1 + n][:, 0:P * 3 // 2].bitcast(BF16).rearrange("p (a n) -> p a n", a=3) for n in range(2)]
        wres = rest[:, 512:768].rearrange("p (a n) -> p a n", a=2)
        sum8 = rest[:, 0:512].bitcast(BF16).rearrange("p (m n) -> p m n", m=8)

        a_free = [*drained, x2_ok[-1]]
        k_ld = sp.dma(ld["w0"], lambda e: e.dma_start(wqp, io["wqp"]), *a_free)
        k_ld = sp.dma(ld["w0"], lambda e: e.dma_start(keyp, io["keysT"]))
        for c in range(4):
            d_ld = sp.dma(ld["w1"], lambda e: e.dma_start(
                downT[:, :, c * 1024:(c + 1) * 1024], io["downT"][:, c * 1024:(c + 1) * 1024].rearrange("(k p) n -> p k n", p=P)))
        u_ld = sp.dma(ld["bias"], lambda e: e.dma_start(up_sb, io["up"].rearrange("(c p) n -> p c n", p=P)))

        blocks = [(0, 1, 16), (1, 1, 8), (2, 2, 5), (4, 4, 3), (8, 8, 1)]
        first = [0] * 17
        for a0, na, nb in blocks:
            for a in range(a0, a0 + na):
                first[a + 1] = first[a] + nb
        NCAND = first[16]
        kc = [dve.do(lambda e: e.memset(t_[:, m, :], v), *a_free) for m in range(16)
              for t_, v in ((ta, float(first[m])), (tm, float(m)), (td, float(first[m] - first[m - 1]) if m else 0.0))]
        io_ok = pool.do(lambda e: e.iota(iotax, [[1, P], [0, SUB]], base=0, channel_multiplier=0,
                                         allow_small_or_imprecise_dtypes=True), *a_free)

        for c in range(KD):
            for half in range(2):
                b = 2 * c + half
                t = pe.do(lambda e: [e.matmul(banks[:, b, g * PKEYS:(g + 1) * PKEYS], wqp[:, half * 8 + g, c * P:(c + 1) * P],
                                              keyp[:, half * 8 + g, :], start=True, stop=True) for g in range(8)][-1], k_ld, *a_free)
                wk_ok = act.do(lambda e: e.copy(wkey[:, c, half * 512:(half + 1) * 512], banks[:, b, :]), t)

        sq = [[], []]
        for i in range(NT):
            n = i % 2
            sq_ok = act.do(lambda e: e.activation(ys_b[n][:, :], att[:, i, :], ACT.Square, accum_out=ssq[:, i:i + 1]),
                           x2_ok[-1], *sq[n])
            sq[n] = [sq_ok]
        r_ok = rsqrt_cols(rms[:, :], ssq[:, :], 1e-5, [sq_ok])
        tf = [[wk_ok], [wk_ok]]
        for i in range(NT):
            n = i % 2
            t = dve.do(lambda e: e.tensor_scalar(att[:, i, :], att[:, i, :], rms[:, i:i + 1], None, ALU.mult), r_ok)
            t = pe.do(lambda e: [e.transpose(banks[:, 4 + n, c * P:(c + 1) * P], att[:, i, c * P:(c + 1) * P], ident[:, :])
                                 for c in range(KD)][-1], t, *tf[n])
            att_free = t
            for c in range(KD):
                xn_ok = act.do(lambda e: e.activation(xnT[:, c, i * P:(i + 1) * P], banks[:, 4 + n, c * P:(c + 1) * P],
                                                      ACT.Copy, scale=normw[:, c:c + 1]), t, s_ld)
            tf[n] = [xn_ok]

        B_SIM, B_HID, B_G, B_OUT, B_TR = 0, 1, 3, 5, 7
        pf = {b: [xn_ok, wk_ok] for b in range(8)}
        sf = {"sims": [wk_ok, t], "packs": [], "turn": [], "hid": [wk_ok], "lo0": [att_free], "lo1": [att_free]}

        def similar(i):
            for half in range(2):
                t = pe.do(lambda e: [e.matmul(banks[:, B_SIM, :], xnT[:, c, i * P:(i + 1) * P], wkey[:, c, half * 512:(half + 1) * 512],
                                              start=(c == 0), stop=(c == KD - 1)) for c in range(KD)][-1], xn_ok, *pf[B_SIM])
                s_ok = act.do(lambda e: e.copy(sims[:, half * 512:(half + 1) * 512], banks[:, B_SIM, :]), t, *sf["sims"])
                pf[B_SIM] = [s_ok]
            return s_ok

        def keep(i, s_ok):
            turn_, wpart_ = turn[i % 2], wpart[i % 2]

            def top16(vals, idxs, src, spare_, *after):
                n = src.shape[1]
                a = [dve.do(lambda e: e.max(vals(g)[:, 0:8], src[:, g, :]), *after) for g in range(n)]
                b = [dve.do(lambda e: e.max_index(idxs(g)[:, 0:8], vals(g)[:, 0:8], src[:, g, :]), a[g]) for g in range(n)]
                b = [dve.do(lambda e: e.match_replace(spare_[:, g, :], vals(g)[:, 0:8], src[:, g, :], -3e38), a[g]) for g in range(n)]
                a = [dve.do(lambda e: e.max(vals(g)[:, 8:16], spare_[:, g, :]), b[g]) for g in range(n)]
                b = [dve.do(lambda e: e.max_index(idxs(g)[:, 8:16], vals(g)[:, 8:16], spare_[:, g, :]), a[g]) for g in range(n)]
                return b[-1]

            s3 = sims.rearrange("p (g k) -> p g k", k=PKEYS)
            t = top16(lambda g: top[:, g * 16:(g + 1) * 16], lambda g: topi[:, g * 16:(g + 1) * 16], s3,
                      rest.rearrange("p (g k) -> p g k", k=PKEYS), s_ok)
            sf["sims"] = [t]
            tp = top.rearrange("p (h s r) -> p h s r", h=PH, s=2)
            for a0, na, nb in blocks:
                sh = [P, PH, na, nb]
                t = dve.do(lambda e: e.tensor_tensor(
                    cand[:, :, first[a0]:first[a0 + na]].rearrange("p h (a b) -> p h a b", a=na),
                    tp[:, :, 0, a0:a0 + na].rearrange("p h (a o) -> p h a o", o=1).to_broadcast(sh),
                    tp[:, :, 1, 0:nb].rearrange("p h (o b) -> p h o b", o=1).to_broadcast(sh), ALU.add), t)
            k1 = dve.do(lambda e: e.tensor_copy(key_f, topi), t)
            kf = key_f.rearrange("p (h s m) -> p s m h", h=PH, s=2)
            for s in range(2):
                k2 = dve.do(lambda e: e.tensor_copy(di[:, s, 0, :], kf[:, s, 0, :]), k1)
                k2 = dve.do(lambda e: e.tensor_tensor(di[:, s, 1:16, :], kf[:, s, 1:16, :], kf[:, s, 0:15, :], ALU.subtract))
            t = top16(lambda h: w16[:, h * 16:(h + 1) * 16], lambda h: j16[:, h * 16:(h + 1) * 16], cand, cand2, t)
            turned_ = lambda a: a.rearrange("p (h r) -> p r h", h=PH)
            t1 = dve.do(lambda e: e.tensor_copy(jh.rearrange("p (r h) -> p r h", h=PH), turned_(j16)), t)
            dve.do(lambda e: e.tensor_scalar(packs[:, 0:P].rearrange("p (r h) -> p r h", h=PH), turned_(w16), 0.0, None, ALU.max),
                   *sf["packs"])

            def pick(mask_src, edge, steps, dst, *after):
                by_rank = lambda a: a.rearrange("p m (r h) -> p m r h", h=PH)
                every_rank = lambda a: a.rearrange("p m (o h) -> p m o h", o=1).to_broadcast([P, 16, 16, PH])
                t = after[0]
                if edge is not None:
                    t = dve.do(lambda e: e.tensor_tensor(
                        by_rank(cmp_b), mask_src.rearrange("p (o r h) -> p o r h", o=1, h=PH).to_broadcast([P, 16, 16, PH]),
                        every_rank(edge), ALU.is_ge), *after)
                t = dve.do(lambda e: e.tensor_tensor(by_rank(prod), by_rank(cmp_b), every_rank(steps), ALU.mult), t)
                src, dst_ = prod, sum8
                for w in (8, 4, 2):
                    t = dve.do(lambda e: e.tensor_tensor(dst_[:, 0:w, :], src[:, 0:2 * w:2, :], src[:, 1:2 * w:2, :], ALU.add), t)
                    src, dst_ = dst_, src
                return dve.do(lambda e: e.tensor_tensor(dst, src[:, 0, :], src[:, 1, :], ALU.add), t)

            t2 = pick(jh, ta[:, :, :], di[:, 0, :, :], i1h, t1, kc[-1], k2)
            t2 = pick(jh, None, td[:, :, :], bh, t2)
            t2 = dve.do(lambda e: e.tensor_tensor(bh, jh, bh, ALU.subtract), t2)
            t2 = pick(bh, tm[:, :, :], di[:, 1, :, :], i2h, t2)
            t2 = dve.do(lambda e: e.tensor_scalar(q_h, i1h, float(PKEYS // 2), None, ALU.is_ge), t2)
            t3 = dve.do(lambda e: e.scalar_tensor_tensor(packs[:, P:2 * P], q_h, -float(PKEYS // 2), i1h, ALU.mult, ALU.add), t2)
            t3 = dve.do(lambda e: e.scalar_tensor_tensor(packs[:, 2 * P:3 * P], q_h, float(PKEYS), i2h, ALU.mult, ALU.add), t2)
            t = pe.do(lambda e: [e.transpose(banks[:, B_TR, m * P:(m + 1) * P], packs[:, m * P:(m + 1) * P], ident[:, :])
                                 for m in range(3)][-1], t3, *pf[B_TR])
            sf["packs"] = [t]
            t1 = act.do(lambda e: e.copy(wpart_[:, 0, :], banks[:, B_TR, 0:P]), t, *sf["turn"])
            t2 = act.do(lambda e: e.copy(turn_.rearrange("p a n -> p (a n)"), banks[:, B_TR, P:3 * P]))
            t = dve.do(lambda e: e.tensor_tensor(wres[:, 0, :], banks[:, B_TR, 0:P], wpart_[:, 0, :], ALU.subtract), t1, t2)
            pf[B_TR] = [t]
            t = dve.do(lambda e: e.tensor_copy(wpart_[:, 1, :], wres[:, 0, :]), t)
            t = dve.do(lambda e: e.tensor_tensor(wres[:, 1, :], wres[:, 0, :], wpart_[:, 1, :], ALU.subtract), t)
            return dve.do(lambda e: e.tensor_copy(wpart_[:, 2, :], wres[:, 1, :]), t)

        def burst(g, qs, weighed_ok):
            for q in qs:
                if g > 0:
                    o_ok = pe.do(lambda e: [e.matmul(banks[:, B_OUT + n, 0:D], hid[:, c, n * P:(n + 1) * P], up_sb[:, c, :],
                                                     start=(c == 0), stop=(c == NC - 1)) for n in range(2) for c in (2 * q, 2 * q + 1)][-1],
                                 *weighed_ok, u_ld, *pf[B_OUT], *pf[B_OUT + 1])
                    sf["out"] = [o_ok]
                if g * G2 < TOK:
                    b = B_HID + q % 2
                    t = pe.do(lambda e: [e.matmul(banks[:, b, h * G2:(h + 1) * G2], downT[:, c, (2 * q + h) * P:(2 * q + h + 1) * P],
                                                  xnT[:, c, g * G2:(g + 1) * G2], start=(c == 0), stop=(c == KD - 1))
                                         for h in range(2) for c in range(KD)][-1], d_ld, *pf[b])
                    h_ok = act.do(lambda e: e.activation(hid[:, 2 * q:2 * q + 2, :].rearrange("p c t -> p (c t)"), banks[:, b, :],
                                                         ACT.Gelu), t, *sf["hid"])
                    pf[b] = sf["h_ok"] = [h_ok]

        def spread(i, s, kept_ok):
            n = s % 2
            cols = slice(s * SUB, (s + 1) * SUB)
            one = lambda a, k: a.rearrange("p (o t) -> p o t", o=1).to_broadcast([P, k, SUB])
            t = dve.do(lambda e: e.tensor_tensor(lo_b[n], iotax, one(turn[i % 2][:, 1, cols], P), ALU.is_equal), kept_ok, io_ok, *sf[f"lo{n}"])
            t = dve.do(lambda e: e.tensor_tensor(hi_b[n], iotax[:, 0:NC, :], one(turn[i % 2][:, 0, cols], NC), ALU.is_equal))
            t1 = dve.do(lambda e: e.tensor_tensor(
                hw_b[n], hi_b[n].rearrange("p (o a) t -> p o a t", o=1).to_broadcast([P, 3, NC, SUB]),
                wpart[i % 2][:, :, cols].rearrange("p m (o t) -> p m o t", o=1).to_broadcast([P, 3, NC, SUB]), ALU.mult), t)
            b = B_G + n
            t = pe.do(lambda e: [e.matmul(banks[:, b, k * NC:(k + 1) * NC], lo_b[n][:, :, k], hw_b[n][:, m, :, k],
                                          start=(m == 0), stop=(m == 2)) for k in range(SUB) for m in range(3)][-1], t1, *pf[b])
            sf[f"lo{n}"] = [t]
            return t

        def weigh(i, s, g_ok, h_ok):
            b = B_G + s % 2
            t0 = (i % 2) * P + s * SUB
            t = dve.do(lambda e: e.tensor_tensor(hid[:, :, t0:t0 + SUB], hid[:, :, t0:t0 + SUB],
                                                 banks[:, b, :].rearrange("p (t c) -> p c t", c=NC), ALU.mult), g_ok, h_ok)
            pf[b] = [t]
            return t

        kept, w_ok = [], []
        for g in range(TOK // G2 + 1):
            last = g * G2 == TOK
            for n in range(2):
                i = 2 * g + n
                if not last:
                    s_ok = similar(i)
                burst(g, range(n * NC // 4, (n + 1) * NC // 4), w_ok)
                if not last:
                    kept.append(keep(i, s_ok))
            if g > 0:
                for n in range(2):
                    i = 2 * g - 2 + n
                    t = dve.do(lambda e: e.tensor_tensor(x_sb[:, i, :], x_sb[:, i, :], banks[:, B_OUT + n, 0:D], ALU.add), *sf["out"])
                    pf[B_OUT + n] = [t]
                    y_st = sp.dma(ld["store"], lambda e: e.dma_start(out[i * P:(i + 1) * P, :], x_sb[:, i, :]), t)
            if last:
                break
            prev = None
            for n in range(2):
                for s in range(P // SUB):
                    g_ok = spread(2 * g + n, s, kept[-2 + n])
                    if prev:
                        w_ok = [weigh(*prev, sf["h_ok"][0])]
                    prev = (2 * g + n, s, g_ok)
            w_ok = [weigh(*prev, sf["h_ok"][0])]
            sf["turn"] = w_ok
        sp.wait(y_st)


def layout(i):
    A = {k: np.asarray(v) for k, v in i.items()}
    x = A["x"].reshape(TOK, D)

    def cols(b):
        return b.reshape(NE, -1, P).transpose(2, 0, 1)
    order = np.arange(PE_N).reshape(2, PKEYS // 2, PKEYS).transpose(1, 0, 2).reshape(-1)
    wv = A["L0_cond_Wv"].T.reshape(D, HEADS // 2, 2, DH)
    d = dict(
        x=x, xT=x.T, mask=A["mask_SxS_bk1"].view(np.uint32), condT=A["cond_256"].T,
        wqT=A["L0_cond_Wq"].T, wkT=A["L0_cond_Wk"].T, woT=A["L0_cond_Wo"].T,
        wvT=wv.transpose(0, 2, 1, 3).reshape(D, D),
        rms_scale=A["L0_cond_rms_scale"].reshape(1, D), wcT=A["L0_cond_Wc"].T, bc=A["L0_cond_bc"].reshape(1, 2 * D),
        routerT=A["L0_ffn_router_w"].T, w1T=A["L0_ffn_w1"].transpose(0, 2, 1), b1=cols(A["L0_ffn_b1"]),
        w2T=A["L0_ffn_w2"].transpose(0, 2, 1), b2=A["L0_ffn_b2"],
        rms_w=A["L1_cond_rms_w"].reshape(KD, P).T, wg_W=A["L1_cond_wg_W"], wg_b=A["L1_cond_wg_b"].reshape(1, NE),
        gg_W=A["L1_cond_gg_W"], gg_b=A["L1_cond_gg_b"].reshape(1, NE),
        W1=A["L1_cond_W1"], m1=cols(A["L1_cond_b1"]), W2=A["L1_cond_W2"], m2=cols(A["L1_cond_b2"]),
        W3=A["L1_cond_W3"], m3=A["L1_cond_b3"], norm_w=A["L1_ffn_norm_w"].reshape(KD, P).T,
        wqp=A["L1_ffn_wq"].reshape(D, 2 * PH, PDK).transpose(2, 1, 0),
        keysT=A["L1_ffn_keys"].transpose(3, 0, 2, 1).reshape(PDK, 2 * PH, PKEYS),
        downT=A["L1_ffn_expert_down"][order].T, up=A["L1_ffn_expert_up"][order],
    )
    return {k: np.ascontiguousarray(v) for k, v in d.items()}


def kernel(**inputs):
    from concourse import bacc
    from concourse.bass_utils import run_bass_kernel_spmd

    arrays = layout(inputs)
    nc = bacc.Bacc("TRN2", target_bir_lowering=False, num_devices=1)
    io = {n: nc.dram_tensor(f"in_{n}", a.shape, mybir.dt.from_np(a.dtype), kind="ExternalInput").ap()
          for n, a in arrays.items()}
    out = nc.dram_tensor("out_0", [TOK, D], F32, kind="ExternalOutput").ap()
    build(nc, io, out)
    r = run_bass_kernel_spmd(nc, [{f"in_{n}": a for n, a in arrays.items()}], core_ids=[0])
    return r.results[0]["out_0"].reshape(BATCH, SEQ, D)
```

```python
from contextlib import ExitStack

import numpy as np

import concourse.bass as bass
from concourse import mybir

F32 = mybir.dt.float32
BF16 = mybir.dt.bfloat16
U32 = mybir.dt.uint32
I32 = mybir.dt.int32
U8 = mybir.dt.uint8
ALU = mybir.AluOpType
ACT = mybir.ActivationFunctionType
AX = mybir.AxisListType

P = 128
BATCH, SEQ, D = 32, 64, 256
TOK = BATCH * SEQ
NT = TOK // P
KD = D // P
HEADS, DH = 16, 16
COND = 64
NE, TOPK = 8, 2
F0 = 1024
M1 = 512
GT = TOPK * NT + NE - 1
PH, PK, PKEYS, PDK = 8, 16, 64, 128
PE_N = PKEYS * PKEYS
BIG = 1e30


class Lane:

    def __init__(self, eng, sem):
        self.eng, self.sem, self.count, self.passed = eng, sem, 0, {}

    def wait(self, *after):
        for sem, value in after:
            if self.passed.get(id(sem), 0) < value:
                self.passed[id(sem)] = value
                self.eng.wait_ge(sem, value)

    def do(self, emit, *after):
        self.wait(*after)
        self.count += 1
        emit(self.eng).then_inc(self.sem, 1)
        return self.sem, self.count

    def dma(self, slot, emit, *after):
        self.wait(*after)
        slot.count += 16
        emit(self.eng).then_inc(slot.sem, 16)
        return slot.sem, slot.count


class Slot:

    def __init__(self, sem):
        self.sem, self.count = sem, 0


def build(nc, io, out, upto=99, dbg=None):
    root = ExitStack()
    with root:
        scopes = [root]

        def sb(name, shape, dt=F32):
            return scopes[-1].enter_context(nc.sbuf_tensor(name, shape, dt))

        def slot(name):
            return Slot(root.enter_context(nc.semaphore(name)))

        pe, dve, act, pool, sp = (Lane(eng, root.enter_context(nc.semaphore("done_" + n))) for n, eng in (
            ("pe", nc.tensor), ("dve", nc.vector), ("act", nc.scalar), ("pool", nc.gpsimd), ("sp", nc.sync)))
        banks = root.enter_context(nc.psum_tensor("banks", [P, 8, 512], F32))

        ident = sb("ident", [P, P])
        lower = sb("lower", [P, P])
        ones = sb("ones", [P, P])
        x_sb = sb("x_sb", [P, NT, D])
        att = sb("att", [P, NT, D])
        REG = 4096
        NREG = NE
        iota16 = sb("iota16", [P, NE, 16])
        iota8 = sb("iota8", [P, NT, NE])
        iotag = sb("iotag", [P, GT, NE])
        b1c = sb("b1c", [P, NE, F0 // P])
        m1c = sb("m1c", [P, NE, M1 // P])
        m2c = sb("m2c", [P, NE, M1 // P])
        ybias = sb("ybias", [P, NE, D])
        cond1 = sb("cond1", [COND + 2, BATCH])
        gg1 = sb("gg1", [COND + 2, NE])
        rw = sb("rw", [P, KD, NE])
        wgw = sb("wgw", [P, KD, NE])
        rmsw = sb("rmsw", [P, KD])
        normw = sb("normw", [P, KD])
        gate = sb("gate", [P, NT, TOPK])
        slots = sb("slots", [P, TOPK, NT], U32)
        tile_e = sb("tile_e", [P, GT], I32)
        small = sb("small", [P, 64])

        rows_in = nc.dram_tensor("rows_in", [GT * P, D], F32, kind="Internal").ap()
        rows_out = nc.dram_tensor("rows_out", [GT * P, D], F32, kind="Internal").ap()

        ld = {n: slot("ld_" + n) for n in
              ("x", "bias", "small", "wqkvo", "wq", "w0", "w1", "xt0", "xt1", "zero", "scat",
               "store", "mask", "down", "up", "xg0", "xg1", "xg2", "ys0", "ys1", *(f"mix{n}" for n in range(8)))}

        c1 = pool.do(lambda e: e.memset(ident[:, :], 0.0))
        c1 = pool.do(lambda e: e.affine_select(out=ident[:, :], in_=ident[:, :], compare_op=ALU.not_equal,
                                               fill=1.0, base=0, pattern=[[-1, P]], channel_multiplier=1), c1)
        c2 = pool.do(lambda e: e.memset(ones[:, :], 1.0))
        c3 = pool.do(lambda e: e.affine_select(out=lower[:, :], in_=ones[:, :], compare_op=ALU.is_gt,
                                               fill=0.0, base=0, pattern=[[1, P]], channel_multiplier=-1), c2)
        c4 = pool.do(lambda e: e.iota(iota16[:, :, :], [[0, NE], [P, 16]], base=0, channel_multiplier=0,
                                      allow_small_or_imprecise_dtypes=True))
        c4 = pool.do(lambda e: e.iota(iota8[:, :, :], [[0, NT], [1, NE]], base=0, channel_multiplier=0,
                                      allow_small_or_imprecise_dtypes=True))
        c_all = pool.do(lambda e: e.iota(iotag[:, :, :], [[1, GT], [0, NE]], base=0, channel_multiplier=0,
                                         allow_small_or_imprecise_dtypes=True))

        hs_b = [sb(f"hs{n}", [P, 1024]) for n in range(2)]
        weights = sb("weights", [P, NREG * REG])

        NA = 4
        arena = [(NREG - NA) * REG]

        def carve(*shape):
            n = int(np.prod(shape))
            piece = weights[:, arena[0]:arena[0] + n]
            arena[0] += n
            if len(shape) == 1:
                return piece
            names = " ".join(f"d{j}" for j in range(len(shape)))
            return piece.rearrange(f"p ({names}) -> p {names}", **{f"d{j}": shape[j] for j in range(len(shape))})

        wq, wk, wv, wo = (carve(KD, D) for _ in range(4))
        xt = [carve(KD, 512) for _ in range(2)]
        qt = [carve(KD, 512) for _ in range(2)]
        kts = [carve(KD, 512) for _ in range(2)]
        kbd = [carve(KD, 8, SEQ) for _ in range(2)]
        scm = carve(HEADS, SEQ)
        prb = carve(HEADS, SEQ)
        pts = carve(8, P)
        vbd = [[carve(8, 2 * DH) for _ in range(2)] for _ in range(2)]
        ots = carve(KD, P)
        sqj = carve(D)
        hmask = sb("hmask", [P, 8, 1])
        mask4 = sb("mask4", [P, SEQ // 4], U32)
        mask8 = mask4[:, :].bitcast(U8)
        mneg = sb("mneg", [P, 1, SEQ])
        valid = sb("valid", [P, 4])
        mx = sb("mx", [P, HEADS])
        nmx = sb("nmx", [P, HEADS])
        rsum = sb("rsum", [P, HEADS])
        rinv = sb("rinv", [P, HEADS])
        ssq = sb("ssq", [P, NT])
        rms = sb("rms", [P, NT])

        wq_ld = sp.dma(ld["wq"], lambda e: e.dma_start(wq[:, :, :], io["wqT"].rearrange("(c p) n -> p c n", p=P)))
        xt_ld = [sp.dma(ld[f"xt{n}"], lambda e, n=n: e.dma_start(
            xt[n][:, :, :], io["xT"][:, n * 512:(n + 1) * 512].rearrange("(c p) t -> p c t", p=P))) for n in range(2)]
        for t, n in ((wk, "wkT"), (wv, "wvT"), (wo, "woT")):
            w_ld = sp.dma(ld["wqkvo"], lambda e, t=t, n=n: e.dma_start(
                t[:, :, :], io[n].rearrange("(c p) n -> p c n", p=P)))
        sp.dma(ld["mask"], lambda e: e.dma_start(mask4[0:SEQ, :], io["mask"]))
        m_ld = sp.dma(ld["mask"], lambda e: e.dma_start(mask4[SEQ:P, :], io["mask"]))
        x_ld = sp.dma(ld["x"], lambda e: e.dma_start(x_sb[:, :, :], io["x"].rearrange("(n p) d -> p n d", p=P)))

        def small_load(dst, src):
            return sp.dma(ld["small"], lambda e: e.dma_start(dst, src))
        small_load(rw[:, :, :], io["routerT"].rearrange("(c p) n -> p c n", p=P))
        small_load(wgw[:, :, :], io["wg_W"].rearrange("(c p) n -> p c n", p=P))
        small_load(rmsw[:, :], io["rms_w"])
        small_load(normw[:, :], io["norm_w"])
        small_load(b1c[:, :, :], io["b1"])
        small_load(m1c[:, :, :], io["m1"])
        small_load(m2c[:, :, :], io["m2"])
        small_load(cond1[0:COND, :], io["condT"])
        small_load(gg1[0:COND, :], io["gg_W"])
        small_load(gg1[COND:COND + 1, :], io["gg_b"])
        small_load(gg1[COND + 1:COND + 2, :], io["wg_b"])
        small_load(ybias[:, :, :], io["b2"].rearrange("(a e) d -> a e d", a=1).to_broadcast([P, NE, D]))
        modw = carve(2 * D)[0:COND + 1, :]
        rsbc = carve(D)
        small_load(modw[0:COND, :], io["wcT"])
        small_load(modw[COND:COND + 1, :], io["bc"])
        s_ld = small_load(rsbc[:, :], io["rms_scale"].to_broadcast([P, D]))

        def region(r):
            return weights[:, r * REG:(r + 1) * REG]

        def load_l0(e_, *after):
            w = region(e_)
            sp.dma(ld["w0"], lambda e: e.dma_start(w[:, 0:2048].rearrange("p (c f) -> p c f", c=KD),
                                                   io["w1T"][e_].rearrange("(c p) f -> p c f", p=P)), *after)
            return sp.dma(ld["w0"], lambda e: e.dma_start(w[:, 2048:4096].rearrange("p (c f) -> p c f", c=F0 // P),
                                                          io["w2T"][e_].rearrange("(c p) f -> p c f", p=P)))

        for e_ in range(NREG - NA):
            load_l0(e_)
        zt = hs_b[1][:, 0:2 * D]
        z = pool.do(lambda e: e.memset(zt, 0.0))
        for j in range(0, GT - 1, 2):
            sp.dma(ld["zero"], lambda e: e.dma_start(rows_in[j * P:(j + 2) * P, :].rearrange("(a p) d -> p a d", p=P),
                                                     zt.rearrange("p (a d) -> p a d", a=2)), z)
        zero_ok = sp.dma(ld["zero"], lambda e: e.dma_start(rows_in[(GT - 1) * P:GT * P, :], zt[:, 0:D]))

        h1 = pool.do(lambda e: e.memset(hmask[:, :, :], 1.0))
        h1 = pool.do(lambda e: e.affine_select(out=hmask[:, :, 0], in_=hmask[:, :, 0], compare_op=ALU.is_ge, fill=0.0,
                                               base=0, pattern=[[-DH, 8]], channel_multiplier=1), h1)
        hm_ok = pool.do(lambda e: e.affine_select(out=hmask[:, :, 0], in_=hmask[:, :, 0], compare_op=ALU.is_ge, fill=0.0,
                                                  base=DH - 1, pattern=[[DH, 8]], channel_multiplier=-1), h1)
        v0 = [pool.do(lambda e: e.memset(v, 0.0)) for vs in vbd for v in vs][-1]
        mk = dve.do(lambda e: e.tensor_scalar(mneg[:, 0, :], mask8, -BIG, None, ALU.mult), m_ld)
        mk1 = dve.do(lambda e: e.tensor_scalar(scm[:, 0, :], mask8, -1.0, 1.0, ALU.mult, ALU.add))
        mk2 = dve.do(lambda e: e.tensor_reduce(valid[:, 0:1], scm[:, 0, :], AX.X, ALU.max), mk1)
        mk3 = dve.do(lambda e: e.reciprocal(valid[:, 1:2], valid[:, 0:1]), mk2)
        mk4 = dve.do(lambda e: e.tensor_tensor(valid[:, 2:3], valid[:, 0:1], valid[:, 1:2], ALU.mult), mk3)

        B_S, B_T, B_P, B_O, B_W = 0, 2, 4, 5, 6
        free = {n: [] for n in ("s", "t", "p4", "p7", "o", "w", "qk0", "qk1", "kbd", "vbd0", "vbd1",
                                "scm", "prb", "pts", "ots", "xt0", "xt1", "rsum")}
        free["vbd0"] = free["vbd1"] = [v0]
        free["scm"] = [mk2]
        pb = [4, 7]
        nproj = 0

        def turns():
            nonlocal nproj
            nproj += 1
            return pb[nproj % 2]

        def project(w, src, c, after):
            b = turns()

            def emit(e):
                for k in range(KD):
                    m = e.matmul(banks[:, b, :], w[:, k, c * P:(c + 1) * P], src[:, k, :], start=(k == 0), stop=(k == KD - 1))
                return m
            return b, pe.do(emit, *after, *free[f"p{b}"])

        att_ok = {}
        v_ok, kb_ok, s_ok, e_ok, q_ok = {}, {}, {}, {}, {}
        NG = TOK // 512
        stage_qk = [(w, dst, c) for w, dst in ((wq, qt), (wk, kts)) for c in range(KD)]

        def queries_keys(g, part):
            w, dst, c = stage_qk[part]
            if part == 0 and g >= 2:
                xt_ld.append(sp.dma(ld[f"xt{g % 2}"], lambda e: e.dma_start(
                    xt[g % 2][:, :, :], io["xT"][:, g * 512:(g + 1) * 512].rearrange("(c p) t -> p c t", p=P)),
                    *free[f"xt{g % 2}"]))
            b, t = project(w, xt[g % 2], c, [wq_ld if w is wq else w_ld, xt_ld[g]])
            t = act.do(lambda e: e.copy(dst[g % 2][:, c, :], banks[:, b, :]), t, *free[f"qk{g % 2}"])
            free[f"p{b}"] = q_ok[g] = [t]

        def keys_values(i):
            g, tl = i // 4, (i % 4) * P
            xg, vs = xt[g % 2], vbd[i % 2]
            for bb in range(2):
                t0 = tl + bb * SEQ
                vb = turns()
                t = pe.do(lambda e: [e.matmul(banks[par * SEQ:(par + 1) * SEQ, vb, 0:P], xg[:, k, t0:t0 + SEQ],
                                              wv[:, k, par * P:(par + 1) * P], start=(k == 0), stop=(k == KD - 1))
                                     for par in range(2) for k in range(KD)][-1], w_ld, *free[f"p{vb}"])
                free[f"xt{g % 2}"] = [t]
                for par in range(2):
                    t2 = dve.do(lambda e: e.tensor_copy(
                        vs[bb][par * SEQ:(par + 1) * SEQ, :, par * DH:(par + 1) * DH],
                        banks[par * SEQ:(par + 1) * SEQ, vb, 0:P].rearrange("p (h d) -> p h d", h=8)),
                        t, *free[f"vbd{i % 2}"])
                free[f"p{vb}"] = [t2]
                for c in range(KD):
                    t3 = dve.do(lambda e: e.tensor_tensor(
                        kbd[bb][:, c, :, :], kts[g % 2][:, c:c + 1, t0:t0 + SEQ].to_broadcast([P, 8, SEQ]),
                        hmask[:, :, :].to_broadcast([P, 8, SEQ]), ALU.mult), *q_ok[g], hm_ok, *free["kbd"])
            v_ok[i], kb_ok[i] = t2, t3

        def scores(i):
            g, tl = i // 4, (i % 4) * P
            s_ok[i] = pe.do(lambda e: [e.matmul(banks[bb * SEQ:(bb + 1) * SEQ, B_S + c, :],
                                                qt[g % 2][:, c, tl + bb * SEQ:tl + (bb + 1) * SEQ],
                                                kbd[bb][:, c, :, :].rearrange("p h t -> p (h t)"), start=True, stop=True)
                                       for bb in range(2) for c in range(KD)][-1], kb_ok[i], *q_ok[g], *free["s"])
            free["kbd"] = [s_ok[i]]
            if i % 4 == 3:
                free[f"qk{g % 2}"] = [s_ok[i]]

        def exponentials(i):
            sc = banks[:, B_S:B_S + 2, :].rearrange("p a (h t) -> p (a h) t", h=8)
            t = dve.do(lambda e: e.tensor_tensor(scm, sc, mneg[:, :, :].to_broadcast([P, HEADS, SEQ]), ALU.add),
                       s_ok[i], mk, *free["scm"])
            free["s"] = [t]
            t = dve.do(lambda e: e.tensor_reduce(mx[:, :], scm, AX.X, ALU.max), t)
            t = dve.do(lambda e: e.tensor_scalar(nmx[:, :], mx[:, :], -(DH ** -0.5), None, ALU.mult), t, *free["scm"])
            for h in range(HEADS):
                t4 = act.do(lambda e: e.activation(prb[:, h, :], scm[:, h, :], ACT.Exp, bias=nmx[:, h:h + 1],
                                                   scale=DH ** -0.5, accum_out=rsum[:, h:h + 1]),
                            t, *free["prb"], *free["rsum"])
            free["scm"] = [t4]
            e_ok[i] = t4

        def normalise(i):
            t = dve.do(lambda e: e.reciprocal(rinv[:, :], rsum[:, :]), e_ok[i])
            free["rsum"] = [t]
            t = dve.do(lambda e: e.tensor_scalar(rinv[:, :], rinv[:, :], valid[:, 2:3], None, ALU.mult), t, mk4)
            t = dve.do(lambda e: e.tensor_tensor(
                prb, prb, rinv[:, :].rearrange("p (h o) -> p h o", o=1).to_broadcast([P, HEADS, SEQ]), ALU.mult), t)
            t = pe.do(lambda e: [e.transpose(banks[:, B_T + hp // 4, (hp % 4) * P:(hp % 4 + 1) * P],
                                             prb[:, 2 * hp:2 * hp + 2, :].rearrange("p h t -> p (h t)"), ident[:, :])
                                 for hp in range(8)][-1], t, c_all, *free["t"])
            free["prb"] = [t]
            t1 = act.do(lambda e: e.copy(pts[:, 0:4, :].rearrange("p h t -> p (h t)"), banks[:, B_T, :]), t, *free["pts"])
            t2 = act.do(lambda e: e.copy(pts[:, 4:8, :].rearrange("p h t -> p (h t)"), banks[:, B_T + 1, :]))
            free["t"] = [t2]
            return t2

        def weigh_values(i, p_ok):
            t = pe.do(lambda e: [e.matmul(banks[32 * (hp % 4):32 * (hp % 4) + 32, B_O, (hp // 4) * P + bb * SEQ:(hp // 4) * P + (bb + 1) * SEQ],
                                          vbd[i % 2][bb][:, hp, :], pts[:, hp, bb * SEQ:(bb + 1) * SEQ], start=True, stop=True,
                                          tile_position=(0, 32 * (hp % 4)))
                                 for bb in range(2) for hp in range(8)][-1], p_ok, v_ok[i], *free["o"])
            free["pts"] = free[f"vbd{i % 2}"] = [t]
            t = dve.do(lambda e: e.tensor_copy(ots.rearrange("p c t -> p (c t)"), banks[:, B_O, 0:2 * P]), t, *free["ots"])
            free["o"] = [t]
            return t

        def output(i, o_ok):
            t = pe.do(lambda e: [e.matmul(banks[:, B_W, 0:D], ots[:, c, :], wo[:, c, :], start=(c == 0), stop=(c == KD - 1))
                                 for c in range(KD)][-1], o_ok, *free["w"])
            free["ots"] = [t]
            a_ok = dve.do(lambda e: e.tensor_copy(att[:, i, :], banks[:, B_W, 0:D]), t)
            free["w"] = [a_ok]
            att_ok[i] = a_ok

        for part in range(4):
            queries_keys(0, part)
        keys_values(0)
        scores(0)
        exponentials(0)
        keys_values(1)
        scores(1)
        for part in range(3):
            queries_keys(1, part)
        for i in range(NT):
            p_ok = normalise(i)
            if i + 1 < NT:
                exponentials(i + 1)
            o_ok = weigh_values(i, p_ok)
            if i + 2 < NT:
                keys_values(i + 2)
            output(i, o_ok)
            if i + 2 < NT:
                scores(i + 2)
            if (i + 3) // 4 + 1 < NG:
                queries_keys((i + 3) // 4 + 1, (i + 3) % 4)
            sq_ok = act.do(lambda e: e.activation(sqj, att[:, i, :], ACT.Square, accum_out=ssq[:, i:i + 1]), att_ok[i])

        def rsqrt_cols(dst, src, eps, after):
            t = dve.do(lambda e: e.tensor_scalar(dst, src, 1.0 / D, eps, ALU.mult, ALU.add), *after)
            t = act.do(lambda e: e.activation(dst, dst, ACT.Sqrt), t)
            return dve.do(lambda e: e.reciprocal(dst, dst), t)
        r_ok = rsqrt_cols(rms[:, :], ssq[:, :], 1e-6, [sq_ok])
        silu1 = sb("silu1", [COND + 1, BATCH])
        condx = sb("condx", [COND + 2, 2, P])
        t = dve.do(lambda e: e.memset(silu1[COND:COND + 1, :], 1.0))
        one_ok = dve.do(lambda e: e.memset(cond1[COND:COND + 2, :], 1.0))
        si_ok = act.do(lambda e: e.activation(silu1[0:COND, :], cond1[0:COND, :], ACT.Silu), s_ld)

        tokens4 = sb("tokens4", [P, 4 * D])
        gmod = tokens4[:, 0:2 * D].rearrange("p (n d) -> p n d", n=2)
        xnt = tokens4[:, 2 * D:].rearrange("p (n c t) -> p n c t", n=2, c=KD)
        logit = sb("logit", [P, NT, NE])
        cfree = [[], []]
        mfree, tfree, xfree = [free["s"], free["s"]], [free["t"], free["t"]], [[], []]
        xn_ok, mod_ok = [], {}

        def modulation(i):
            n = i % 2
            ce = act.do(lambda e: e.copy(
                condx[0:COND + 1, n, :].rearrange("p (b s) -> p b s", b=2),
                silu1[:, 2 * i:2 * i + 2].rearrange("p (b s) -> p b s", s=1).to_broadcast([COND + 1, 2, SEQ])),
                si_ok, one_ok, *cfree[n])
            mod_ok[i] = pe.do(lambda e: e.matmul(banks[:, n, :], condx[0:COND + 1, n, :], modw[:, :], start=True, stop=True),
                              ce, s_ld, *mfree[n])
            cfree[n] = [mod_ok[i]]

        def logits(i, after):
            t = pe.do(lambda e: [e.matmul(banks[:, 4, i * NE:(i + 1) * NE], xnt[:, i % 2, c, :], rw[:, c, :],
                                          start=(c == 0), stop=(c == KD - 1)) for c in range(KD)][-1], after, *free["p4"])
            xfree[i % 2] = [t]
            return t

        modulation(0)
        for i in range(NT):
            n = i % 2
            if i + 1 < NT:
                modulation(i + 1)
            t1 = dve.do(lambda e: e.scalar_tensor_tensor(gmod[:, n, :], banks[:, n, D:2 * D], 1.0, rsbc[:, :], ALU.add, ALU.mult),
                        mod_ok[i])
            t1 = dve.do(lambda e: e.scalar_tensor_tensor(att[:, i, :], att[:, i, :], rms[:, i:i + 1], gmod[:, n, :],
                                                         ALU.mult, ALU.mult), t1, r_ok)
            t1 = dve.do(lambda e: e.tensor_tensor(att[:, i, :], att[:, i, :], banks[:, n, 0:D], ALU.add), t1)
            mfree[n] = [t1]
            xn_ok.append(t1)
            t1 = pe.do(lambda e: [e.transpose(banks[:, 2 + n, c * P:(c + 1) * P], att[:, i, c * P:(c + 1) * P], ident[:, :])
                                  for c in range(KD)][-1], t1, *tfree[n])
            t1 = act.do(lambda e: e.copy(xnt[:, n, :, :].rearrange("p c t -> p (c t)"), banks[:, 2 + n, 0:2 * P]), t1, *xfree[n])
            tfree[n] = [t1]
            if i > 0:
                l_ok = logits(i - 1, xt_ok)
            xt_ok = t1
        l_ok = logits(NT - 1, xt_ok)
        t = dve.do(lambda e: e.tensor_copy(logit[:, :, :].rearrange("p a b -> p (a b)"), banks[:, 4, 0:NT * NE]), l_ok)
        a_end = [sq_ok, xn_ok[-1], l_ok]
        for e_ in range(NREG - NA, NE):
            w0_ld = load_l0(e_, *a_end)

        if upto == 1:
            dbg.update(att=att, logit=logit)
            w1 = sp.dma(ld["store"], lambda e: e.dma_start(io["dbg0"].rearrange("(n p) d -> p n d", p=P), att[:, :, :]), t, xn_ok[-1])
            w1 = sp.dma(ld["store"], lambda e: e.dma_start(io["dbg1"].rearrange("(n p) d -> p n d", p=P), logit[:, :, :]), t)
            sp.wait(w1)
            return

        onehot = sb("onehot", [P, TOPK, NT, NE])
        both = sb("both", [P, NT, NE])
        before = sb("before", [P, NT, NE])
        top8 = sb("top8", [P, NT, 8])
        idx8 = sb("idx8", [P, NT, 8], U32)
        count = sb("count", [P, NE])
        ntile = sb("ntile", [P, NE])
        upto_e = sb("upto_e", [P, NE])
        base_e = sb("base_e", [P, NE])
        thr = sb("thr", [P, NE, 16])
        place = sb("place", [P, NT, NE])
        hit = sb("hit", [P, NT, NE])
        slot_f = sb("slot_f", [P, TOPK, NT])
        te = sb("te", [P, GT, NE])
        te_f = sb("te_f", [P, GT])
        zcol = sb("zcol", [P, NT])

        def route(score, region_of_first, *after):
            for i in range(NT):
                t = dve.do(lambda e: e.max(top8[:, i, :], score[:, i, :]), *after)
                t_i = dve.do(lambda e: e.max_index(idx8[:, i, :], top8[:, i, :], score[:, i, :]), t)
            for k in range(TOPK):
                t = dve.do(lambda e: e.tensor_tensor(onehot[:, k, :, :], iota8[:, :, :],
                                                     idx8[:, :, k:k + 1].to_broadcast([P, NT, NE]), ALU.is_equal), t_i, c_all)
            t = dve.do(lambda e: e.tensor_tensor(both[:, :, :], onehot[:, 0, :, :], onehot[:, 1, :, :], ALU.add), t)
            z = dve.do(lambda e: e.memset(before[:, 0, :], 0.0))
            for i in range(1, NT):
                t = z = dve.do(lambda e: e.tensor_tensor(before[:, i, :], before[:, i - 1, :], both[:, i - 1, :], ALU.add), t, z)
            t = dve.do(lambda e: e.tensor_tensor(hit[:, 0, :], before[:, NT - 1, :], both[:, NT - 1, :], ALU.add), t)
            p_ok = pe.do(lambda e: (e.matmul(banks[:, 4, 0:NT * NE], lower[:, :], both[:, :, :].rearrange("p a b -> p (a b)"), start=True, stop=False),
                                    e.matmul(banks[:, 4, 0:NT * NE], ones[:, :], before[:, :, :].rearrange("p a b -> p (a b)"), start=False, stop=True),
                                    )[-1], t, *after)
            n_ok = pe.do(lambda e: e.matmul(banks[:, 5, 0:NE], ones[:, :], hit[:, 0, :], start=True, stop=True))
            t = dve.do(lambda e: e.tensor_copy(place[:, :, :].rearrange("p a b -> p (a b)"), banks[:, 4, 0:NT * NE]), p_ok)
            t = dve.do(lambda e: e.tensor_copy(count[:, :], banks[:, 5, 0:NE]), n_ok)
            t = dve.do(lambda e: e.tensor_tensor(thr[:, :, :], count[:, :].rearrange("p (a o) -> p a o", o=1).to_broadcast([P, NE, 16]),
                                                 iota16[:, :, :], ALU.is_gt), t)
            t = dve.do(lambda e: e.tensor_reduce(ntile[:, :], thr[:, :, :], AX.X, ALU.add), t)
            t = dve.do(lambda e: e.tensor_copy(upto_e[:, 0:1], ntile[:, 0:1]), t)
            for k in range(1, NE):
                t = dve.do(lambda e: e.tensor_tensor(upto_e[:, k:k + 1], upto_e[:, k - 1:k], ntile[:, k:k + 1], ALU.add), t)
            t = dve.do(lambda e: e.tensor_tensor(base_e[:, :], upto_e[:, :], ntile[:, :], ALU.subtract), t)
            t1 = dve.do(lambda e: e.tensor_scalar(base_e[:, :], base_e[:, :], float(P), None, ALU.mult), t)
            t = dve.do(lambda e: e.tensor_tensor(te[:, :, :], iotag[:, :, :],
                                                 upto_e[:, :].rearrange("p (o a) -> p o a", o=1).to_broadcast([P, GT, NE]), ALU.is_ge), t)
            t = dve.do(lambda e: e.tensor_reduce(te_f[:, :], te[:, :, :], AX.X, ALU.add), t)
            te_ok = dve.do(lambda e: e.tensor_scalar(tile_e[:, :], te_f[:, :], float(NE - 1), None, ALU.min), t)
            t = dve.do(lambda e: e.tensor_tensor(place[:, :, :], place[:, :, :],
                                                 base_e[:, :].rearrange("p (o a) -> p o a", o=1).to_broadcast([P, NT, NE]), ALU.add), t1)
            for k in range(TOPK):
                t2 = dve.do(lambda e: e.tensor_tensor(hit[:, :, :], place[:, :, :], onehot[:, k, :, :], ALU.mult), t)
                t = dve.do(lambda e: e.tensor_reduce(slot_f[:, k, :], hit[:, :, :], AX.X, ALU.add), t2)
            slot_ok = dve.do(lambda e: e.tensor_copy(slots[:, :, :], slot_f[:, :, :]), t)
            return slot_ok, te_ok

        def scatter(src, *after):
            for i in range(NT):
                for k in range(TOPK):
                    t = pool.dma(ld["scat"], lambda e: e.indirect_dma_start(
                        rows_in[:, :], bass.IndirectOffsetOnAxis(ap=slots[:, k, i:i + 1], axis=0), src[:, i, :], None), *after)
            return t

        def gather_mix(use, *after):
            done = []
            for i in range(NT):
                ns = [(i * TOPK + k) % 8 for k in range(TOPK)]
                ok = [pool.dma(ld[f"mix{n}"], lambda e: e.indirect_dma_start(
                    mixb[n], None, rows_out[:, :], bass.IndirectOffsetOnAxis(ap=slots[:, k, i:i + 1], axis=0)),
                    *after, *mix_free[n]) for k, n in enumerate(ns)]
                t = use(i, mixb[ns[0]], mixb[ns[1]], *ok)
                for n in ns:
                    mix_free[n] = [t]
                done.append(t)
            return done

        xg_b = [sb(f"xg{n}", [P, D]) for n in range(3)]
        ht_b = [sb(f"ht{n}", [P, 1024]) for n in range(2)]
        ys_b = [sb(f"ys{n}", [P, D]) for n in range(2)]
        xgt_b = [xnt[:, n, :, :] for n in range(2)]
        bcol = sb("bcol", [P, 2, 8])
        mixb = [hs_b[n // 4][:, (n % 4) * D:(n % 4 + 1) * D] for n in range(8)]
        mix_free = [[] for _ in mixb]
        B_X, B_H, B_T2, B_Y = 0, 1, 3, 5

        early_l1 = []

        def expert_of(lane, j, te_ok):
            lane.wait(te_ok)
            return lane.eng.value_load(tile_e[0:1, j:j + 1], min_val=0, max_val=NE - 1)

        def load_l1(r, *after):
            w = region(r)
            sp.dma(ld["w1"], lambda e: e.dma_start(w[:, 0:1024].rearrange("p (c f) -> p c f", c=KD),
                                                   io["W1"][r].rearrange("(c p) f -> p c f", p=P)), *after)
            sp.dma(ld["w1"], lambda e: e.dma_start(w[:, 1024:3072].rearrange("p (c f) -> p c f", c=M1 // P),
                                                   io["W2"][r].rearrange("(c p) f -> p c f", p=P)))
            return sp.dma(ld["w1"], lambda e: e.dma_start(w[:, 3072:4096].rearrange("p (c f) -> p c f", c=M1 // P),
                                                          io["W3"][r].rearrange("(c p) f -> p c f", p=P)))

        def expert_layer0(scat_ok, te_ok, w_ok, bank_free):
            xfree_, xtfree, hsfree, htfree, ysfree = [[], [], []], [[], []], [[], []], [[], []], [[], []]
            bfree = {b: list(bank_free) for b in range(8)}
            xt_ok, x_ok = {}, {}
            bcfree = [[], []]

            def fetch(j):
                n = j % 3
                if j < GT:
                    x_ok[j] = sp.dma(ld[f"xg{n}"], lambda e: e.dma_start(xg_b[n][:, :], rows_in[j * P:(j + 1) * P, :]),
                                     scat_ok, *xfree_[n])

            def inputs(j):
                n = j % 3
                t = pe.do(lambda e: [e.transpose(banks[:, B_X, c * P:(c + 1) * P], xg_b[n][:, c * P:(c + 1) * P], ident[:, :])
                                     for c in range(KD)][-1], x_ok[j], *bfree[B_X])
                xfree_[n] = [t]
                t = dve.do(lambda e: e.tensor_copy(xgt_b[j % 2].rearrange("p c t -> p (c t)"), banks[:, B_X, 0:D]),
                           t, *xtfree[j % 2])
                bfree[B_X] = [t]
                xt_ok[j] = t

            def outputs(j, h_ok, rd):
                by = B_Y + j % 2
                w2 = 2048
                t = pe.do(lambda e: [e.matmul(banks[:, by, 0:D], ht_b[j % 2][:, c * P:(c + 1) * P],
                                              weights[:, bass.ds(rd * REG + w2 + c * D, D)],
                                              start=(c == 0), stop=(c == F0 // P - 1)) for c in range(F0 // P)][-1],
                          h_ok, *bfree[by])
                htfree[j % 2] = [t]
                rv = expert_of(dve, j, te_ok)
                t = dve.do(lambda e: e.tensor_tensor(ys_b[j % 2][:, :], banks[:, by, 0:D],
                                                     ybias_f[:, bass.ds(rv * D, D)], ALU.add), t, *ysfree[j % 2])
                bfree[by] = [t]
                t = sp.dma(ld[f"ys{j % 2}"], lambda e: e.dma_start(rows_out[j * P:(j + 1) * P, :], ys_b[j % 2][:, :]), t)
                ysfree[j % 2] = [t]
                return t

            fetch(0)
            fetch(1)
            inputs(0)
            pending, ends = None, []
            for j in range(GT):
                n = j % 2
                fetch(j + 2)
                rd = expert_of(pe, j, te_ok)

                def emit(e):
                    for half in range(2):
                        for k in range(KD):
                            m = e.matmul(banks[:, B_H + half, :], xgt_b[n][:, k, :],
                                         weights[:, bass.ds(rd * REG + k * F0 + half * 512, 512)],
                                         start=(k == 0), stop=(k == KD - 1))
                    return m
                t = pe.do(emit, xt_ok[j], *w_ok, *bfree[B_H], *bfree[B_H + 1])
                xtfree[n] = [t]
                t1 = dve.do(lambda e: e.tensor_copy(hs_b[n][:, 0:512], banks[:, B_H, :]), t, *hsfree[n])
                t2 = act.do(lambda e: e.copy(hs_b[n][:, 512:1024], banks[:, B_H + 1, :]), t, *hsfree[n])
                bfree[B_H], bfree[B_H + 1] = [t1], [t2]
                if pending:
                    ends.append(outputs(*pending))
                if j % NT == 0 and j:
                    early_l1.append(j // NT - 1)
                    load_l1(early_l1[-1], *htfree[(j - 1) % 2])
                if j + 1 < GT:
                    inputs(j + 1)
                t = pe.do(lambda e: [e.transpose(banks[:, B_T2 + c // 4, (c % 4) * P:(c % 4 + 1) * P],
                                                 hs_b[n][:, c * P:(c + 1) * P], ident[:, :]) for c in range(8)][-1],
                          t1, t2, *bfree[B_T2], *bfree[B_T2 + 1])
                hsfree[n] = [t]
                rv = expert_of(dve, j, te_ok)
                bc = dve.do(lambda e: e.tensor_copy(bcol[:, n, :], b1f[:, bass.ds(rv * 8, 8)]), *bcfree[n])
                for c in range(8):
                    h_ok = act.do(lambda e: e.activation(ht_b[n][:, c * P:(c + 1) * P],
                                                         banks[:, B_T2 + c // 4, (c % 4) * P:(c % 4 + 1) * P],
                                                         ACT.Gelu, bias=bcol[:, n, c:c + 1]), t, bc, *htfree[n])
                bcfree[n] = [h_ok]
                bfree[B_T2] = bfree[B_T2 + 1] = [h_ok]
                pending = (j, h_ok, rd)
            ends.append(outputs(*pending))
            return ends[-2:], [h_ok, bfree[B_Y + (GT - 1) % 2][0], bfree[B_Y + GT % 2][0]]

        ybias_f = ybias[:, :, :].rearrange("p e d -> p (e d)")
        b1f = b1c[:, :, :].rearrange("p e c -> p (e c)")

        slot_ok, te_ok = route(logit, None, t)
        g1 = dve.do(lambda e: e.tensor_tensor(slot_f[:, 0, :], top8[:, :, 1], top8[:, :, 0], ALU.subtract), slot_ok)
        g2 = act.do(lambda e: e.activation(slot_f[:, 1, :], slot_f[:, 0, :], ACT.Exp), g1)
        g3 = dve.do(lambda e: e.tensor_scalar(slot_f[:, 0, :], slot_f[:, 1, :], 1.0, None, ALU.add), g2)
        g4 = dve.do(lambda e: e.reciprocal(gate[:, :, 0], slot_f[:, 0, :]), g3)
        gate_ok = dve.do(lambda e: e.tensor_tensor(gate[:, :, 1], gate[:, :, 0], slot_f[:, 1, :], ALU.mult), g4)
        scat = scatter(att, slot_ok, zero_ok, xn_ok[-1])
        ends, drained = expert_layer0(scat, te_ok, [w0_ld], [t, slot_ok])

        wgr = sb("wgr", [P, KD, NE])
        for c in range(KD):
            wg_ok = dve.do(lambda e: e.tensor_scalar(wgr[:, c, :], wgw[:, c, :], rmsw[:, c:c + 1], None, ALU.mult), s_ld)

        def mix0(i, y0, y1, ok0, ok1):
            t = dve.do(lambda e: e.scalar_tensor_tensor(x_sb[:, i, :], y0, gate[:, i, 0:1], x_sb[:, i, :], ALU.mult, ALU.add),
                       ok0, gate_ok, x_ld)
            return dve.do(lambda e: e.scalar_tensor_tensor(x_sb[:, i, :], y1, gate[:, i, 1:2], x_sb[:, i, :], ALU.mult, ALU.add),
                          t, ok1)
        x1_ok = gather_mix(mix0, *ends, *drained)
        if upto == 2:
            w1 = sp.dma(ld["store"], lambda e: e.dma_start(io["dbg0"].rearrange("(n p) d -> p n d", p=P), x_sb[:, :, :]), x1_ok[-1])
            sp.wait(w1)
            return

        for r_ in range(NE):
            if r_ not in early_l1:
                w1_ld = load_l1(r_, *drained, *x1_ok[-1:])
        yb_ld = sp.dma(ld["bias"], lambda e: e.dma_start(
            ybias[:, :, :], io["m3"].rearrange("(a e) d -> a e d", a=1).to_broadcast([P, NE, D])))

        score = sb("score", [P, NT, NE])

        def gate_logits(i, after):
            t = pe.do(lambda e: [e.matmul(banks[:, 4, i * NE:(i + 1) * NE], xnt[:, i % 2, c, :], wgr[:, c, :],
                                          start=(c == 0), stop=(c == KD - 1)) for c in range(KD)][-1], after, wg_ok)
            xfree[i % 2] = [t]
            return t
        smx = sb("smx", [P, NT])
        for i in range(NT):
            n = i % 2
            sq_ok = act.do(lambda e: e.activation(ys_b[n][:, :], x_sb[:, i, :], ACT.Square, accum_out=ssq[:, i:i + 1]), x1_ok[i], *ends)
            ce = act.do(lambda e: e.copy(
                condx[:, n, :].rearrange("p (b s) -> p b s", b=2),
                cond1[:, 2 * i:2 * i + 2].rearrange("p (b s) -> p b s", s=1).to_broadcast([COND + 2, 2, SEQ])),
                *cfree[n])
            cg_ok = pe.do(lambda e: e.matmul(banks[:, 5, i * NE:(i + 1) * NE], condx[:, n, :], gg1[:, :], start=True, stop=True),
                          ce, *drained)
            cfree[n] = [cg_ok]
            t1 = pe.do(lambda e: [e.transpose(banks[:, 2 + n, c * P:(c + 1) * P], x_sb[:, i, c * P:(c + 1) * P], ident[:, :])
                                  for c in range(KD)][-1], x1_ok[i], *tfree[n])
            t1 = act.do(lambda e: e.copy(xnt[:, n, :, :].rearrange("p c t -> p (c t)"), banks[:, 2 + n, 0:2 * P]), t1, *xfree[n])
            tfree[n] = [t1]
            if i > 0:
                l_ok = gate_logits(i - 1, turned_ok)
            turned_ok = t1
        l_ok = gate_logits(NT - 1, turned_ok)
        r_ok = rsqrt_cols(rms[:, :], ssq[:, :], 1e-6, [sq_ok])
        rows8 = lambda a: a.rearrange("p (n o) -> p n o", o=1).to_broadcast([P, NT, NE])
        t = dve.do(lambda e: e.tensor_tensor(score[:, :, :], banks[:, 4, 0:NT * NE].rearrange("p (n k) -> p n k", k=NE),
                                             rows8(rms[:, :]), ALU.mult), r_ok, l_ok)
        t = dve.do(lambda e: e.tensor_tensor(score[:, :, :], score[:, :, :], banks[:, 5, 0:NT * NE].rearrange("p (n k) -> p n k", k=NE),
                                             ALU.add), t, cg_ok)
        t = dve.do(lambda e: e.tensor_reduce(smx[:, :], score[:, :, :], AX.X, ALU.max), t)
        t = dve.do(lambda e: e.tensor_tensor(score[:, :, :], score[:, :, :], rows8(smx[:, :]), ALU.subtract), t)
        t = act.do(lambda e: e.activation(score[:, :, :], score[:, :, :], ACT.Exp), t)
        t = dve.do(lambda e: e.tensor_reduce(smx[:, :], score[:, :, :], AX.X, ALU.add), t)
        t = dve.do(lambda e: e.reciprocal(smx[:, :], smx[:, :]), t)
        t = dve.do(lambda e: e.tensor_tensor(score[:, :, :], score[:, :, :], rows8(smx[:, :]), ALU.mult), t)
        slot_ok, te_ok = route(score, None, t)
        gate_ok = dve.do(lambda e: e.tensor_copy(gate[:, :, :], top8[:, :, 0:TOPK]), slot_ok)
        scat = scatter(x_sb, slot_ok, x1_ok[-1])

        m1f = m1c[:, :, :].rearrange("p e c -> p (e c)")
        m2f = m2c[:, :, :].rearrange("p e c -> p (e c)")

        def expert_layer1(scat_ok, te_ok, w_ok, bank_free):
            A_X, A_H1, A_H2, A_T1, A_T2, A_Y = 0, 1, 2, 3, 4, 5
            bfree = {b: list(bank_free) for b in range(8)}
            fr = {(n, k): [] for n in ("xg", "xgt", "h1", "h2", "t1", "t2", "bc", "ys") for k in range(3)}
            ok, rd, ends = {}, {}, []

            def fetch(j):
                n = j % 3
                if j < GT:
                    ok["load", j] = sp.dma(ld[f"xg{n}"], lambda e: e.dma_start(xg_b[n][:, :], rows_in[j * P:(j + 1) * P, :]),
                                           scat_ok, *fr["xg", n])

            def inputs(j):
                n = j % 3
                t = pe.do(lambda e: [e.transpose(banks[:, A_X, c * P:(c + 1) * P], xg_b[n][:, c * P:(c + 1) * P], ident[:, :])
                                     for c in range(KD)][-1], ok["load", j], *bfree[A_X])
                fr["xg", n] = [t]
                t = dve.do(lambda e: e.tensor_copy(xgt_b[j % 2].rearrange("p c t -> p (c t)"), banks[:, A_X, 0:D]),
                           t, *fr["xgt", j % 2])
                bfree[A_X] = [t]
                ok["x", j] = t

            def hidden(j, bank, src, chunks, offset):
                return pe.do(lambda e: [e.matmul(banks[:, bank, :], src(c), weights[:, bass.ds(rd[j] * REG + offset + c * M1, M1)],
                                                 start=(c == 0), stop=(c == chunks - 1)) for c in range(chunks)][-1],
                             ok["x" if offset == 0 else "t1", j], *w_ok, *bfree[bank])

            def turned(j, bank, src, after):
                return pe.do(lambda e: [e.transpose(banks[:, bank, c * P:(c + 1) * P], src[:, c * P:(c + 1) * P], ident[:, :])
                                        for c in range(M1 // P)][-1], after, *bfree[bank])

            fetch(0)
            fetch(1)
            inputs(0)
            for j in range(GT + 2):
                fetch(j + 2)
                if j < GT:
                    n = j % 2
                    rd[j] = expert_of(pe, j, te_ok)
                    t = hidden(j, A_H1, lambda c: xgt_b[n][:, c, :], KD, 0)
                    fr["xgt", n] = [t]
                    h1 = dve.do(lambda e: e.tensor_copy(hs_b[n][:, 0:M1], banks[:, A_H1, :]), t, *fr["h1", n])
                    bfree[A_H1] = [h1]
                    rv = expert_of(dve, j, te_ok)
                    dve.do(lambda e: e.tensor_copy(bcol[:, n, 0:4], m1f[:, bass.ds(rv * 4, 4)]), *fr["bc", n])
                    bc = dve.do(lambda e: e.tensor_copy(bcol[:, n, 4:8], m2f[:, bass.ds(rv * 4, 4)]))
                    if j + 1 < GT:
                        inputs(j + 1)
                if 1 <= j <= GT:
                    q, m = j - 1, (j - 1) % 2
                    t = hidden(q, A_H2, lambda c: ht_b[m][:, c * P:(c + 1) * P], M1 // P, 1024)
                    fr["t1", m] = [t]
                    h2 = act.do(lambda e: e.copy(hs_b[m][:, M1:], banks[:, A_H2, :]), t, *fr["h2", m])
                    bfree[A_H2] = [h2]
                if j < GT:
                    t = turned(j, A_T1, hs_b[n][:, 0:M1], h1)
                    fr["h1", n] = [t]
                    for c in range(4):
                        t1 = act.do(lambda e: e.activation(ht_b[n][:, c * P:(c + 1) * P], banks[:, A_T1, c * P:(c + 1) * P],
                                                           ACT.Relu, bias=bcol[:, n, c:c + 1]), t, bc, *fr["t1", n])
                    bfree[A_T1], ok["t1", j] = [t1], t1
                if 2 <= j:
                    q2, m2 = j - 2, (j - 2) % 2
                    by = A_Y + q2 % 2
                    t = pe.do(lambda e: [e.matmul(banks[:, by, 0:D], ht_b[m2][:, M1 + c * P:M1 + (c + 1) * P],
                                                  weights[:, bass.ds(rd[q2] * REG + 3072 + c * D, D)],
                                                  start=(c == 0), stop=(c == M1 // P - 1)) for c in range(M1 // P)][-1],
                              ok["t2", q2], *bfree[by])
                    fr["t2", m2] = [t]
                    rv = expert_of(dve, q2, te_ok)
                    t = dve.do(lambda e: e.tensor_tensor(ys_b[m2][:, :], banks[:, by, 0:D],
                                                         ybias_f[:, bass.ds(rv * D, D)], ALU.add), t, yb_ld, *fr["ys", m2])
                    bfree[by] = [t]
                    t = sp.dma(ld[f"ys{m2}"], lambda e: e.dma_start(rows_out[q2 * P:(q2 + 1) * P, :], ys_b[m2][:, :]), t)
                    fr["ys", m2] = [t]
                    ends.append(t)
                if 1 <= j <= GT:
                    t = turned(q, A_T2, hs_b[m][:, M1:], h2)
                    fr["h2", m] = [t]
                    for c in range(4):
                        t2 = dve.do(lambda e: e.tensor_scalar(ht_b[m][:, M1 + c * P:M1 + (c + 1) * P], banks[:, A_T2, c * P:(c + 1) * P],
                                                              bcol[:, m, 4 + c:5 + c], 0.0, ALU.add, ALU.max), t, *fr["t2", m])
                    bfree[A_T2], ok["t2", q] = [t2], t2
                    fr["bc", m] = [ok["t1", q], t2]
            return ends[-2:], [t2, ok["t1", GT - 1], bfree[A_Y][0], bfree[A_Y + 1][0], fr["t2", 0][0], fr["t2", 1][0]]

        ends, drained = expert_layer1(scat, te_ok, [w1_ld], [t, slot_ok, gate_ok])
        mix_free = [[] for _ in mixb]

        NC, G2, SUB = PE_N // P, 2 * P, 16
        arena[0] = 0
        downT = carve(KD, PE_N)
        up_sb = carve(NC, D)
        wkey = carve(KD, 2 * PH * PKEYS)
        xnT = carve(KD, TOK)
        iotax = carve(P * SUB // 2).bitcast(BF16).rearrange("p (a t) -> p a t", t=SUB)
        hid = carve(NC, G2)
        hidf = hid.rearrange("p c t -> p (c t)")
        wqp = hidf[:, 0:4096].rearrange("p (g n) -> p g n", g=2 * PH)
        keyp = hidf[:, 4096:5120].rearrange("p (g n) -> p g n", g=2 * PH)
        attf = att[:, :, :].rearrange("p n d -> p (n d)")
        lo_b, hi_b, hw_b = [], [], []
        for n in range(2):
            o = n * 2048
            lo_b.append(attf[:, o:o + 1024].bitcast(BF16).rearrange("p (a t) -> p a t", t=SUB))
            hi_b.append(attf[:, o + 1024:o + 1280].bitcast(BF16).rearrange("p (a t) -> p a t", t=SUB))
            hw_b.append(attf[:, o + 1280:o + 2048].bitcast(BF16).rearrange("p (m a t) -> p m a t", m=3, t=SUB))
        sims, rest = [ht_b[0][:, :], tokens4[:, :]], ht_b[1][:, :]
        scr = [hs_b[0][:, :], hs_b[1][:, :]]
        top = scr[0][:, 0:256]
        topi = scr[0][:, 256:512].bitcast(U32)
        w16 = scr[0][:, 512:640]
        j16 = scr[0][:, 640:768].bitcast(U32)
        packs = scr[1][:, 0:384]
        cand = ybias_f[:, 0:432].rearrange("p (h j) -> p h j", h=PH)
        cand2 = ybias_f[:, 432:864].rearrange("p (h j) -> p h j", h=PH)
        lk = ybias_f[:, 864:2048].bitcast(BF16)
        edges = [thr[:, :, :].rearrange("p e m -> p (e m)").bitcast(BF16), xg_b[1][:, P * 3 // 2:D].bitcast(BF16)]
        ta, tm, td = (a.rearrange("p (m h) -> p m h", h=PH) for a in (edges[0][:, 0:P], edges[0][:, P:2 * P], edges[1]))
        di = scr[1][:, 384:512].bitcast(BF16).rearrange("p (s m h) -> p s m h", s=2, m=16)
        key_f = scr[1][:, 512:768]
        cmp_b = carve(16 * P // 2).bitcast(BF16).rearrange("p (m n) -> p m n", m=16)
        prod = lk[:, 0:2048].rearrange("p (m n) -> p m n", m=16)
        prod2 = rest.bitcast(BF16).rearrange("p (m n) -> p m n", m=16)
        jh = lk[:, 2048:2176]
        bh = lk[:, 2176:2304]
        i1h = scr[1][:, 768:832].bitcast(BF16)
        i2h = scr[1][:, 832:896].bitcast(BF16)
        q_h = scr[1][:, 896:960].bitcast(BF16)
        turn = [xg_b[0][:, n * P:(n + 1) * P].bitcast(BF16).rearrange("p (a n) -> p a n", a=2) for n in range(2)]
        wpart = [xg_b[1 + n][:, 0:P * 3 // 2].bitcast(BF16).rearrange("p (a n) -> p a n", a=3) for n in range(2)]
        wres = rest[:, 512:768].rearrange("p (a n) -> p a n", a=2)
        sum8 = ybias_f[:, 0:512].bitcast(BF16).rearrange("p (m n) -> p m n", m=8)

        a_free = [*drained]
        k_ld = sp.dma(ld["w0"], lambda e: e.dma_start(wqp, io["wqp"]), *a_free)
        k_ld = sp.dma(ld["w0"], lambda e: e.dma_start(keyp, io["keysT"]))
        blocks = [(0, 1, 16), (1, 1, 8), (2, 2, 5), (4, 4, 3), (8, 8, 1)]
        first = [0] * 17
        for a0, na, nb in blocks:
            for a in range(a0, a0 + na):
                first[a + 1] = first[a] + nb
        NCAND = first[16]
        kc = [dve.do(lambda e: e.memset(t_[:, m, :], v), *a_free) for m in range(16)
              for t_, v in ((ta, float(first[m])), (tm, float(m)), (td, float(first[m] - first[m - 1]) if m else 0.0))]
        for c in range(KD):
            for half in range(2):
                b = 2 * c + half
                t = pe.do(lambda e: [e.matmul(banks[:, b, g * PKEYS:(g + 1) * PKEYS], wqp[:, half * 8 + g, c * P:(c + 1) * P],
                                              keyp[:, half * 8 + g, :], start=True, stop=True) for g in range(8)][-1], k_ld, *a_free)
                wk_ok = act.do(lambda e: e.copy(wkey[:, c, half * 512:(half + 1) * 512], banks[:, b, :]), t)

        sq, tf = [[], []], [[wk_ok], [wk_ok]]
        sq_ok, xn_ok, loads = {}, {}, []
        SPLIT = 4
        part = PE_N // SPLIT
        for c in range(SPLIT):
            loads.append(lambda e, c=c: e.dma_start(downT[:, :, c * part:(c + 1) * part],
                                                    io["downT"][:, c * part:(c + 1) * part].rearrange("(k p) n -> p k n", p=P)))
        for c in range(SPLIT):
            loads.append(lambda e, c=c: e.dma_start(up_sb[:, c * part // P:(c + 1) * part // P, :],
                                                    io["up"][c * part:(c + 1) * part, :].rearrange("(c p) n -> p c n", p=P)))

        def mix1(i, y0, y1, ok0, ok1):
            n = i % 2
            t = dve.do(lambda e: e.tensor_scalar(att[:, i, :], y0, gate[:, i, 0:1], None, ALU.mult), ok0)
            t = dve.do(lambda e: e.scalar_tensor_tensor(att[:, i, :], y1, gate[:, i, 1:2], att[:, i, :], ALU.mult, ALU.add),
                       t, ok1)
            sq_ok[i] = act.do(lambda e: e.activation(ys_b[n][:, :], att[:, i, :], ACT.Square, accum_out=ssq[:, i:i + 1]),
                              t, *ends, *sq[n])
            sq[n] = [sq_ok[i]]
            if i % 2 == 0:
                weight_ld.append(sp.dma(ld["down" if i // 2 < SPLIT else "up"], loads[i // 2], t))
            if i % 4 == 1 and i > 4:
                norm_group(i // 4 - 1)
            return t

        def norm_group(q):
            r_ok = rsqrt_cols(rms[:, 4 * q:4 * q + 4], ssq[:, 4 * q:4 * q + 4], 1e-5, [sq_ok[4 * q + 3]])
            for i in range(4 * q, 4 * q + 4):
                n = i % 2
                t = dve.do(lambda e: e.tensor_scalar(att[:, i, :], att[:, i, :], rms[:, i:i + 1], None, ALU.mult), r_ok)
                t = pe.do(lambda e: [e.transpose(banks[:, 4 + n, c * P:(c + 1) * P], att[:, i, c * P:(c + 1) * P], ident[:, :])
                                     for c in range(KD)][-1], t, *tf[n])
                att_free[0] = t
                for c in range(KD):
                    xn_ok[i] = act.do(lambda e: e.activation(xnT[:, c, i * P:(i + 1) * P], banks[:, 4 + n, c * P:(c + 1) * P],
                                                             ACT.Copy, scale=normw[:, c:c + 1]), t, s_ld)
                tf[n] = [xn_ok[i]]

        weight_ld, att_free = [], [None]
        gather_mix(mix1, *ends, *drained)
        norm_group(NT // 4 - 1)
        att_free, xn_ok = att_free[0], xn_ok[NT - 1]
        d_ld, u_ld = weight_ld[SPLIT - 1], weight_ld[-1]
        io_ok = pool.do(lambda e: e.iota(iotax, [[1, P], [0, SUB]], base=0, channel_multiplier=0,
                                         allow_small_or_imprecise_dtypes=True), *a_free)

        B_SIM, B_HID, B_G, B_OUT, B_TR = 0, 1, 3, 5, 7
        pf = {b: [xn_ok, wk_ok] for b in range(8)}
        sf = {"sims0": [wk_ok, att_free], "sims1": [wk_ok, att_free], "packs": [], "turn": [], "hid": [wk_ok], "lo0": [att_free], "lo1": [att_free]}
        s_ok, kept, w_ok = {}, {}, {}

        def similar(i):
            for half in range(2):
                t = pe.do(lambda e: [e.matmul(banks[:, B_SIM, :], xnT[:, c, i * P:(i + 1) * P], wkey[:, c, half * 512:(half + 1) * 512],
                                              start=(c == 0), stop=(c == KD - 1)) for c in range(KD)][-1], xn_ok, *pf[B_SIM])
                s_ok[i] = act.do(lambda e: e.copy(sims[i % 2][:, half * 512:(half + 1) * 512], banks[:, B_SIM, :]),
                                 t, *sf[f"sims{i % 2}"])
                pf[B_SIM] = [s_ok[i]]

        def select(i):

            def top16(vals, idxs, src, spare_, *after):
                n = src.shape[1]
                a = [dve.do(lambda e: e.max(vals(g)[:, 0:8], src[:, g, :]), *after) for g in range(n)]
                b = [dve.do(lambda e: e.max_index(idxs(g)[:, 0:8], vals(g)[:, 0:8], src[:, g, :]), a[g]) for g in range(n)]
                b = [dve.do(lambda e: e.match_replace(spare_[:, g, :], vals(g)[:, 0:8], src[:, g, :], -3e38), a[g]) for g in range(n)]
                a = [dve.do(lambda e: e.max(vals(g)[:, 8:16], spare_[:, g, :]), b[g]) for g in range(n)]
                b = [dve.do(lambda e: e.max_index(idxs(g)[:, 8:16], vals(g)[:, 8:16], spare_[:, g, :]), a[g]) for g in range(n)]
                return b[-1]

            s3 = sims[i % 2].rearrange("p (g k) -> p g k", k=PKEYS)
            t = top16(lambda g: top[:, g * 16:(g + 1) * 16], lambda g: topi[:, g * 16:(g + 1) * 16], s3,
                      rest.rearrange("p (g k) -> p g k", k=PKEYS), s_ok[i])
            sf[f"sims{i % 2}"] = [t]
            tp = top.rearrange("p (h s r) -> p h s r", h=PH, s=2)
            for a0, na, nb in blocks:
                sh = [P, PH, na, nb]
                c_ok = dve.do(lambda e: e.tensor_tensor(
                    cand[:, :, first[a0]:first[a0 + na]].rearrange("p h (a b) -> p h a b", a=na),
                    tp[:, :, 0, a0:a0 + na].rearrange("p h (a o) -> p h a o", o=1).to_broadcast(sh),
                    tp[:, :, 1, 0:nb].rearrange("p h (o b) -> p h o b", o=1).to_broadcast(sh), ALU.add), t)
            k1 = dve.do(lambda e: e.tensor_copy(key_f, topi), t)
            kf = key_f.rearrange("p (h s m) -> p s m h", h=PH, s=2)
            for s in range(2):
                dve.do(lambda e: e.tensor_copy(di[:, s, 0, :], kf[:, s, 0, :]), k1)
                k2 = dve.do(lambda e: e.tensor_tensor(di[:, s, 1:16, :], kf[:, s, 1:16, :], kf[:, s, 0:15, :], ALU.subtract))
            t = top16(lambda h: w16[:, h * 16:(h + 1) * 16], lambda h: j16[:, h * 16:(h + 1) * 16], cand, cand2, c_ok)
            turned_ = lambda a: a.rearrange("p (h r) -> p r h", h=PH)
            t1 = dve.do(lambda e: e.tensor_copy(jh.rearrange("p (r h) -> p r h", h=PH), turned_(j16)), t)
            dve.do(lambda e: e.tensor_scalar(packs[:, 0:P].rearrange("p (r h) -> p r h", h=PH), turned_(w16), 0.0, None, ALU.max),
                   *sf["packs"])

            by_rank = lambda a: a.rearrange("p m (r h) -> p m r h", h=PH)
            every_rank = lambda a: a.rearrange("p m (o h) -> p m o h", o=1).to_broadcast([P, 16, 16, PH])

            def compare(position, edge, *after):
                return dve.do(lambda e: e.tensor_tensor(
                    by_rank(cmp_b), position.rearrange("p (o r h) -> p o r h", o=1, h=PH).to_broadcast([P, 16, 16, PH]),
                    every_rank(edge), ALU.is_ge), *after)

            def products(dst, steps, *after):
                return dve.do(lambda e: e.tensor_tensor(by_rank(dst), by_rank(cmp_b), every_rank(steps), ALU.mult), *after)

            def tree(prod_, half, dst, t):
                src, dst_ = prod_, half
                for w in (8, 4, 2):
                    t = dve.do(lambda e: e.tensor_tensor(dst_[:, 0:w, :], src[:, 0:2 * w:2, :], src[:, 1:2 * w:2, :], ALU.add), t)
                    yield t
                    src, dst_ = dst_, src
                yield dve.do(lambda e: e.tensor_tensor(dst, src[:, 0, :], src[:, 1, :], ALU.add), t)

            c_ok = compare(jh, ta, t1, kc[-1], k2)
            tb = products(prod, td, c_ok)
            ti = products(prod2, di[:, 0, :, :], c_ok)
            for tb, ti in zip(tree(prod, sum8, bh, tb), tree(prod2, cmp_b, i1h, ti)):
                pass
            t2 = dve.do(lambda e: e.tensor_tensor(bh, jh, bh, ALU.subtract), tb)
            tq = dve.do(lambda e: e.tensor_scalar(q_h, i1h, float(PKEYS // 2), None, ALU.is_ge), ti)
            c_ok = compare(bh, tm, t2)
            dve.do(lambda e: e.scalar_tensor_tensor(packs[:, P:2 * P], q_h, -float(PKEYS // 2), i1h, ALU.mult, ALU.add), tq)
            t2 = products(prod, di[:, 1, :, :], c_ok)
            for t2 in tree(prod, sum8, i2h, t2):
                pass
            t3 = dve.do(lambda e: e.scalar_tensor_tensor(packs[:, 2 * P:3 * P], q_h, float(PKEYS), i2h, ALU.mult, ALU.add), t2)
            return t3

        def turn_over(i, picked_ok):
            turn_, wpart_ = turn[i % 2], wpart[i % 2]
            t = pe.do(lambda e: [e.transpose(banks[:, B_TR, m * P:(m + 1) * P], packs[:, m * P:(m + 1) * P], ident[:, :])
                                 for m in range(3)][-1], picked_ok, *pf[B_TR])
            sf["packs"] = [t]
            act.do(lambda e: e.copy(wpart_[:, 0, :], banks[:, B_TR, 0:P]), t, *sf["turn"])
            return act.do(lambda e: e.copy(turn_.rearrange("p a n -> p (a n)"), banks[:, B_TR, P:3 * P]))

        def rest_parts(i, turned_ok):
            wpart_ = wpart[i % 2]
            t = dve.do(lambda e: e.tensor_tensor(wres[:, 0, :], banks[:, B_TR, 0:P], wpart_[:, 0, :], ALU.subtract), turned_ok)
            pf[B_TR] = [t]
            t = dve.do(lambda e: e.tensor_copy(wpart_[:, 1, :], wres[:, 0, :]), t, *sf["turn"])
            t = dve.do(lambda e: e.tensor_tensor(wres[:, 1, :], wres[:, 0, :], wpart_[:, 1, :], ALU.subtract), t)
            kept[i] = dve.do(lambda e: e.tensor_copy(wpart_[:, 2, :], wres[:, 1, :]), t)

        def outputs_of(g, n, q):
            o_ok[2 * g + n] = pe.do(lambda e: [e.matmul(banks[:, B_OUT + n, 0:D], hid[:, c, n * P:(n + 1) * P], up_sb[:, c, :],
                                                        start=(c == 0), stop=(c == NC - 1)) for c in (2 * q, 2 * q + 1)][-1],
                                    w_ok[2 * g + n], u_ld, *pf[B_OUT + n])

        def burst(g, qs):
            for q in qs:
                if g > 0:
                    for n in range(2):
                        if n or q >= early[g - 1]:
                            outputs_of(g - 1, n, q)
                    sf["hid"] = [o_ok[2 * g - 1], o_ok[2 * g - 2]]
                if g < GROUPS:
                    b = B_HID + q % 2
                    t = pe.do(lambda e: [e.matmul(banks[:, b, h * G2:(h + 1) * G2], downT[:, c, (2 * q + h) * P:(2 * q + h + 1) * P],
                                                  xnT[:, c, g * G2:(g + 1) * G2], start=(c == 0), stop=(c == KD - 1))
                                         for h in range(2) for c in range(KD)][-1], d_ld, *pf[b])
                    h_ok[g] = act.do(lambda e: e.activation(hid[:, 2 * q:2 * q + 2, :].rearrange("p c t -> p (c t)"), banks[:, b, :],
                                                            ACT.Gelu), t, *sf["hid"])
                    pf[b] = [h_ok[g]]

        def spread(i, s):
            n = s % 2
            cols = slice(s * SUB, (s + 1) * SUB)
            one = lambda a, k: a.rearrange("p (o t) -> p o t", o=1).to_broadcast([P, k, SUB])
            th = dve.do(lambda e: e.tensor_tensor(hi_b[n], iotax[:, 0:NC, :], one(turn[i % 2][:, 0, cols], NC), ALU.is_equal), kept[i], io_ok, *sf[f"lo{n}"])
            dve.do(lambda e: e.tensor_tensor(lo_b[n], iotax, one(turn[i % 2][:, 1, cols], P), ALU.is_equal))
            t1 = dve.do(lambda e: e.tensor_tensor(
                hw_b[n], hi_b[n].rearrange("p (o a) t -> p o a t", o=1).to_broadcast([P, 3, NC, SUB]),
                wpart[i % 2][:, :, cols].rearrange("p m (o t) -> p m o t", o=1).to_broadcast([P, 3, NC, SUB]), ALU.mult), th)
            b = B_G + n
            t = pe.do(lambda e: [e.matmul(banks[:, b, k * NC:(k + 1) * NC], lo_b[n][:, :, k], hw_b[n][:, m, :, k],
                                          start=(m == 0), stop=(m == 2)) for k in range(SUB) for m in range(3)][-1], t1, *pf[b])
            sf[f"lo{n}"] = [t]
            return t

        def weigh(i, s, g_ok):
            b = B_G + s % 2
            t0 = (i % 2) * P + s * SUB
            t = dve.do(lambda e: e.tensor_tensor(hid[:, :, t0:t0 + SUB], hid[:, :, t0:t0 + SUB],
                                                 banks[:, b, :].rearrange("p (t c) -> p c t", c=NC), ALU.mult), g_ok, h_ok[i // 2])
            pf[b] = [t]
            w_ok[i] = t

        def add_out(i):
            t = dve.do(lambda e: e.tensor_tensor(x_sb[:, i, :], x_sb[:, i, :], banks[:, B_OUT + i % 2, 0:D], ALU.add), o_ok[i])
            pf[B_OUT + i % 2] = [t]
            return sp.dma(ld["store"], lambda e: e.dma_start(out[i * P:(i + 1) * P, :], x_sb[:, i, :]), t)

        GROUPS = TOK // G2
        NQ, NS = NC // 2, P // SUB
        o_ok, h_ok = {}, {}
        early = [4] * (GROUPS - 1) + [NQ]
        similar(0)
        similar(1)
        for g in range(GROUPS):
            i0, i1 = 2 * g, 2 * g + 1
            p0 = select(i0)
            burst(g, range(NQ // 2))
            turned_ok = turn_over(i0, p0)
            burst(g, range(NQ // 2, NQ))
            p1 = select(i1)
            rest_parts(i0, turned_ok)
            turned_ok = turn_over(i1, p1)
            prev, out_q = None, 0
            for step in range(2 * NS):
                i, s = (i0, i1)[step // NS], step % NS
                g_ok = spread(i, s)
                if step == 2:
                    rest_parts(i1, turned_ok)
                    if g > 0:
                        add_out(i0 - 2)
                        add_out(i0 - 1)
                if step in (3, 6) and g + 1 < GROUPS:
                    similar(i0 + 2 + (step == 6))
                if prev:
                    weigh(*prev)
                prev = (i, s, g_ok)
                if step > NS:
                    upto_q = early[g] * (step - NS) // (NS - 1)
                    for q in range(out_q, upto_q):
                        outputs_of(g, 0, q)
                    out_q = upto_q
            weigh(*prev)
            sf["turn"] = [w_ok[i1]]
        burst(GROUPS, range(NQ))
        add_out(NT - 2)
        y_st = add_out(NT - 1)
        sp.wait(y_st)


def layout(i):
    A = {k: np.asarray(v) for k, v in i.items()}
    x = A["x"].reshape(TOK, D)

    def cols(b):
        return b.reshape(NE, -1, P).transpose(2, 0, 1)
    order = np.arange(PE_N).reshape(2, PKEYS // 2, PKEYS).transpose(1, 0, 2).reshape(-1)
    wv = A["L0_cond_Wv"].T.reshape(D, HEADS // 2, 2, DH)
    d = dict(
        x=x, xT=x.T, mask=A["mask_SxS_bk1"].view(np.uint32), condT=A["cond_256"].T,
        wqT=A["L0_cond_Wq"].T, wkT=A["L0_cond_Wk"].T, woT=A["L0_cond_Wo"].T,
        wvT=wv.transpose(0, 2, 1, 3).reshape(D, D),
        rms_scale=A["L0_cond_rms_scale"].reshape(1, D), wcT=A["L0_cond_Wc"].T, bc=A["L0_cond_bc"].reshape(1, 2 * D),
        routerT=A["L0_ffn_router_w"].T, w1T=A["L0_ffn_w1"].transpose(0, 2, 1), b1=cols(A["L0_ffn_b1"]),
        w2T=A["L0_ffn_w2"].transpose(0, 2, 1), b2=A["L0_ffn_b2"],
        rms_w=A["L1_cond_rms_w"].reshape(KD, P).T, wg_W=A["L1_cond_wg_W"], wg_b=A["L1_cond_wg_b"].reshape(1, NE),
        gg_W=A["L1_cond_gg_W"], gg_b=A["L1_cond_gg_b"].reshape(1, NE),
        W1=A["L1_cond_W1"], m1=cols(A["L1_cond_b1"]), W2=A["L1_cond_W2"], m2=cols(A["L1_cond_b2"]),
        W3=A["L1_cond_W3"], m3=A["L1_cond_b3"], norm_w=A["L1_ffn_norm_w"].reshape(KD, P).T,
        wqp=A["L1_ffn_wq"].reshape(D, 2 * PH, PDK).transpose(2, 1, 0),
        keysT=A["L1_ffn_keys"].transpose(3, 0, 2, 1).reshape(PDK, 2 * PH, PKEYS),
        downT=A["L1_ffn_expert_down"][order].T, up=A["L1_ffn_expert_up"][order],
    )
    return {k: np.ascontiguousarray(v) for k, v in d.items()}


def kernel(**inputs):
    from concourse import bacc
    from concourse.bass_utils import run_bass_kernel_spmd

    arrays = layout(inputs)
    nc = bacc.Bacc("TRN2", target_bir_lowering=False, num_devices=1)
    io = {n: nc.dram_tensor(f"in_{n}", a.shape, mybir.dt.from_np(a.dtype), kind="ExternalInput").ap()
          for n, a in arrays.items()}
    out = nc.dram_tensor("out_0", [TOK, D], F32, kind="ExternalOutput").ap()
    build(nc, io, out)
    r = run_bass_kernel_spmd(nc, [{f"in_{n}": a for n, a in arrays.items()}], core_ids=[0])
    return r.results[0]["out_0"].reshape(BATCH, SEQ, D)
```

```python
from contextlib import ExitStack

import numpy as np

import concourse.bass as bass
from concourse import mybir

F32 = mybir.dt.float32
BF16 = mybir.dt.bfloat16
U32 = mybir.dt.uint32
I32 = mybir.dt.int32
U8 = mybir.dt.uint8
ALU = mybir.AluOpType
ACT = mybir.ActivationFunctionType
AX = mybir.AxisListType

P = 128
BATCH, SEQ, D = 32, 64, 256
TOK = BATCH * SEQ
NT = TOK // P
KD = D // P
HEADS, DH = 16, 16
COND = 64
NE, TOPK = 8, 2
F0 = 1024
M1 = 512
GT = TOPK * NT + NE - 1
PH, PKEYS, PDK = 8, 64, 128
PE_N = PKEYS * PKEYS
BIG = 1e30
ROUND = 1.5 * 2 ** 23


class Lane:

    def __init__(self, eng, sem):
        self.eng, self.sem, self.count, self.passed = eng, sem, 0, {}

    def wait(self, *after):
        for sem, value in after:
            if self.passed.get(id(sem), 0) < value:
                self.passed[id(sem)] = value
                self.eng.wait_ge(sem, value)

    def do(self, emit, *after):
        self.wait(*after)
        self.count += 1
        emit(self.eng).then_inc(self.sem, 1)
        return self.sem, self.count

    def dma(self, slot, emit, *after):
        self.wait(*after)
        slot.count += 16
        emit(self.eng).then_inc(slot.sem, 16)
        return slot.sem, slot.count


class Slot:

    def __init__(self, sem):
        self.sem, self.count = sem, 0


def build(nc, io, out):
    root = ExitStack()
    with root:
        scopes = [root]

        def sb(name, shape, dt=F32):
            return scopes[-1].enter_context(nc.sbuf_tensor(name, shape, dt))

        def slot(name):
            return Slot(root.enter_context(nc.semaphore(name)))

        pe, dve, act, pool, sp = (Lane(eng, root.enter_context(nc.semaphore("done_" + n))) for n, eng in (
            ("pe", nc.tensor), ("dve", nc.vector), ("act", nc.scalar), ("pool", nc.gpsimd), ("sp", nc.sync)))
        banks = root.enter_context(nc.psum_tensor("banks", [P, 8, 512], F32))

        ident = sb("ident", [P, P])
        lower = sb("lower", [P, P])
        ones = sb("ones", [P, P])
        x_sb = sb("x_sb", [P, NT, D])
        att = sb("att", [P, NT, D])
        REG = 4096
        NREG = NE
        iota16 = sb("iota16", [P, NE, 16])
        iota8 = sb("iota8", [P, NT, NE])
        iotag = sb("iotag", [P, GT, NE])
        b1c = sb("b1c", [P, NE, F0 // P])
        m1c = sb("m1c", [P, NE, M1 // P])
        m2c = sb("m2c", [P, NE, M1 // P])
        ybias = sb("ybias", [P, NE, D])
        cond1 = sb("cond1", [COND + 2, BATCH])
        gg1 = sb("gg1", [COND + 2, NE])
        rw = sb("rw", [P, KD, NE])
        wgw = sb("wgw", [P, KD, NE])
        rmsw = sb("rmsw", [P, KD])
        normw = sb("normw", [P, KD])
        gate = sb("gate", [P, NT, TOPK])
        slots = sb("slots", [P, TOPK, NT], U32)
        tile_e = sb("tile_e", [P, GT], I32)
        iotap = sb("iotap", [P, P])
        token_t = sb("token_t", [P, NT])
        token_p = sb("token_p", [P, 1])
        inverse = sb("inverse", [P, GT], U32)

        rows_in = nc.dram_tensor("rows_in", [TOK, D], F32, kind="Internal").ap()
        rows_out = nc.dram_tensor("rows_out", [GT * P, D], F32, kind="Internal").ap()

        ld = {n: slot("ld_" + n) for n in
              ("x", "bias", "small", "wqkvo", "wq", "w0", "w1", "xt0", "xt1", "rows",
               "store", "mask", "down", "up", "xg0", "xg1", "xg2", "ys0", "ys1", *(f"mix{n}" for n in range(8)))}

        c1 = pool.do(lambda e: e.memset(ident[:, :], 0.0))
        c1 = pool.do(lambda e: e.affine_select(out=ident[:, :], in_=ident[:, :], compare_op=ALU.not_equal,
                                               fill=1.0, base=0, pattern=[[-1, P]], channel_multiplier=1), c1)
        c2 = pool.do(lambda e: e.memset(ones[:, :], 1.0))
        pool.do(lambda e: e.affine_select(out=lower[:, :], in_=ones[:, :], compare_op=ALU.is_gt,
                                               fill=0.0, base=0, pattern=[[1, P]], channel_multiplier=-1), c2)
        pool.do(lambda e: e.iota(iota16[:, :, :], [[0, NE], [P, 16]], base=0, channel_multiplier=0,
                                      allow_small_or_imprecise_dtypes=True))
        pool.do(lambda e: e.iota(iotap[:, :], [[1, P]], base=0, channel_multiplier=0, allow_small_or_imprecise_dtypes=True))
        pool.do(lambda e: e.iota(token_t[:, :], [[P, NT]], base=0, channel_multiplier=0, allow_small_or_imprecise_dtypes=True))
        pool.do(lambda e: e.iota(token_p[:, :], [[0, 1]], base=0, channel_multiplier=1, allow_small_or_imprecise_dtypes=True))
        pool.do(lambda e: e.iota(iota8[:, :, :], [[0, NT], [1, NE]], base=0, channel_multiplier=0,
                                      allow_small_or_imprecise_dtypes=True))
        c_all = pool.do(lambda e: e.iota(iotag[:, :, :], [[1, GT], [0, NE]], base=0, channel_multiplier=0,
                                         allow_small_or_imprecise_dtypes=True))

        hs_b = [sb(f"hs{n}", [P, 1024]) for n in range(2)]
        tokens4 = sb("tokens4", [P, 4 * D])
        weights = sb("weights", [P, NREG * REG])

        NA = 4
        arena = [(NREG - NA) * REG]

        def carve(*shape):
            n = int(np.prod(shape))
            piece = weights[:, arena[0]:arena[0] + n]
            arena[0] += n
            if len(shape) == 1:
                return piece
            names = " ".join(f"d{j}" for j in range(len(shape)))
            return piece.rearrange(f"p ({names}) -> p {names}", **{f"d{j}": shape[j] for j in range(len(shape))})

        wq, wk, wv, wo = (carve(KD, D) for _ in range(4))
        xt = [carve(KD, 512) for _ in range(2)]
        qt = [carve(KD, 512) for _ in range(2)]
        kts = [carve(KD, 512) for _ in range(2)]
        kbd = [carve(KD, 8, SEQ) for _ in range(2)]
        by_head = lambda a: a.rearrange("p (h t) -> p h t", h=HEADS)
        scm = [carve(HEADS, SEQ), by_head(hs_b[0][:, :])]
        prb = [carve(HEADS, SEQ), by_head(tokens4[:, :])]
        pts = carve(8, P)
        vbd = [[carve(8, 2 * DH) for _ in range(2)] for _ in range(3)]
        ots = carve(KD, P)
        sqj = carve(D)
        hmask = sb("hmask", [P, 8, 1])
        mask4 = sb("mask4", [P, SEQ // 4], U32)
        mask8 = mask4[:, :].bitcast(U8)
        mneg = sb("mneg", [P, 1, SEQ])
        valid = sb("valid", [P, 3])
        mx = sb("mx", [P, 2, HEADS])
        nmx = sb("nmx", [P, 2, HEADS])
        rsum = sb("rsum", [P, 2, HEADS])
        rinv = sb("rinv", [P, 2, HEADS])
        ssq = sb("ssq", [P, NT])
        rms = sb("rms", [P, NT])

        wq_ld = sp.dma(ld["wq"], lambda e: e.dma_start(wq[:, :, :], io["wqT"].rearrange("(c p) n -> p c n", p=P)))
        xt_ld = [sp.dma(ld[f"xt{n}"], lambda e, n=n: e.dma_start(
            xt[n][:, :, :], io["xT"][:, n * 512:(n + 1) * 512].rearrange("(c p) t -> p c t", p=P))) for n in range(2)]
        for t, n in ((wk, "wkT"), (wv, "wvT"), (wo, "woT")):
            w_ld = sp.dma(ld["wqkvo"], lambda e, t=t, n=n: e.dma_start(
                t[:, :, :], io[n].rearrange("(c p) n -> p c n", p=P)))
        sp.dma(ld["mask"], lambda e: e.dma_start(mask4[0:SEQ, :], io["mask"]))
        m_ld = sp.dma(ld["mask"], lambda e: e.dma_start(mask4[SEQ:P, :], io["mask"]))
        x_ld = sp.dma(ld["x"], lambda e: e.dma_start(x_sb[:, :, :], io["x"].rearrange("(n p) d -> p n d", p=P)))

        def small_load(dst, src):
            return sp.dma(ld["small"], lambda e: e.dma_start(dst, src))
        small_load(rw[:, :, :], io["routerT"].rearrange("(c p) n -> p c n", p=P))
        small_load(wgw[:, :, :], io["wg_W"].rearrange("(c p) n -> p c n", p=P))
        small_load(rmsw[:, :], io["rms_w"])
        small_load(normw[:, :], io["norm_w"])
        small_load(b1c[:, :, :], io["b1"])
        small_load(m1c[:, :, :], io["m1"])
        small_load(m2c[:, :, :], io["m2"])
        small_load(cond1[0:COND, :], io["condT"])
        small_load(gg1[0:COND, :], io["gg_W"])
        small_load(gg1[COND:COND + 1, :], io["gg_b"])
        small_load(gg1[COND + 1:COND + 2, :], io["wg_b"])
        small_load(ybias[:, :, :], io["b2"].rearrange("(a e) d -> a e d", a=1).to_broadcast([P, NE, D]))
        modw = carve(2 * D)[0:COND + 1, :]
        rsbc = carve(D)
        small_load(modw[0:COND, :], io["wcT"])
        small_load(modw[COND:COND + 1, :], io["bc"])
        s_ld = small_load(rsbc[:, :], io["rms_scale"].to_broadcast([P, D]))

        def region(r):
            return weights[:, r * REG:(r + 1) * REG]

        def load_l0(e_, *after):
            w = region(e_)
            sp.dma(ld["w0"], lambda e: e.dma_start(w[:, 0:2048].rearrange("p (c f) -> p c f", c=KD),
                                                   io["w1T"][e_].rearrange("(c p) f -> p c f", p=P)), *after)
            return sp.dma(ld["w0"], lambda e: e.dma_start(w[:, 2048:4096].rearrange("p (c f) -> p c f", c=F0 // P),
                                                          io["w2T"][e_].rearrange("(c p) f -> p c f", p=P)))

        for e_ in range(NREG - NA):
            load_l0(e_)

        h1 = pool.do(lambda e: e.memset(hmask[:, :, :], 1.0))
        h1 = pool.do(lambda e: e.affine_select(out=hmask[:, :, 0], in_=hmask[:, :, 0], compare_op=ALU.is_ge, fill=0.0,
                                               base=0, pattern=[[-DH, 8]], channel_multiplier=1), h1)
        hm_ok = pool.do(lambda e: e.affine_select(out=hmask[:, :, 0], in_=hmask[:, :, 0], compare_op=ALU.is_ge, fill=0.0,
                                                  base=DH - 1, pattern=[[DH, 8]], channel_multiplier=-1), h1)
        v0 = [pool.do(lambda e: e.memset(v, 0.0)) for vs in vbd for v in vs][-1]
        mk = dve.do(lambda e: e.tensor_scalar(mneg[:, 0, :], mask8, -BIG, None, ALU.mult), m_ld)
        mk1 = dve.do(lambda e: e.tensor_scalar(scm[0][:, 0, :], mask8, -1.0, 1.0, ALU.mult, ALU.add))
        mk2 = dve.do(lambda e: e.tensor_reduce(valid[:, 0:1], scm[0][:, 0, :], AX.X, ALU.max), mk1)
        mk3 = dve.do(lambda e: e.reciprocal(valid[:, 1:2], valid[:, 0:1]), mk2)
        mk4 = dve.do(lambda e: e.tensor_tensor(valid[:, 2:3], valid[:, 0:1], valid[:, 1:2], ALU.mult), mk3)

        B_S, B_T, B_O, B_W = 0, 2, 5, 6
        free = {n: [] for n in ("s", "t", "p4", "p7", "o", "w", "qk0", "qk1", "kbd", "vbd0", "vbd1", "vbd2",
                                "scm0", "scm1", "prb0", "prb1", "pts", "ots", "xt0", "xt1", "rsum0", "rsum1")}
        free["vbd0"] = free["vbd1"] = free["vbd2"] = [v0]
        free["scm0"] = [mk2]
        pb = [4, 7]
        nproj = 0

        def turns():
            nonlocal nproj
            nproj += 1
            return pb[nproj % 2]

        def project(w, src, c, after):
            b = turns()

            def emit(e):
                for k in range(KD):
                    m = e.matmul(banks[:, b, :], w[:, k, c * P:(c + 1) * P], src[:, k, :], start=(k == 0), stop=(k == KD - 1))
                return m
            return b, pe.do(emit, *after, *free[f"p{b}"])

        att_ok = {}
        v_ok, kb_ok, s_ok, e_ok, q_ok = {}, {}, {}, {}, {}
        NG = TOK // 512
        stage_qk = [(w, dst, c) for w, dst in ((wq, qt), (wk, kts)) for c in range(KD)]

        def queries_keys(g, part):
            w, dst, c = stage_qk[part]
            if part == 0 and g >= 2:
                xt_ld.append(sp.dma(ld[f"xt{g % 2}"], lambda e: e.dma_start(
                    xt[g % 2][:, :, :], io["xT"][:, g * 512:(g + 1) * 512].rearrange("(c p) t -> p c t", p=P)),
                    *free[f"xt{g % 2}"]))
            b, t = project(w, xt[g % 2], c, [wq_ld if w is wq else w_ld, xt_ld[g]])
            t = act.do(lambda e: e.copy(dst[g % 2][:, c, :], banks[:, b, :]), t, *free[f"qk{g % 2}"])
            free[f"p{b}"] = q_ok[g] = [t]

        def keys(i):
            g, tl = i // 4, (i % 4) * P
            for bb in range(2):
                t0 = tl + bb * SEQ
                for c in range(KD):
                    kb_ok[i] = dve.do(lambda e: e.tensor_tensor(
                        kbd[bb][:, c, :, :], kts[g % 2][:, c:c + 1, t0:t0 + SEQ].to_broadcast([P, 8, SEQ]),
                        hmask[:, :, :].to_broadcast([P, 8, SEQ]), ALU.mult), *q_ok[g], hm_ok, *free["kbd"])

        def values(i):
            g, tl = i // 4, (i % 4) * P
            xg, vs = xt[g % 2], vbd[i % 3]
            for bb in range(2):
                t0 = tl + bb * SEQ
                vb = turns()
                t = pe.do(lambda e: [e.matmul(banks[par * SEQ:(par + 1) * SEQ, vb, 0:P], xg[:, k, t0:t0 + SEQ],
                                              wv[:, k, par * P:(par + 1) * P], start=(k == 0), stop=(k == KD - 1))
                                     for par in range(2) for k in range(KD)][-1], w_ld, *free[f"p{vb}"])
                free[f"xt{g % 2}"] = [t]
                for par in range(2):
                    v_ok[i] = dve.do(lambda e: e.tensor_copy(
                        vs[bb][par * SEQ:(par + 1) * SEQ, :, par * DH:(par + 1) * DH],
                        banks[par * SEQ:(par + 1) * SEQ, vb, 0:P].rearrange("p (h d) -> p h d", h=8)),
                        t, *free[f"vbd{i % 3}"])
                free[f"p{vb}"] = [v_ok[i]]

        def scores(i):
            g, tl = i // 4, (i % 4) * P
            s_ok[i] = pe.do(lambda e: [e.matmul(banks[bb * SEQ:(bb + 1) * SEQ, B_S + c, :],
                                                qt[g % 2][:, c, tl + bb * SEQ:tl + (bb + 1) * SEQ],
                                                kbd[bb][:, c, :, :].rearrange("p h t -> p (h t)"), start=True, stop=True)
                                       for bb in range(2) for c in range(KD)][-1], kb_ok[i], *q_ok[g], *free["s"])
            free["kbd"] = [s_ok[i]]
            if i % 4 == 3:
                free[f"qk{g % 2}"] = [s_ok[i]]

        def exponentials(i):
            n = i % 2
            sc = banks[:, B_S:B_S + 2, :].rearrange("p a (h t) -> p (a h) t", h=8)
            t = dve.do(lambda e: e.tensor_tensor(scm[n], sc, mneg[:, :, :].to_broadcast([P, HEADS, SEQ]), ALU.add),
                       s_ok[i], mk, *free[f"scm{n}"])
            free["s"] = [t]
            t = dve.do(lambda e: e.tensor_reduce(mx[:, n, :], scm[n], AX.X, ALU.max), t)
            t = dve.do(lambda e: e.tensor_scalar(nmx[:, n, :], mx[:, n, :], -(DH ** -0.5), None, ALU.mult), t)
            for h in range(HEADS):
                t4 = act.do(lambda e: e.activation(prb[n][:, h, :], scm[n][:, h, :], ACT.Exp, bias=nmx[:, n, h:h + 1],
                                                   scale=DH ** -0.5, accum_out=rsum[:, n, h:h + 1]),
                            t, *free[f"prb{n}"], *free[f"rsum{n}"])
            free[f"scm{n}"] = [t4]
            e_ok[i] = t4

        def normalise(i):
            n = i % 2
            t = dve.do(lambda e: e.reciprocal(rinv[:, n, :], rsum[:, n, :]), e_ok[i])
            free[f"rsum{n}"] = [t]
            t = dve.do(lambda e: e.tensor_scalar(rinv[:, n, :], rinv[:, n, :], valid[:, 2:3], None, ALU.mult), t, mk4)
            t = dve.do(lambda e: e.tensor_tensor(
                prb[n], prb[n], rinv[:, n, :].rearrange("p (h o) -> p h o", o=1).to_broadcast([P, HEADS, SEQ]), ALU.mult), t)
            t = pe.do(lambda e: [e.transpose(banks[:, B_T + hp // 4, (hp % 4) * P:(hp % 4 + 1) * P],
                                             prb[n][:, 2 * hp:2 * hp + 2, :].rearrange("p h t -> p (h t)"), ident[:, :])
                                 for hp in range(8)][-1], t, c_all, *free["t"])
            free[f"prb{n}"] = [t]
            t1 = act.do(lambda e: e.copy(pts[:, 0:4, :].rearrange("p h t -> p (h t)"), banks[:, B_T, :]), t, *free["pts"])
            t2 = act.do(lambda e: e.copy(pts[:, 4:8, :].rearrange("p h t -> p (h t)"), banks[:, B_T + 1, :]))
            free["t"] = [t2]
            return t2

        def weigh_values(i, p_ok):
            t = pe.do(lambda e: [e.matmul(banks[32 * (hp % 4):32 * (hp % 4) + 32, B_O, (hp // 4) * P + bb * SEQ:(hp // 4) * P + (bb + 1) * SEQ],
                                          vbd[i % 3][bb][:, hp, :], pts[:, hp, bb * SEQ:(bb + 1) * SEQ], start=True, stop=True,
                                          tile_position=(0, 32 * (hp % 4)))
                                 for bb in range(2) for hp in range(8)][-1], p_ok, v_ok[i], *free["o"])
            free["pts"] = free[f"vbd{i % 3}"] = [t]
            t = dve.do(lambda e: e.tensor_copy(ots.rearrange("p c t -> p (c t)"), banks[:, B_O, 0:2 * P]), t, *free["ots"])
            free["o"] = [t]
            return t

        def output(i, o_ok):
            t = pe.do(lambda e: [e.matmul(banks[:, B_W, 0:D], ots[:, c, :], wo[:, c, :], start=(c == 0), stop=(c == KD - 1))
                                 for c in range(KD)][-1], o_ok, *free["w"])
            free["ots"] = [t]
            return t

        def keep_output(i, t):
            a_ok = dve.do(lambda e: e.tensor_copy(att[:, i, :], banks[:, B_W, 0:D]), t)
            free["w"] = [a_ok]
            att_ok[i] = a_ok

        for part in range(4):
            queries_keys(0, part)
        for i in range(2):
            keys(i)
            values(i)
            scores(i)
            if i == 0:
                exponentials(0)
        for part in range(3):
            queries_keys(1, part)
        p_ok = sq_ok = None
        for i in range(NT + 1):
            if i + 1 < NT:
                exponentials(i + 1)
            if i + 2 < NT:
                keys(i + 2)
            if i > 0:
                o_ok = weigh_values(i - 1, p_ok)
            if i + 2 < NT:
                values(i + 2)
            if i > 0:
                o_ok = output(i - 1, o_ok)
            if i + 2 < NT:
                scores(i + 2)
            if i < NT:
                p_ok = normalise(i)
            if i > 0:
                keep_output(i - 1, o_ok)
            if (i + 3) // 4 + 1 < NG:
                queries_keys((i + 3) // 4 + 1, (i + 3) % 4)
            if i > 0:
                sq_ok = act.do(lambda e: e.activation(sqj, att[:, i - 1, :], ACT.Square, accum_out=ssq[:, i - 1:i]),
                               att_ok[i - 1], *([sq_ok] if sq_ok else []))

        def rsqrt_cols(dst, src, eps, after):
            t = dve.do(lambda e: e.tensor_scalar(dst, src, 1.0 / D, eps, ALU.mult, ALU.add), *after)
            t = act.do(lambda e: e.activation(dst, dst, ACT.Sqrt), t)
            return dve.do(lambda e: e.reciprocal(dst, dst), t)
        r_ok = rsqrt_cols(rms[:, :], ssq[:, :], 1e-6, [sq_ok])
        silu1 = sb("silu1", [COND + 1, BATCH])
        condx = sb("condx", [COND + 2, 2, P])
        t = dve.do(lambda e: e.memset(silu1[COND:COND + 1, :], 1.0))
        one_ok = dve.do(lambda e: e.memset(cond1[COND:COND + 2, :], 1.0))
        si_ok = act.do(lambda e: e.activation(silu1[0:COND, :], cond1[0:COND, :], ACT.Silu), s_ld)

        gmod = tokens4[:, 0:2 * D].rearrange("p (n d) -> p n d", n=2)
        xnt = tokens4[:, 2 * D:].rearrange("p (n c t) -> p n c t", n=2, c=KD)
        logit = sb("logit", [P, NT, NE])
        cfree = [[], []]
        mfree, tfree, xfree = [free["s"], free["s"]], [free["t"], free["t"]], [[], []]
        att_end = [att_ok[NT - 1], free["prb0"][0], free["prb1"][0]]
        xn_ok, mod_ok = [], {}

        def modulation(i):
            n = i % 2
            ce = act.do(lambda e: e.copy(
                condx[0:COND + 1, n, :].rearrange("p (b s) -> p b s", b=2),
                silu1[:, 2 * i:2 * i + 2].rearrange("p (b s) -> p b s", s=1).to_broadcast([COND + 1, 2, SEQ])),
                si_ok, one_ok, *cfree[n])
            mod_ok[i] = pe.do(lambda e: e.matmul(banks[:, n, :], condx[0:COND + 1, n, :], modw[:, :], start=True, stop=True),
                              ce, s_ld, *mfree[n])
            cfree[n] = [mod_ok[i]]

        def logits(i, after):
            t = pe.do(lambda e: [e.matmul(banks[:, 4, i * NE:(i + 1) * NE], xnt[:, i % 2, c, :], rw[:, c, :],
                                          start=(c == 0), stop=(c == KD - 1)) for c in range(KD)][-1], after, *free["p4"])
            xfree[i % 2] = [t]
            return t

        modulation(0)
        for i in range(NT):
            n = i % 2
            if i + 1 < NT:
                modulation(i + 1)
            t1 = dve.do(lambda e: e.scalar_tensor_tensor(gmod[:, n, :], banks[:, n, D:2 * D], 1.0, rsbc[:, :], ALU.add, ALU.mult),
                        mod_ok[i], *att_end)
            t1 = dve.do(lambda e: e.scalar_tensor_tensor(att[:, i, :], att[:, i, :], rms[:, i:i + 1], gmod[:, n, :],
                                                         ALU.mult, ALU.mult), t1, r_ok)
            t1 = dve.do(lambda e: e.tensor_tensor(att[:, i, :], att[:, i, :], banks[:, n, 0:D], ALU.add), t1)
            mfree[n] = [t1]
            xn_ok.append(t1)
            t1 = pe.do(lambda e: [e.transpose(banks[:, 2 + n, c * P:(c + 1) * P], att[:, i, c * P:(c + 1) * P], ident[:, :])
                                  for c in range(KD)][-1], t1, *tfree[n])
            t1 = act.do(lambda e: e.copy(xnt[:, n, :, :].rearrange("p c t -> p (c t)"), banks[:, 2 + n, 0:2 * P]), t1, *xfree[n])
            tfree[n] = [t1]
            if i > 0:
                l_ok = logits(i - 1, xt_ok)
            xt_ok = t1
        l_ok = logits(NT - 1, xt_ok)
        t = dve.do(lambda e: e.tensor_copy(logit[:, :, :].rearrange("p a b -> p (a b)"), banks[:, 4, 0:NT * NE]), l_ok)
        for i in range(0, NT, 4):
            rows_ld = sp.dma(ld["rows"], lambda e: e.dma_start(
                rows_in[i * P:(i + 4) * P, :].rearrange("(n p) d -> p n d", p=P), att[:, i:i + 4, :]), xn_ok[i + 3])
        a_end = [sq_ok, xn_ok[-1], l_ok]
        for e_ in range(NREG - NA, NE):
            w0_ld = load_l0(e_, *a_end)


        onehot = sb("onehot", [P, TOPK, NT, NE])
        both = sb("both", [P, NT, NE])
        before = sb("before", [P, NT, NE])
        top8 = sb("top8", [P, NT, 8])
        idx8 = sb("idx8", [P, NT, 8], U32)
        ntile = sb("ntile", [P, NE])
        upto_e = sb("upto_e", [P, NE])
        base_e = sb("base_e", [P, NE])
        thr = sb("thr", [P, NE, 16])
        sums = sb("sums", [P, NT, NE])
        slot_r = sb("slot_r", [P, TOPK, NT])
        slot_t = sb("slot_t", [P, TOPK, NT])
        slot_f = sb("slot_f", [P, TOPK, NT])
        te = sb("te", [P, GT, NE])
        te_f = sb("te_f", [P, GT])

        ht_b = [sb(f"ht{n}", [P, 1024]) for n in range(2)]
        rows_hot = [hs_b[k][:, :].bitcast(BF16).rearrange("p (i j) -> p i j", j=P) for k in range(TOPK)]
        tiles_hot = [ht_b[k][:, 0:3 * NT * GT // 2].bitcast(BF16).rearrange("p (m i j) -> p m i j", m=3, j=GT) for k in range(TOPK)]

        def route(score, *after):
            t = [dve.do(lambda e: e.max(top8[:, i, :], score[:, i, :]), *after) for i in range(NT)]
            t_i = [dve.do(lambda e: e.max_index(idx8[:, i, :], top8[:, i, :], score[:, i, :]), t[i]) for i in range(NT)][-1]
            for k in range(TOPK):
                t = dve.do(lambda e: e.tensor_tensor(onehot[:, k, :, :], iota8[:, :, :],
                                                     idx8[:, :, k:k + 1].to_broadcast([P, NT, NE]), ALU.is_equal), t_i, c_all)
            t = dve.do(lambda e: e.tensor_tensor(both[:, :, :], onehot[:, 0, :, :], onehot[:, 1, :, :], ALU.add), t)
            src = both[:, :, :]
            for m, dst in zip((1, 2, 4, 8), (before[:, :, :], sums[:, :, :]) * 2):
                dve.do(lambda e: e.tensor_copy(dst[:, 0:m, :], src[:, 0:m, :]), t)
                t = dve.do(lambda e: e.tensor_tensor(dst[:, m:, :], src[:, m:, :], src[:, 0:NT - m, :], ALU.add), t)
                src = dst
            t = dve.do(lambda e: e.tensor_tensor(before[:, :, :], sums[:, :, :], both[:, :, :], ALU.subtract), t)
            n_ok = pe.do(lambda e: e.matmul(banks[:, 5, 0:NE], ones[:, :], sums[:, NT - 1, :], start=True, stop=True), t, *after)
            p_ok = pe.do(lambda e: (e.matmul(banks[:, 4, 0:NT * NE], lower[:, :], both[:, :, :].rearrange("p a b -> p (a b)"), start=True, stop=False),
                                    e.matmul(banks[:, 4, 0:NT * NE], ones[:, :], before[:, :, :].rearrange("p a b -> p (a b)"), start=False, stop=True),
                                    )[-1])
            t = dve.do(lambda e: e.tensor_tensor(thr[:, :, :], banks[:, 5, 0:NE].rearrange("p (a o) -> p a o", o=1).to_broadcast([P, NE, 16]),
                                                 iota16[:, :, :], ALU.is_gt), n_ok)
            t = dve.do(lambda e: e.tensor_reduce(ntile[:, :], thr[:, :, :], AX.X, ALU.add), t)
            src = ntile[:, :]
            for m, dst in zip((1, 2, 4), (upto_e[:, :], base_e[:, :], upto_e[:, :])):
                dve.do(lambda e: e.tensor_copy(dst[:, 0:m], src[:, 0:m]), t)
                t = dve.do(lambda e: e.tensor_tensor(dst[:, m:], src[:, m:], src[:, 0:NE - m], ALU.add), t)
                src = dst
            t1 = dve.do(lambda e: e.tensor_tensor(base_e[:, :], upto_e[:, :], ntile[:, :], ALU.subtract), t)
            t = dve.do(lambda e: e.tensor_tensor(te[:, :, :], iotag[:, :, :],
                                                 upto_e[:, :].rearrange("p (o a) -> p o a", o=1).to_broadcast([P, GT, NE]), ALU.is_ge), t)
            t2 = dve.do(lambda e: e.scalar_tensor_tensor(sums[:, :, :], base_e[:, :].rearrange("p (o a) -> p o a", o=1).to_broadcast([P, NT, NE]),
                                                         float(P), banks[:, 4, 0:NT * NE].rearrange("p (n k) -> p n k", k=NE),
                                                         ALU.mult, ALU.add), t1, p_ok)
            t = dve.do(lambda e: e.tensor_reduce(te_f[:, :], te[:, :, :], AX.X, ALU.add), t)
            for k in range(TOPK):
                t2 = dve.do(lambda e: e.tensor_tensor(onehot[:, k, :, :], onehot[:, k, :, :], sums[:, :, :], ALU.mult), t2)
            te_ok = dve.do(lambda e: e.tensor_scalar(tile_e[:, :], te_f[:, :], float(NE - 1), None, ALU.min), t)
            t = dve.do(lambda e: e.tensor_reduce(slot_f[:, :, :], onehot[:, :, :, :], AX.X, ALU.add), t2)
            slot_ok = dve.do(lambda e: e.tensor_copy(slots[:, :, :], slot_f[:, :, :]), t)
            t = dve.do(lambda e: e.tensor_scalar(slot_t[:, :, :], slot_f[:, :, :], 1.0 / P, 0.5 / P - 0.5, ALU.mult, ALU.add), t)
            t = dve.do(lambda e: e.tensor_scalar(slot_t[:, :, :], slot_t[:, :, :], ROUND, None, ALU.add), t)
            t = dve.do(lambda e: e.tensor_scalar(slot_t[:, :, :], slot_t[:, :, :], -ROUND, None, ALU.add), t)
            t = dve.do(lambda e: e.scalar_tensor_tensor(slot_r[:, :, :], slot_t[:, :, :], -float(P), slot_f[:, :, :], ALU.mult, ALU.add), t)
            for k in range(TOPK):
                rows, tiles = rows_hot[k], tiles_hot[k]
                by_tile = lambda a: a.rearrange("p (i o) -> p i o", o=1).to_broadcast([P, NT, GT])
                t = dve.do(lambda e: e.tensor_tensor(tiles[:, 0, :, :], iotag[:, :, 0].rearrange("p (o j) -> p o j", o=1).to_broadcast([P, NT, GT]),
                                                     by_tile(slot_t[:, k, :]), ALU.is_equal), t, *after)
                t1 = dve.do(lambda e: e.tensor_tensor(rows, iotap[:, :].rearrange("p (o j) -> p o j", o=1).to_broadcast([P, NT, P]),
                                                      slot_r[:, k, :].rearrange("p (i o) -> p i o", o=1).to_broadcast([P, NT, P]), ALU.is_equal))
                dve.do(lambda e: e.tensor_scalar(tiles[:, 1, :, :], tiles[:, 0, :, :], token_p[:, 0:1], None, ALU.mult), t)
                t = dve.do(lambda e: e.tensor_tensor(tiles[:, 2, :, :], tiles[:, 0, :, :], by_tile(token_t[:, :]), ALU.mult))
                i_ok = pe.do(lambda e: [e.matmul(banks[:, 6, 0:GT], rows[:, i, :], tiles[:, part, i, :],
                                                 start=(k == 0 and i == 0 and part == 1), stop=(k == 1 and i == NT - 1 and part == 2))
                                        for i in range(NT) for part in (1, 2)][-1], t)
            inv_ok = dve.do(lambda e: e.tensor_copy(inverse[:, :], banks[:, 6, 0:GT]), i_ok)
            return slot_ok, te_ok, inv_ok

        def gather_mix(use, mixb, *after):
            done = []
            mix_free = [[] for _ in mixb]
            for i in range(NT):
                ns = [(i * TOPK + k) % 8 for k in range(TOPK)]
                ok = [pool.dma(ld[f"mix{n}"], lambda e: e.indirect_dma_start(
                    mixb[n], None, rows_out[:, :], bass.IndirectOffsetOnAxis(ap=slots[:, k, i:i + 1], axis=0)),
                    *after, *mix_free[n]) for k, n in enumerate(ns)]
                t = use(i, mixb[ns[0]], mixb[ns[1]], *ok)
                for n in ns:
                    mix_free[n] = [t]
                done.append(t)
            return done

        xg_b = [sb(f"xg{n}", [P, D]) for n in range(3)]
        ys_b = [sb(f"ys{n}", [P, D]) for n in range(2)]
        xgt_b = [xnt[:, n, :, :] for n in range(2)]
        bcol = sb("bcol", [P, 2, 8])
        mixb = [hs_b[n // 4][:, (n % 4) * D:(n % 4 + 1) * D] for n in range(8)]
        B_X, B_H, B_T2, B_Y = 0, 1, 3, 5

        early_l1 = []

        def expert_of(lane, j, te_ok):
            lane.wait(te_ok)
            return lane.eng.value_load(tile_e[0:1, j:j + 1], min_val=0, max_val=NE - 1)

        def load_l1(r, *after):
            w = region(r)
            sp.dma(ld["w1"], lambda e: e.dma_start(w[:, 0:1024].rearrange("p (c f) -> p c f", c=KD),
                                                   io["W1"][r].rearrange("(c p) f -> p c f", p=P)), *after)
            sp.dma(ld["w1"], lambda e: e.dma_start(w[:, 1024:3072].rearrange("p (c f) -> p c f", c=M1 // P),
                                                   io["W2"][r].rearrange("(c p) f -> p c f", p=P)))
            return sp.dma(ld["w1"], lambda e: e.dma_start(w[:, 3072:4096].rearrange("p (c f) -> p c f", c=M1 // P),
                                                          io["W3"][r].rearrange("(c p) f -> p c f", p=P)))

        def expert_layer0(rows_ok, te_ok, w_ok, bank_free):
            xfree_, xtfree, hsfree, htfree, ysfree = [[], [], []], [[], []], [[], []], [[], []], [[], []]
            bfree = {b: list(bank_free) for b in range(8)}
            xt_ok, x_ok = {}, {}
            bcfree = [[], []]

            def fetch(j):
                n = j % 3
                if j < GT:
                    x_ok[j] = pool.dma(ld[f"xg{n}"], lambda e: e.indirect_dma_start(
                        xg_b[n][:, :], None, rows_in[:, :], bass.IndirectOffsetOnAxis(ap=inverse[:, j:j + 1], axis=0)),
                        *rows_ok, *xfree_[n])

            def inputs(j):
                n = j % 3
                t = pe.do(lambda e: [e.transpose(banks[:, B_X, c * P:(c + 1) * P], xg_b[n][:, c * P:(c + 1) * P], ident[:, :])
                                     for c in range(KD)][-1], x_ok[j], *bfree[B_X])
                xfree_[n] = [t]
                t = dve.do(lambda e: e.tensor_copy(xgt_b[j % 2].rearrange("p c t -> p (c t)"), banks[:, B_X, 0:D]),
                           t, *xtfree[j % 2])
                bfree[B_X] = [t]
                xt_ok[j] = t

            def outputs(j, h_ok, rd):
                by = B_Y + j % 2
                w2 = 2048
                t = pe.do(lambda e: [e.matmul(banks[:, by, 0:D], ht_b[j % 2][:, c * P:(c + 1) * P],
                                              weights[:, bass.ds(rd * REG + w2 + c * D, D)],
                                              start=(c == 0), stop=(c == F0 // P - 1)) for c in range(F0 // P)][-1],
                          h_ok, *bfree[by])
                htfree[j % 2] = [t]
                rv = expert_of(dve, j, te_ok)
                t = dve.do(lambda e: e.tensor_tensor(ys_b[j % 2][:, :], banks[:, by, 0:D],
                                                     ybias_f[:, bass.ds(rv * D, D)], ALU.add), t, *ysfree[j % 2])
                bfree[by] = [t]
                t = sp.dma(ld[f"ys{j % 2}"], lambda e: e.dma_start(rows_out[j * P:(j + 1) * P, :], ys_b[j % 2][:, :]), t)
                ysfree[j % 2] = [t]
                return t

            fetch(0)
            fetch(1)
            inputs(0)
            pending, ends = None, []
            for j in range(GT):
                n = j % 2
                fetch(j + 2)
                rd = expert_of(pe, j, te_ok)

                def emit(e):
                    for half in range(2):
                        for k in range(KD):
                            m = e.matmul(banks[:, B_H + half, :], xgt_b[n][:, k, :],
                                         weights[:, bass.ds(rd * REG + k * F0 + half * 512, 512)],
                                         start=(k == 0), stop=(k == KD - 1))
                    return m
                t = pe.do(emit, xt_ok[j], *w_ok, *bfree[B_H], *bfree[B_H + 1])
                xtfree[n] = [t]
                t1 = dve.do(lambda e: e.tensor_copy(hs_b[n][:, 0:512], banks[:, B_H, :]), t, *hsfree[n])
                t2 = act.do(lambda e: e.copy(hs_b[n][:, 512:1024], banks[:, B_H + 1, :]), t, *hsfree[n])
                bfree[B_H], bfree[B_H + 1] = [t1], [t2]
                if pending:
                    ends.append(outputs(*pending))
                if j % NT == 0 and j:
                    early_l1.append(j // NT - 1)
                    load_l1(early_l1[-1], *htfree[(j - 1) % 2])
                if j + 1 < GT:
                    inputs(j + 1)
                t = pe.do(lambda e: [e.transpose(banks[:, B_T2 + c // 4, (c % 4) * P:(c % 4 + 1) * P],
                                                 hs_b[n][:, c * P:(c + 1) * P], ident[:, :]) for c in range(8)][-1],
                          t1, t2, *bfree[B_T2], *bfree[B_T2 + 1])
                hsfree[n] = [t]
                rv = expert_of(dve, j, te_ok)
                bc = dve.do(lambda e: e.tensor_copy(bcol[:, n, :], b1f[:, bass.ds(rv * 8, 8)]), *bcfree[n])
                for c in range(8):
                    h_ok = act.do(lambda e: e.activation(ht_b[n][:, c * P:(c + 1) * P],
                                                         banks[:, B_T2 + c // 4, (c % 4) * P:(c % 4 + 1) * P],
                                                         ACT.Gelu, bias=bcol[:, n, c:c + 1]), t, bc, *htfree[n])
                bcfree[n] = [h_ok]
                bfree[B_T2] = bfree[B_T2 + 1] = [h_ok]
                pending = (j, h_ok, rd)
            ends.append(outputs(*pending))
            return ends[-2:], [h_ok, bfree[B_Y + (GT - 1) % 2][0], bfree[B_Y + GT % 2][0]]

        ybias_f = ybias[:, :, :].rearrange("p e d -> p (e d)")
        b1f = b1c[:, :, :].rearrange("p e c -> p (e c)")

        slot_ok, te_ok, inv_ok = route(logit, t, *a_end)
        g1 = dve.do(lambda e: e.tensor_tensor(slot_f[:, 0, :], top8[:, :, 1], top8[:, :, 0], ALU.subtract), slot_ok)
        g2 = act.do(lambda e: e.activation(slot_f[:, 1, :], slot_f[:, 0, :], ACT.Exp), g1)
        g3 = dve.do(lambda e: e.tensor_scalar(slot_f[:, 0, :], slot_f[:, 1, :], 1.0, None, ALU.add), g2)
        g4 = dve.do(lambda e: e.reciprocal(gate[:, :, 0], slot_f[:, 0, :]), g3)
        gate_ok = dve.do(lambda e: e.tensor_tensor(gate[:, :, 1], gate[:, :, 0], slot_f[:, 1, :], ALU.mult), g4)
        ends, drained = expert_layer0([rows_ld, inv_ok], te_ok, [w0_ld], [t, inv_ok])

        wgr = sb("wgr", [P, KD, NE])
        for c in range(KD):
            wg_ok = dve.do(lambda e: e.tensor_scalar(wgr[:, c, :], wgw[:, c, :], rmsw[:, c:c + 1], None, ALU.mult), s_ld)

        def mix0(i, y0, y1, ok0, ok1):
            if i % 4 == 2:
                early_l1.append(len(early_l1))
                load_l1(early_l1[-1], ok1, *drained)
            t = dve.do(lambda e: e.scalar_tensor_tensor(x_sb[:, i, :], y0, gate[:, i, 0:1], x_sb[:, i, :], ALU.mult, ALU.add),
                       ok0, gate_ok, x_ld)
            return dve.do(lambda e: e.scalar_tensor_tensor(x_sb[:, i, :], y1, gate[:, i, 1:2], x_sb[:, i, :], ALU.mult, ALU.add),
                          t, ok1)
        x1_ok = gather_mix(mix0, mixb, *ends, *drained)

        for i in range(0, NT, 4):
            rows_ld = sp.dma(ld["rows"], lambda e: e.dma_start(
                rows_in[i * P:(i + 4) * P, :].rearrange("(n p) d -> p n d", p=P), x_sb[:, i:i + 4, :]), *drained, x1_ok[i + 3])
        for r_ in range(len(early_l1), NE):
            w1_ld = load_l1(r_, *drained)
        yb_ld = sp.dma(ld["bias"], lambda e: e.dma_start(
            ybias[:, :, :], io["m3"].rearrange("(a e) d -> a e d", a=1).to_broadcast([P, NE, D])))

        score = logit

        def gate_logits(i, after):
            t = pe.do(lambda e: [e.matmul(banks[:, 4, i * NE:(i + 1) * NE], xnt[:, i % 2, c, :], wgr[:, c, :],
                                          start=(c == 0), stop=(c == KD - 1)) for c in range(KD)][-1], after, wg_ok)
            xfree[i % 2] = [t]
            return t
        smx = sb("smx", [P, NT])
        for i in range(NT):
            n = i % 2
            sq_ok = act.do(lambda e: e.activation(ys_b[n][:, :], x_sb[:, i, :], ACT.Square, accum_out=ssq[:, i:i + 1]), x1_ok[i], *ends)
            ce = act.do(lambda e: e.copy(
                condx[:, n, :].rearrange("p (b s) -> p b s", b=2),
                cond1[:, 2 * i:2 * i + 2].rearrange("p (b s) -> p b s", s=1).to_broadcast([COND + 2, 2, SEQ])),
                *cfree[n])
            cg_ok = pe.do(lambda e: e.matmul(banks[:, 5, i * NE:(i + 1) * NE], condx[:, n, :], gg1[:, :], start=True, stop=True),
                          ce, *drained)
            cfree[n] = [cg_ok]
            t1 = pe.do(lambda e: [e.transpose(banks[:, 2 + n, c * P:(c + 1) * P], x_sb[:, i, c * P:(c + 1) * P], ident[:, :])
                                  for c in range(KD)][-1], x1_ok[i], *tfree[n])
            t1 = act.do(lambda e: e.copy(xnt[:, n, :, :].rearrange("p c t -> p (c t)"), banks[:, 2 + n, 0:2 * P]), t1, *xfree[n])
            tfree[n] = [t1]
            if i > 0:
                l_ok = gate_logits(i - 1, turned_ok)
            turned_ok = t1
        l_ok = gate_logits(NT - 1, turned_ok)
        r_ok = rsqrt_cols(rms[:, :], ssq[:, :], 1e-6, [sq_ok])
        rows8 = lambda a: a.rearrange("p (n o) -> p n o", o=1).to_broadcast([P, NT, NE])
        t = dve.do(lambda e: e.tensor_tensor(score[:, :, :], banks[:, 4, 0:NT * NE].rearrange("p (n k) -> p n k", k=NE),
                                             rows8(rms[:, :]), ALU.mult), r_ok, l_ok)
        t = dve.do(lambda e: e.tensor_tensor(score[:, :, :], score[:, :, :], banks[:, 5, 0:NT * NE].rearrange("p (n k) -> p n k", k=NE),
                                             ALU.add), t, cg_ok)
        t = dve.do(lambda e: e.tensor_reduce(smx[:, :], score[:, :, :], AX.X, ALU.max), t)
        t = dve.do(lambda e: e.tensor_tensor(score[:, :, :], score[:, :, :], rows8(smx[:, :]), ALU.subtract), t)
        t = act.do(lambda e: e.activation(score[:, :, :], score[:, :, :], ACT.Exp), t)
        t = dve.do(lambda e: e.tensor_reduce(smx[:, :], score[:, :, :], AX.X, ALU.add), t)
        t = dve.do(lambda e: e.reciprocal(smx[:, :], smx[:, :]), t)
        t = dve.do(lambda e: e.tensor_tensor(score[:, :, :], score[:, :, :], rows8(smx[:, :]), ALU.mult), t)
        slot_ok, te_ok, inv_ok = route(score, t, *drained)
        gate_ok = dve.do(lambda e: e.tensor_copy(gate[:, :, :], top8[:, :, 0:TOPK]), slot_ok)

        m1f = m1c[:, :, :].rearrange("p e c -> p (e c)")
        m2f = m2c[:, :, :].rearrange("p e c -> p (e c)")

        def expert_layer1(rows_ok, te_ok, w_ok, bank_free, first_two_free):
            A_X, A_H1, A_H2, A_T1, A_T2, A_Y = 0, 1, 2, 3, 4, 5
            bfree = {b: list(bank_free) for b in range(8)}
            fr = {(n, k): [] for n in ("xg", "xgt", "h1", "h2", "t1", "t2", "bc", "ys") for k in range(3)}
            ok, rd, ends = {}, {}, []

            def fetch(j):
                n = j % 3
                if j < GT:
                    ok["load", j] = pool.dma(ld[f"xg{n}"], lambda e: e.indirect_dma_start(
                        xg_b[n][:, :], None, rows_in[:, :], bass.IndirectOffsetOnAxis(ap=inverse[:, j:j + 1], axis=0)),
                        *rows_ok, *fr["xg", n])

            def inputs(j):
                n = j % 3
                t = pe.do(lambda e: [e.transpose(banks[:, A_X, c * P:(c + 1) * P], xg_b[n][:, c * P:(c + 1) * P], ident[:, :])
                                     for c in range(KD)][-1], ok["load", j], *bfree[A_X])
                fr["xg", n] = [t]
                t = dve.do(lambda e: e.tensor_copy(xgt_b[j % 2].rearrange("p c t -> p (c t)"), banks[:, A_X, 0:D]),
                           t, *fr["xgt", j % 2])
                bfree[A_X] = [t]
                ok["x", j] = t

            def hidden(j, bank, src, chunks, offset):
                return pe.do(lambda e: [e.matmul(banks[:, bank, :], src(c), weights[:, bass.ds(rd[j] * REG + offset + c * M1, M1)],
                                                 start=(c == 0), stop=(c == chunks - 1)) for c in range(chunks)][-1],
                             ok["x" if offset == 0 else "t1", j], *w_ok, *bfree[bank])

            def turned(j, bank, src, after):
                return pe.do(lambda e: [e.transpose(banks[:, bank, c * P:(c + 1) * P], src[:, c * P:(c + 1) * P], ident[:, :])
                                        for c in range(M1 // P)][-1], after, *bfree[bank])

            fetch(0)
            fetch(1)
            inputs(0)
            for j in range(GT + 2):
                fetch(j + 2)
                if j < GT:
                    n = j % 2
                    rd[j] = expert_of(pe, j, te_ok)
                    t = hidden(j, A_H1, lambda c: xgt_b[n][:, c, :], KD, 0)
                    fr["xgt", n] = [t]
                    h1 = dve.do(lambda e: e.tensor_copy(hs_b[n][:, 0:M1], banks[:, A_H1, :]), t, *fr["h1", n])
                    bfree[A_H1] = [h1]
                    rv = expert_of(dve, j, te_ok)
                    dve.do(lambda e: e.tensor_copy(bcol[:, n, 0:4], m1f[:, bass.ds(rv * 4, 4)]), *fr["bc", n])
                    bc = dve.do(lambda e: e.tensor_copy(bcol[:, n, 4:8], m2f[:, bass.ds(rv * 4, 4)]))
                    if j + 1 < GT:
                        inputs(j + 1)
                if 1 <= j <= GT:
                    q, m = j - 1, (j - 1) % 2
                    t = hidden(q, A_H2, lambda c: ht_b[m][:, c * P:(c + 1) * P], M1 // P, 1024)
                    fr["t1", m] = [t]
                    h2 = act.do(lambda e: e.copy(hs_b[m][:, M1:], banks[:, A_H2, :]), t, *fr["h2", m])
                    bfree[A_H2] = [h2]
                if j < GT:
                    t = turned(j, A_T1, hs_b[n][:, 0:M1], h1)
                    fr["h1", n] = [t]
                    for c in range(4):
                        t1 = act.do(lambda e: e.activation(ht_b[n][:, c * P:(c + 1) * P], banks[:, A_T1, c * P:(c + 1) * P],
                                                           ACT.Relu, bias=bcol[:, n, c:c + 1]), t, bc, *fr["t1", n])
                    bfree[A_T1], ok["t1", j] = [t1], t1
                if 2 <= j:
                    q2, m2 = j - 2, (j - 2) % 2
                    by = A_Y + q2 % 2
                    t = pe.do(lambda e: [e.matmul(banks[:, by, 0:D], ht_b[m2][:, M1 + c * P:M1 + (c + 1) * P],
                                                  weights[:, bass.ds(rd[q2] * REG + 3072 + c * D, D)],
                                                  start=(c == 0), stop=(c == M1 // P - 1)) for c in range(M1 // P)][-1],
                              ok["t2", q2], *bfree[by])
                    fr["t2", m2] = [t]
                    if q2 == 2 * NT - 1:
                        first_two_free(t)
                    rv = expert_of(dve, q2, te_ok)
                    t = dve.do(lambda e: e.tensor_tensor(ys_b[m2][:, :], banks[:, by, 0:D],
                                                         ybias_f[:, bass.ds(rv * D, D)], ALU.add), t, yb_ld, *fr["ys", m2])
                    bfree[by] = [t]
                    t = sp.dma(ld[f"ys{m2}"], lambda e: e.dma_start(rows_out[q2 * P:(q2 + 1) * P, :], ys_b[m2][:, :]), t)
                    fr["ys", m2] = [t]
                    ends.append(t)
                if 1 <= j <= GT:
                    t = turned(q, A_T2, hs_b[m][:, M1:], h2)
                    fr["h2", m] = [t]
                    for c in range(4):
                        t2 = dve.do(lambda e: e.tensor_scalar(ht_b[m][:, M1 + c * P:M1 + (c + 1) * P], banks[:, A_T2, c * P:(c + 1) * P],
                                                              bcol[:, m, 4 + c:5 + c], 0.0, ALU.add, ALU.max), t, *fr["t2", m])
                    bfree[A_T2], ok["t2", q] = [t2], t2
                    fr["bc", m] = [ok["t1", q], t2]
            return ends[-2:], [t2, ok["t1", GT - 1], bfree[A_Y][0], bfree[A_Y + 1][0], fr["t2", 0][0], fr["t2", 1][0]]

        NC, G2, SUB = PE_N // P, 2 * P, 16
        arena[0] = 0
        hid = carve(NC, G2)
        hidf = hid.rearrange("p c t -> p (c t)")
        wqp = hidf[:, 0:4096].rearrange("p (g n) -> p g n", g=2 * PH)
        keyp = hidf[:, 4096:5120].rearrange("p (g n) -> p g n", g=2 * PH)
        key_ld = []

        def load_keys(*after):
            sp.dma(ld["w0"], lambda e: e.dma_start(wqp, io["wqp"]), *after)
            key_ld.append(sp.dma(ld["w0"], lambda e: e.dma_start(keyp, io["keysT"])))

        ends, drained = expert_layer1([rows_ld, inv_ok], te_ok, [w1_ld], [t, inv_ok, gate_ok], load_keys)

        downT = carve(KD, PE_N)
        up_sb = carve(NC, D)
        wkey = carve(KD, 2 * PH * PKEYS)
        xnT = carve(KD, TOK)
        iotax = carve(P * SUB // 2).bitcast(BF16).rearrange("p (a t) -> p a t", t=SUB)
        attf = att[:, :, :].rearrange("p n d -> p (n d)")
        lo_b, hi_b, hw_b = [], [], []
        for n in range(2):
            o = n * 2048
            lo_b.append(attf[:, o:o + 1024].bitcast(BF16).rearrange("p (a t) -> p a t", t=SUB))
            hi_b.append(attf[:, o + 1024:o + 1280].bitcast(BF16).rearrange("p (a t) -> p a t", t=SUB))
            hw_b.append(attf[:, o + 1280:o + 2048].bitcast(BF16).rearrange("p (m a t) -> p m a t", m=3, t=SUB))
        sims, rest = [ht_b[0][:, :], tokens4[:, :]], ht_b[1][:, :]
        scr = [hs_b[0][:, :], hs_b[1][:, :]]
        top = scr[0][:, 0:256]
        topi = scr[0][:, 256:512].bitcast(U32)
        w16 = scr[0][:, 512:640]
        j16 = scr[0][:, 640:768].bitcast(U32)
        packs = scr[1][:, 0:384]
        cand = ybias_f[:, 0:432].rearrange("p (h j) -> p h j", h=PH)
        cand2 = ybias_f[:, 432:864].rearrange("p (h j) -> p h j", h=PH)
        lk = ybias_f[:, 864:2048].bitcast(BF16)
        edges = [thr[:, :, :].rearrange("p e m -> p (e m)").bitcast(BF16), xg_b[1][:, P * 3 // 2:D].bitcast(BF16)]
        ta, tm, td = (a.rearrange("p (m h) -> p m h", h=PH) for a in (edges[0][:, 0:P], edges[0][:, P:2 * P], edges[1]))
        di = scr[1][:, 384:512].bitcast(BF16).rearrange("p (s m h) -> p s m h", s=2, m=16)
        key_f = scr[1][:, 512:768]
        cmp_b = carve(16 * P // 2).bitcast(BF16).rearrange("p (m n) -> p m n", m=16)
        prod = lk[:, 0:2048].rearrange("p (m n) -> p m n", m=16)
        prod2 = rest.bitcast(BF16).rearrange("p (m n) -> p m n", m=16)
        jh = lk[:, 2048:2176]
        bh = lk[:, 2176:2304]
        i1h = scr[1][:, 768:832].bitcast(BF16)
        i2h = scr[1][:, 832:896].bitcast(BF16)
        q_h = scr[1][:, 896:960].bitcast(BF16)
        turn = [xg_b[0][:, n * P:(n + 1) * P].bitcast(BF16).rearrange("p (a n) -> p a n", a=2) for n in range(2)]
        wpart = [xg_b[1 + n][:, 0:P * 3 // 2].bitcast(BF16).rearrange("p (a n) -> p a n", a=3) for n in range(2)]
        wres = rest[:, 512:768].rearrange("p (a n) -> p a n", a=2)
        sum8 = ybias_f[:, 0:512].bitcast(BF16).rearrange("p (m n) -> p m n", m=8)

        blocks = [(0, 1, 16), (1, 1, 8), (2, 2, 5), (4, 4, 3), (8, 8, 1)]
        first = [0] * 17
        for a0, na, nb in blocks:
            for a in range(a0, a0 + na):
                first[a + 1] = first[a] + nb
        kc = [dve.do(lambda e: e.memset(t_[:, m, :], v), *drained) for m in range(16)
              for t_, v in ((ta, float(first[m])), (tm, float(m)), (td, float(first[m] - first[m - 1]) if m else 0.0))]

        for c in range(KD):
            for half in range(2):
                b = 2 * c + half
                t = pe.do(lambda e: [e.matmul(banks[:, b, g * PKEYS:(g + 1) * PKEYS], wqp[:, half * 8 + g, c * P:(c + 1) * P],
                                              keyp[:, half * 8 + g, :], start=True, stop=True) for g in range(8)][-1], key_ld[0], *drained)
                wk_ok = act.do(lambda e: e.copy(wkey[:, c, half * 512:(half + 1) * 512], banks[:, b, :]), t)

        B_SIM, B_HID, B_G, B_OUT, B_TR = 0, 1, 3, 5, 7
        pf = {b: [wk_ok] for b in range(8)}
        sf = {"sims0": [wk_ok], "sims1": [wk_ok], "packs": [], "sums": [], "turn": [], "hid": [wk_ok]}
        s_ok, kept, w_ok, picked = {}, {}, {}, {}

        def similar(i, halves=(0, 1)):
            for half in halves:
                t = pe.do(lambda e: [e.matmul(banks[:, B_SIM, :], xnT[:, c, i * P:(i + 1) * P], wkey[:, c, half * 512:(half + 1) * 512],
                                              start=(c == 0), stop=(c == KD - 1)) for c in range(KD)][-1], xn_ok[i], *pf[B_SIM])
                s_ok[i] = act.do(lambda e: e.copy(sims[i % 2][:, half * 512:(half + 1) * 512], banks[:, B_SIM, :]),
                                 t, *sf[f"sims{i % 2}"])
                pf[B_SIM] = [s_ok[i]]

        def select(i):

            def top16(vals, idxs, src, spare_, *after):
                n = src.shape[1]
                a = [dve.do(lambda e: e.max(vals(g)[:, 0:8], src[:, g, :]), *after) for g in range(n)]
                yield
                b = [dve.do(lambda e: e.max_index(idxs(g)[:, 0:8], vals(g)[:, 0:8], src[:, g, :]), a[g]) for g in range(n)]
                yield
                b = [dve.do(lambda e: e.match_replace(spare_[:, g, :], vals(g)[:, 0:8], src[:, g, :], -3e38), a[g]) for g in range(n)]
                yield
                a = [dve.do(lambda e: e.max(vals(g)[:, 8:16], spare_[:, g, :]), b[g]) for g in range(n)]
                yield
                b = [dve.do(lambda e: e.max_index(idxs(g)[:, 8:16], vals(g)[:, 8:16], spare_[:, g, :]), a[g]) for g in range(n)]
                yield
                return b[-1]

            s3 = sims[i % 2].rearrange("p (g k) -> p g k", k=PKEYS)
            t = yield from top16(lambda g: top[:, g * 16:(g + 1) * 16], lambda g: topi[:, g * 16:(g + 1) * 16], s3,
                      rest.rearrange("p (g k) -> p g k", k=PKEYS), s_ok[i])
            sf[f"sims{i % 2}"] = [t]
            tp = top.rearrange("p (h s r) -> p h s r", h=PH, s=2)
            for a0, na, nb in blocks:
                sh = [P, PH, na, nb]
                c_ok = dve.do(lambda e: e.tensor_tensor(
                    cand[:, :, first[a0]:first[a0 + na]].rearrange("p h (a b) -> p h a b", a=na),
                    tp[:, :, 0, a0:a0 + na].rearrange("p h (a o) -> p h a o", o=1).to_broadcast(sh),
                    tp[:, :, 1, 0:nb].rearrange("p h (o b) -> p h o b", o=1).to_broadcast(sh), ALU.add), t, *sf["sums"])
            k1 = dve.do(lambda e: e.tensor_copy(key_f, topi), t)
            kf = key_f.rearrange("p (h s m) -> p s m h", h=PH, s=2)
            for s in range(2):
                dve.do(lambda e: e.tensor_copy(di[:, s, 0, :], kf[:, s, 0, :]), k1)
                k2 = dve.do(lambda e: e.tensor_tensor(di[:, s, 1:16, :], kf[:, s, 1:16, :], kf[:, s, 0:15, :], ALU.subtract))
            t = yield from top16(lambda h: w16[:, h * 16:(h + 1) * 16], lambda h: j16[:, h * 16:(h + 1) * 16], cand, cand2, c_ok)
            turned_ = lambda a: a.rearrange("p (h r) -> p r h", h=PH)
            t1 = dve.do(lambda e: e.tensor_copy(jh.rearrange("p (r h) -> p r h", h=PH), turned_(j16)), t)
            dve.do(lambda e: e.tensor_scalar(packs[:, 0:P].rearrange("p (r h) -> p r h", h=PH), turned_(w16), 0.0, None, ALU.max),
                   *sf["packs"])

            by_rank = lambda a: a.rearrange("p m (r h) -> p m r h", h=PH)
            every_rank = lambda a: a.rearrange("p m (o h) -> p m o h", o=1).to_broadcast([P, 16, 16, PH])

            def compare(position, edge, *after):
                return dve.do(lambda e: e.tensor_tensor(
                    by_rank(cmp_b), position.rearrange("p (o r h) -> p o r h", o=1, h=PH).to_broadcast([P, 16, 16, PH]),
                    every_rank(edge), ALU.is_ge), *after)

            def products(dst, steps, *after):
                return dve.do(lambda e: e.tensor_tensor(by_rank(dst), by_rank(cmp_b), every_rank(steps), ALU.mult), *after)

            def tree(prod_, half, dst, t):
                src, dst_ = prod_, half
                for w in (8, 4, 2):
                    t = dve.do(lambda e: e.tensor_tensor(dst_[:, 0:w, :], src[:, 0:2 * w:2, :], src[:, 1:2 * w:2, :], ALU.add), t)
                    yield t
                    src, dst_ = dst_, src
                yield dve.do(lambda e: e.tensor_tensor(dst, src[:, 0, :], src[:, 1, :], ALU.add), t)

            yield
            c_ok = compare(jh, ta, t1, kc[-1], k2)
            tb = products(prod, td, c_ok)
            ti = products(prod2, di[:, 0, :, :], c_ok)
            for tb, ti in zip(tree(prod, sum8, bh, tb), tree(prod2, cmp_b, i1h, ti)):
                pass
            t2 = dve.do(lambda e: e.tensor_tensor(bh, jh, bh, ALU.subtract), tb)
            tq = dve.do(lambda e: e.tensor_scalar(q_h, i1h, float(PKEYS // 2), None, ALU.is_ge), ti)
            yield
            c_ok = compare(bh, tm, t2)
            dve.do(lambda e: e.scalar_tensor_tensor(packs[:, P:2 * P], q_h, -float(PKEYS // 2), i1h, ALU.mult, ALU.add), tq)
            yield "chain"
            t2 = products(prod, di[:, 1, :, :], c_ok)
            yield "chain"
            for t2 in tree(prod, sum8, i2h, t2):
                sf["sums"] = [t2]
                yield "chain"
            t3 = dve.do(lambda e: e.scalar_tensor_tensor(packs[:, 2 * P:3 * P], q_h, float(PKEYS), i2h, ALU.mult, ALU.add), t2)
            picked[i] = t3

        sq, tf = [[], []], [[wk_ok], [wk_ok]]
        sq_ok, xn_ok, loads = {}, {}, []
        SPLIT = 4
        part = PE_N // SPLIT
        for c in range(SPLIT):
            loads.append(lambda e, c=c: e.dma_start(downT[:, :, c * part:(c + 1) * part],
                                                    io["downT"][:, c * part:(c + 1) * part].rearrange("(k p) n -> p k n", p=P)))
        for c in range(SPLIT):
            loads.append(lambda e, c=c: e.dma_start(up_sb[:, c * part // P:(c + 1) * part // P, :],
                                                    io["up"][c * part:(c + 1) * part, :].rearrange("(c p) n -> p c n", p=P)))

        def mix1(i, y0, y1, ok0, ok1):
            n = i % 2
            t = dve.do(lambda e: e.tensor_scalar(att[:, i, :], y0, gate[:, i, 0:1], None, ALU.mult), ok0)
            t = dve.do(lambda e: e.scalar_tensor_tensor(att[:, i, :], y1, gate[:, i, 1:2], att[:, i, :], ALU.mult, ALU.add),
                       t, ok1)
            sq_ok[i] = act.do(lambda e: e.activation(ys_b[n][:, :], att[:, i, :], ACT.Square, accum_out=ssq[:, i:i + 1]),
                              t, *ends, *sq[n])
            sq[n] = [sq_ok[i]]
            if i >= NT - 2 * SPLIT or i >= 3 and i % 2:
                c = len(weight_ld)
                if c < 2 * SPLIT:
                    weight_ld.append(sp.dma(ld["down" if c < SPLIT else "up"], loads[c], t))
            if i % 4 == 0 and i:
                norm_group(i // 4 - 1)
                if i == 4:
                    similar(0)
                    similar(1)
            if i > 4:
                next(selection, None)
                next(selection, None)
            return t

        def norm_group(q):
            r_ok = rsqrt_cols(rms[:, 4 * q:4 * q + 4], ssq[:, 4 * q:4 * q + 4], 1e-5, [sq_ok[4 * q + 3]])
            for i in range(4 * q, 4 * q + 4):
                n = i % 2
                t = dve.do(lambda e: e.tensor_scalar(att[:, i, :], att[:, i, :], rms[:, i:i + 1], None, ALU.mult), r_ok)
                t = pe.do(lambda e: [e.transpose(banks[:, 4 + n, c * P:(c + 1) * P], att[:, i, c * P:(c + 1) * P], ident[:, :])
                                     for c in range(KD)][-1], t, *tf[n])
                att_free[0] = t
                for c in range(KD):
                    xn_ok[i] = act.do(lambda e: e.activation(xnT[:, c, i * P:(i + 1) * P], banks[:, 4 + n, c * P:(c + 1) * P],
                                                             ACT.Copy, scale=normw[:, c:c + 1]), t, s_ld)
                tf[n] = [xn_ok[i]]

        weight_ld, att_free = [], [None]
        selection = select(0)
        mixb2 = [hidf[:, 5120 + n * D:5120 + (n + 1) * D] for n in range(8)]
        x2_ok = gather_mix(mix1, mixb2, *ends, *drained)
        norm_group(NT // 4 - 1)
        for b in range(8):
            pf[b] = pf[b] + [xn_ok[NT - 1]]
        sf["lo0"], sf["lo1"] = [att_free[0]], [att_free[0]]
        sf["hid"] = [x2_ok[-1]]
        d_ld, u_ld = weight_ld[SPLIT - 1], weight_ld[-1]
        io_ok = pool.do(lambda e: e.iota(iotax, [[1, P], [0, SUB]], base=0, channel_multiplier=0,
                                         allow_small_or_imprecise_dtypes=True), *drained)

        def turn_over(i, picked_ok):
            turn_, wpart_ = turn[i % 2], wpart[i % 2]
            t = pe.do(lambda e: [e.transpose(banks[:, B_TR, m * P:(m + 1) * P], packs[:, m * P:(m + 1) * P], ident[:, :])
                                 for m in range(3)][-1], picked_ok, *pf[B_TR])
            sf["packs"] = [t]
            act.do(lambda e: e.copy(wpart_[:, 0, :], banks[:, B_TR, 0:P]), t, *sf["turn"])
            return act.do(lambda e: e.copy(turn_.rearrange("p a n -> p (a n)"), banks[:, B_TR, P:3 * P]))

        def rest_parts(i, turned_ok):
            wpart_ = wpart[i % 2]
            t = dve.do(lambda e: e.tensor_tensor(wres[:, 0, :], banks[:, B_TR, 0:P], wpart_[:, 0, :], ALU.subtract), turned_ok)
            pf[B_TR] = [t]
            yield
            t = dve.do(lambda e: e.tensor_copy(wpart_[:, 1, :], wres[:, 0, :]), t, *sf["turn"])
            yield
            t = dve.do(lambda e: e.tensor_tensor(wres[:, 1, :], wres[:, 0, :], wpart_[:, 1, :], ALU.subtract), t)
            yield
            kept[i] = dve.do(lambda e: e.tensor_copy(wpart_[:, 2, :], wres[:, 1, :]), t)

        def outputs_of(g, n, q):
            o_ok[2 * g + n] = pe.do(lambda e: [e.matmul(banks[:, B_OUT + n, 0:D], hid[:, c, n * P:(n + 1) * P], up_sb[:, c, :],
                                                        start=(c == 0), stop=(c == NC - 1)) for c in (2 * q, 2 * q + 1)][-1],
                                    w_ok[2 * g + n], u_ld, *pf[B_OUT + n])

        def burst(g, qs):
            for q in qs:
                if g > 0:
                    for n in range(2):
                        if n or q >= early[g - 1]:
                            outputs_of(g - 1, n, q)
                    sf["hid"] = [o_ok[2 * g - 1], o_ok[2 * g - 2]]
                if g < GROUPS:
                    b = B_HID + q % 2
                    t = pe.do(lambda e: [e.matmul(banks[:, b, h * G2:(h + 1) * G2], downT[:, c, (2 * q + h) * P:(2 * q + h + 1) * P],
                                                  xnT[:, c, g * G2:(g + 1) * G2], start=(c == 0), stop=(c == KD - 1))
                                         for h in range(2) for c in range(KD)][-1], d_ld, *pf[b])
                    h_ok[g] = act.do(lambda e: e.activation(hid[:, 2 * q:2 * q + 2, :].rearrange("p c t -> p (c t)"), banks[:, b, :],
                                                            ACT.Gelu), t, *sf["hid"])
                    pf[b] = [h_ok[g]]

        def spread(i, s):
            n = s % 2
            cols = slice(s * SUB, (s + 1) * SUB)
            one = lambda a, k: a.rearrange("p (o t) -> p o t", o=1).to_broadcast([P, k, SUB])
            th = dve.do(lambda e: e.tensor_tensor(hi_b[n], iotax[:, 0:NC, :], one(turn[i % 2][:, 0, cols], NC), ALU.is_equal), kept[i], io_ok, *sf[f"lo{n}"])
            dve.do(lambda e: e.tensor_tensor(lo_b[n], iotax, one(turn[i % 2][:, 1, cols], P), ALU.is_equal))
            t1 = dve.do(lambda e: e.tensor_tensor(
                hw_b[n], hi_b[n].rearrange("p (o a) t -> p o a t", o=1).to_broadcast([P, 3, NC, SUB]),
                wpart[i % 2][:, :, cols].rearrange("p m (o t) -> p m o t", o=1).to_broadcast([P, 3, NC, SUB]), ALU.mult), th)
            b = B_G + n
            t = pe.do(lambda e: [e.matmul(banks[:, b, k * NC:(k + 1) * NC], lo_b[n][:, :, k], hw_b[n][:, m, :, k],
                                          start=(m == 0), stop=(m == 2)) for k in range(SUB) for m in range(3)][-1], t1, *pf[b])
            sf[f"lo{n}"] = [t]
            return t

        def weigh(i, s, g_ok):
            b = B_G + s % 2
            t0 = (i % 2) * P + s * SUB
            t = dve.do(lambda e: e.tensor_tensor(hid[:, :, t0:t0 + SUB], hid[:, :, t0:t0 + SUB],
                                                 banks[:, b, :].rearrange("p (t c) -> p c t", c=NC), ALU.mult), g_ok, h_ok[i // 2])
            pf[b] = [t]
            w_ok[i] = t

        def add_out(i):
            t = dve.do(lambda e: e.tensor_tensor(x_sb[:, i, :], x_sb[:, i, :], banks[:, B_OUT + i % 2, 0:D], ALU.add), o_ok[i])
            pf[B_OUT + i % 2] = [t]
            return sp.dma(ld["store"], lambda e: e.dma_start(out[i * P:(i + 1) * P, :], x_sb[:, i, :]), t)

        def alternate(main, fill):
            for kind in main:
                if kind == "chain":
                    next(fill, None)

        GROUPS = TOK // G2
        NQ, NS = NC // 2, P // SUB
        o_ok, h_ok = {}, {}
        early = [6] * (GROUPS - 1) + [NQ]
        turn_after = [3] + [12] * (GROUPS - 1)
        ahead = (3, 5, 7, 9)
        for g in range(GROUPS):
            i0, i1 = 2 * g, 2 * g + 1
            selection1 = select(i1)
            alternate(selection if g == 0 else select(i0), selection1)
            burst(g, range(turn_after[g]))
            turned_ok = turn_over(i0, picked[i0])
            burst(g, range(turn_after[g], NQ))
            rest0 = rest_parts(i0, turned_ok)
            alternate(selection1, rest0)
            alternate(rest0, iter(()))
            turned_ok = turn_over(i1, picked[i1])
            prev, out_q = None, 0
            for step in range(2 * NS):
                i, s = (i0, i1)[step // NS], step % NS
                g_ok = spread(i, s)
                if step == 2:
                    rest1 = rest_parts(i1, turned_ok)
                    for i_ in (i0 - 2, i0 - 1) if g > 0 else ():
                        next(rest1)
                        add_out(i_)
                    alternate(rest1, iter(()))
                if step in ahead and g + 1 < GROUPS:
                    similar(i0 + 2 + ahead.index(step) // 2, [ahead.index(step) % 2])
                if prev:
                    weigh(*prev)
                prev = (i, s, g_ok)
                if step > NS:
                    upto_q = early[g] * (step - NS) // (NS - 1)
                    for q in range(out_q, upto_q):
                        outputs_of(g, 0, q)
                    out_q = upto_q
            weigh(*prev)
            sf["turn"] = [w_ok[i1]]
        burst(GROUPS, range(NQ))
        add_out(NT - 2)
        y_st = add_out(NT - 1)
        sp.wait(y_st)


def layout(i):
    A = {k: np.asarray(v) for k, v in i.items()}
    x = A["x"].reshape(TOK, D)

    def cols(b):
        return b.reshape(NE, -1, P).transpose(2, 0, 1)
    order = np.arange(PE_N).reshape(2, PKEYS // 2, PKEYS).transpose(1, 0, 2).reshape(-1)
    wv = A["L0_cond_Wv"].T.reshape(D, HEADS // 2, 2, DH)
    d = dict(
        x=x, xT=x.T, mask=A["mask_SxS_bk1"].view(np.uint32), condT=A["cond_256"].T,
        wqT=A["L0_cond_Wq"].T, wkT=A["L0_cond_Wk"].T, woT=A["L0_cond_Wo"].T,
        wvT=wv.transpose(0, 2, 1, 3).reshape(D, D),
        rms_scale=A["L0_cond_rms_scale"].reshape(1, D), wcT=A["L0_cond_Wc"].T, bc=A["L0_cond_bc"].reshape(1, 2 * D),
        routerT=A["L0_ffn_router_w"].T, w1T=A["L0_ffn_w1"].transpose(0, 2, 1), b1=cols(A["L0_ffn_b1"]),
        w2T=A["L0_ffn_w2"].transpose(0, 2, 1), b2=A["L0_ffn_b2"],
        rms_w=A["L1_cond_rms_w"].reshape(KD, P).T, wg_W=A["L1_cond_wg_W"], wg_b=A["L1_cond_wg_b"].reshape(1, NE),
        gg_W=A["L1_cond_gg_W"], gg_b=A["L1_cond_gg_b"].reshape(1, NE),
        W1=A["L1_cond_W1"], m1=cols(A["L1_cond_b1"]), W2=A["L1_cond_W2"], m2=cols(A["L1_cond_b2"]),
        W3=A["L1_cond_W3"], m3=A["L1_cond_b3"], norm_w=A["L1_ffn_norm_w"].reshape(KD, P).T,
        wqp=A["L1_ffn_wq"].reshape(D, 2 * PH, PDK).transpose(2, 1, 0),
        keysT=A["L1_ffn_keys"].transpose(3, 0, 2, 1).reshape(PDK, 2 * PH, PKEYS),
        downT=A["L1_ffn_expert_down"][order].T, up=A["L1_ffn_expert_up"][order],
    )
    return {k: np.ascontiguousarray(v) for k, v in d.items()}


def kernel(**inputs):
    from concourse import bacc
    from concourse.bass_utils import run_bass_kernel_spmd

    arrays = layout(inputs)
    nc = bacc.Bacc("TRN2", target_bir_lowering=False, num_devices=1)
    io = {n: nc.dram_tensor(f"in_{n}", a.shape, mybir.dt.from_np(a.dtype), kind="ExternalInput").ap()
          for n, a in arrays.items()}
    out = nc.dram_tensor("out_0", [TOK, D], F32, kind="ExternalOutput").ap()
    build(nc, io, out)
    r = run_bass_kernel_spmd(nc, [{f"in_{n}": a for n, a in arrays.items()}], core_ids=[0])
    return r.results[0]["out_0"].reshape(BATCH, SEQ, D)
```
